# Optimizing a Trainium2 kernel written in Bass

```python
import numpy as np
import jax
import jax.numpy as jnp

def _softmax(x, axis=-1):
    return jax.nn.softmax(x, axis=axis)

def _gelu(x):
    return jax.nn.gelu(x, approximate=True)

def _silu(x):
    return jax.nn.silu(x)

def _sigmoid(x):
    return jax.nn.sigmoid(x)

def _layernorm(x, axis=-1, eps=1e-05):
    m = jnp.mean(x, axis=axis, keepdims=True)
    v = jnp.var(x, axis=axis, keepdims=True)
    return (x - m) / jnp.sqrt(v + eps)

def _scatter_add(tgt, idx, src, axis=0):
    return tgt.at[idx].add(src)

def _segment_sum(src, seg, n):
    return jax.ops.segment_sum(src, seg, n)
kernel_name = 'mk_lm_tower_d1_tok_ids1024_r4_cd6884'

def setup_inputs(seed: int=0):
    np.random.seed(seed)
    _w = jnp.asarray

    def _rec_inputs():
        import jax
        import jax.numpy as jnp
        _rk = jax.random.key(seed)
        x = jax.random.randint(jax.random.fold_in(_rk, 1), (2, 2048), 0, 31993, jnp.int32)
        return x
    x = _rec_inputs()

    def _L0_tok_setup():
        import jax, jax.numpy as jnp
        import numpy as np
        N_BLOCKS = 6
        D_MODEL = 256
        N_HEADS = 8
        D_K = D_MODEL // N_HEADS
        D_FF = 1024
        VSIZE = 8000
        B, LS = (4, 512)
        LN_EPS = 1e-05

        def _layernorm(x, w, b):
            m = jnp.mean(x, axis=-1, keepdims=True)
            v = jnp.mean((x - m) ** 2, axis=-1, keepdims=True)
            return (x - m) * jax.lax.rsqrt(v + LN_EPS) * w + b
        key = jax.random.key(seed)
        ks = jax.random.split(key, 10)
        s = 0.02
        return {'source': jax.random.randint(ks[0], (B, LS), 0, VSIZE), 'emb_table': s * jax.random.normal(ks[1], (VSIZE, D_MODEL), jnp.float32), 'Wq': s * jax.random.normal(ks[2], (N_BLOCKS, N_HEADS, D_K, D_MODEL), jnp.float32), 'Wk': s * jax.random.normal(ks[3], (N_BLOCKS, N_HEADS, D_K, D_MODEL), jnp.float32), 'Wv': s * jax.random.normal(ks[4], (N_BLOCKS, N_HEADS, D_K, D_MODEL), jnp.float32), 'Wo': s * jax.random.normal(ks[5], (N_BLOCKS, D_MODEL, D_MODEL), jnp.float32), 'ff_w1': s * jax.random.normal(ks[6], (N_BLOCKS, D_FF, D_MODEL), jnp.float32), 'ff_b1': jnp.zeros((N_BLOCKS, D_FF), jnp.float32), 'ff_w2': s * jax.random.normal(ks[7], (N_BLOCKS, D_MODEL, D_FF), jnp.float32), 'ff_b2': jnp.zeros((N_BLOCKS, D_MODEL), jnp.float32), 'ln1_w': jnp.ones((N_BLOCKS, D_MODEL), jnp.float32), 'ln1_b': jnp.zeros((N_BLOCKS, D_MODEL), jnp.float32), 'ln2_w': jnp.ones((N_BLOCKS, D_MODEL), jnp.float32), 'ln2_b': jnp.zeros((N_BLOCKS, D_MODEL), jnp.float32)}
    _L0_tok_all = _L0_tok_setup()
    _L0_tok_in = {k: v for k, v in _L0_tok_all.items() if k in ('emb_table', 'Wq', 'Wk', 'Wv', 'Wo', 'ff_w1', 'ff_b1', 'ff_w2', 'ff_b2', 'ln1_w', 'ln1_b', 'ln2_w', 'ln2_b')}
    del _L0_tok_all

    def _L0_attn_setup():
        import jax, jax.numpy as jnp
        import numpy as np
        B, T, D = (4, 1024, 256)
        H, LH, DH, BUCKETS = (16, 4, 64, 64)

        def _merge_heads(v, h):
            b, t, hd = v.shape
            return v.reshape(b, t, h, hd // h).transpose(0, 2, 1, 3)

        def _bucketed(z, nb):
            Bz, Tz, Dz = z.shape
            return z.reshape(Bz, nb, Tz // nb, Dz)

        def _look_around(z, pad_value):
            pad = [(0, 0)] * z.ndim
            pad[1] = (1, 1)
            p = jnp.pad(z, pad, constant_values=pad_value)
            nb = z.shape[1]
            return jnp.concatenate([p[:, i:i + nb] for i in range(3)], axis=2)
        key = jax.random.key(seed)
        ks = jax.random.split(key, 6)
        x = jax.random.normal(ks[0], (B, T, D), jnp.float32)
        w_q = jax.random.normal(ks[1], (D, H * DH), jnp.float32) * 0.02
        w_kv = jax.random.normal(ks[2], (D, 2 * H * DH), jnp.float32) * 0.02
        w_out = jax.random.normal(ks[3], (H * DH, D), jnp.float32) * 0.02
        b_out = jnp.zeros((D,), jnp.float32)
        sort_w = jax.random.normal(ks[4], (1, H - LH, 2 * DH, BUCKETS), jnp.float32)
        return dict(x=x, w_q=w_q, w_kv=w_kv, w_out=w_out, b_out=b_out, sort_w=sort_w)
    _L0_attn_all = _L0_attn_setup()
    _L0_attn_in = {k: v for k, v in _L0_attn_all.items() if k in ('w_q', 'w_kv', 'w_out', 'b_out', 'sort_w')}
    del _L0_attn_all

    def _L0_ffn_setup():
        import jax, jax.numpy as jnp
        import numpy as np
        import math
        D_MODEL = 256
        D_FF = 1024
        NUM_EXPERTS = 8
        NUM_SHARED = 1
        E_ROUTED = NUM_EXPERTS - NUM_SHARED
        TOP_K = 2
        CAP_FACTOR = 1.25
        B, S = (4, 512)
        T = B * S
        CAPACITY = math.ceil(CAP_FACTOR * T * TOP_K / E_ROUTED)
        SHARED_SCALE = 1.0

        def _layernorm(x, g, b, eps=1e-05):
            mu = jnp.mean(x, axis=-1, keepdims=True)
            var = jnp.mean((x - mu) ** 2, axis=-1, keepdims=True)
            return (x - mu) * jax.lax.rsqrt(var + eps) * g + b
        key = jax.random.key(seed)
        ks = jax.random.split(key, 10)
        s = 0.02
        return {'x': jax.random.normal(ks[0], (B, S, D_MODEL), dtype=jnp.float32), 'ln_g': jnp.ones((D_MODEL,), jnp.float32), 'ln_b': jnp.zeros((D_MODEL,), jnp.float32), 'Wr': jax.random.normal(ks[1], (D_MODEL, E_ROUTED), jnp.float32) * s, 'W1': jax.random.normal(ks[2], (E_ROUTED, D_MODEL, D_FF), jnp.float32) * s, 'W3': jax.random.normal(ks[3], (E_ROUTED, D_MODEL, D_FF), jnp.float32) * s, 'W2': jax.random.normal(ks[4], (E_ROUTED, D_FF, D_MODEL), jnp.float32) * s, 'W1s': jax.random.normal(ks[5], (D_MODEL, D_FF), jnp.float32) * s, 'W3s': jax.random.normal(ks[6], (D_MODEL, D_FF), jnp.float32) * s, 'W2s': jax.random.normal(ks[7], (D_FF, D_MODEL), jnp.float32) * s}
    _L0_ffn_all = _L0_ffn_setup()
    _L0_ffn_in = {k: v for k, v in _L0_ffn_all.items() if k in ('ln_g', 'ln_b', 'Wr', 'W1', 'W3', 'W2', 'W1s', 'W3s', 'W2s')}
    del _L0_ffn_all
    return {'x': x, 'L0_tok_emb_table': _L0_tok_in['emb_table'], 'L0_tok_Wq': _L0_tok_in['Wq'], 'L0_tok_Wk': _L0_tok_in['Wk'], 'L0_tok_Wv': _L0_tok_in['Wv'], 'L0_tok_Wo': _L0_tok_in['Wo'], 'L0_tok_ff_w1': _L0_tok_in['ff_w1'], 'L0_tok_ff_b1': _L0_tok_in['ff_b1'], 'L0_tok_ff_w2': _L0_tok_in['ff_w2'], 'L0_tok_ff_b2': _L0_tok_in['ff_b2'], 'L0_tok_ln1_w': _L0_tok_in['ln1_w'], 'L0_tok_ln1_b': _L0_tok_in['ln1_b'], 'L0_tok_ln2_w': _L0_tok_in['ln2_w'], 'L0_tok_ln2_b': _L0_tok_in['ln2_b'], 'L0_attn_w_q': _L0_attn_in['w_q'], 'L0_attn_w_kv': _L0_attn_in['w_kv'], 'L0_attn_w_out': _L0_attn_in['w_out'], 'L0_attn_b_out': _L0_attn_in['b_out'], 'L0_attn_sort_w': _L0_attn_in['sort_w'], 'L0_ffn_ln_g': _L0_ffn_in['ln_g'], 'L0_ffn_ln_b': _L0_ffn_in['ln_b'], 'L0_ffn_Wr': _L0_ffn_in['Wr'], 'L0_ffn_W1': _L0_ffn_in['W1'], 'L0_ffn_W3': _L0_ffn_in['W3'], 'L0_ffn_W2': _L0_ffn_in['W2'], 'L0_ffn_W1s': _L0_ffn_in['W1s'], 'L0_ffn_W3s': _L0_ffn_in['W3s'], 'L0_ffn_W2s': _L0_ffn_in['W2s']}

def reference(x, L0_tok_emb_table, L0_tok_Wq, L0_tok_Wk, L0_tok_Wv, L0_tok_Wo, L0_tok_ff_w1, L0_tok_ff_b1, L0_tok_ff_w2, L0_tok_ff_b2, L0_tok_ln1_w, L0_tok_ln1_b, L0_tok_ln2_w, L0_tok_ln2_b, L0_attn_w_q, L0_attn_w_kv, L0_attn_w_out, L0_attn_b_out, L0_attn_sort_w, L0_ffn_ln_g, L0_ffn_ln_b, L0_ffn_Wr, L0_ffn_W1, L0_ffn_W3, L0_ffn_W2, L0_ffn_W1s, L0_ffn_W3s, L0_ffn_W2s):
    import jax
    import jax.numpy as jnp

    def _L0_tok_ref(source, emb_table, Wq, Wk, Wv, Wo, ff_w1, ff_b1, ff_w2, ff_b2, ln1_w, ln1_b, ln2_w, ln2_b):
        import jax, jax.numpy as jnp
        import numpy as np
        N_BLOCKS = 6
        D_MODEL = 256
        N_HEADS = 8
        D_K = D_MODEL // N_HEADS
        D_FF = 1024
        VSIZE = 8000
        B, LS = (4, 512)
        LN_EPS = 1e-05

        def _layernorm(x, w, b):
            m = jnp.mean(x, axis=-1, keepdims=True)
            v = jnp.mean((x - m) ** 2, axis=-1, keepdims=True)
            return (x - m) * jax.lax.rsqrt(v + LN_EPS) * w + b
        x = emb_table[source]
        Bx, L, Dm = x.shape
        n_blocks = Wq.shape[0]
        for i in range(n_blocks):
            heads = jnp.einsum('bld,hkd->blhk', x, Wq[i]).reshape(Bx, L, Dm)
            z1 = heads @ Wo[i].T
            a1 = _layernorm(z1 + x, ln1_w[i], ln1_b[i])
            h = jax.nn.relu(a1 @ ff_w1[i].T + ff_b1[i])
            z2 = h @ ff_w2[i].T + ff_b2[i]
            x = _layernorm(z2 + a1, ln2_w[i], ln2_b[i])
        return x

    def _L0_attn_ref(x, w_q, w_kv, w_out, b_out, sort_w):
        import jax, jax.numpy as jnp
        import numpy as np
        B, T, D = (4, 1024, 256)
        H, LH, DH, BUCKETS = (16, 4, 64, 64)

        def _merge_heads(v, h):
            b, t, hd = v.shape
            return v.reshape(b, t, h, hd // h).transpose(0, 2, 1, 3)

        def _bucketed(z, nb):
            Bz, Tz, Dz = z.shape
            return z.reshape(Bz, nb, Tz // nb, Dz)

        def _look_around(z, pad_value):
            pad = [(0, 0)] * z.ndim
            pad[1] = (1, 1)
            p = jnp.pad(z, pad, constant_values=pad_value)
            nb = z.shape[1]
            return jnp.concatenate([p[:, i:i + nb] for i in range(3)], axis=2)
        b, t, d = x.shape
        h, lh, dh, buckets = (H, LH, DH, BUCKETS)
        sh = h - lh
        w = t // buckets
        neg = -jnp.finfo(x.dtype).max
        q = _merge_heads(x @ w_q, h)
        k, v = jnp.split(x @ w_kv, 2, axis=-1)
        k = _merge_heads(k, h)
        v = _merge_heads(v, h)
        lq, sq = (q[:, :lh], q[:, lh:])
        lk, sk = (k[:, :lh], k[:, lh:])
        lv, sv = (v[:, :lh], v[:, lh:])
        B1 = b * lh
        blq = _bucketed(lq.reshape(B1, t, dh), buckets)
        blk = _look_around(_bucketed(lk.reshape(B1, t, dh), buckets), -1.0)
        blv = _look_around(_bucketed(lv.reshape(B1, t, dh), buckets), -1.0)
        ticker = jnp.arange(t, dtype=x.dtype).reshape(1, buckets, w)
        bq_k = _look_around(ticker, -1.0)
        dots = jnp.einsum('bnie,bnje->bnij', blq, blk)
        dots = jnp.where(bq_k[:, :, None, :] == -1.0, neg, dots)
        attn = jax.nn.softmax(dots, axis=-1)
        local_out = jnp.einsum('bnij,bnje->bnie', attn, blv).reshape(b, lh, t, dh)
        B2 = b * sh
        bq = _bucketed(sq.reshape(B2, t, dh), buckets)
        bk = _bucketed(sk.reshape(B2, t, dh), buckets)
        bv = _bucketed(sv.reshape(B2, t, dh), buckets)
        feats = jnp.concatenate([bq.sum(2), bk.sum(2)], axis=-1)
        W = jnp.broadcast_to(sort_w, (b, sh, 2 * dh, buckets)).reshape(B2, 2 * dh, buckets)
        R = jax.nn.relu(jnp.einsum('bud,bdv->buv', feats, W))
        R = jax.nn.softmax(R, axis=-1)
        bk_r = jnp.einsum('buv,bvtd->butd', R, bk)
        bv_r = jnp.einsum('buv,bvtd->butd', R, bv)
        bk2 = jnp.concatenate([bk_r, bk], axis=2)
        bv2 = jnp.concatenate([bv_r, bv], axis=2)
        dots2 = jnp.einsum('buie,buje->buij', bq, bk2) * dh ** (-0.5)
        attn2 = jax.nn.softmax(dots2, axis=-1)
        sink_out = jnp.einsum('buij,buje->buie', attn2, bv2).reshape(b, sh, t, dh)
        out = jnp.concatenate([local_out, sink_out], axis=1)
        out = out.transpose(0, 2, 1, 3).reshape(b, t, h * dh)
        return out @ w_out + b_out

    def _L0_ffn_ref(x, ln_g, ln_b, Wr, W1, W3, W2, W1s, W3s, W2s):
        import jax, jax.numpy as jnp
        import numpy as np
        import math
        D_MODEL = 256
        D_FF = 1024
        NUM_EXPERTS = 8
        NUM_SHARED = 1
        E_ROUTED = NUM_EXPERTS - NUM_SHARED
        TOP_K = 2
        CAP_FACTOR = 1.25
        B, S = (4, 512)
        T = B * S
        CAPACITY = math.ceil(CAP_FACTOR * T * TOP_K / E_ROUTED)
        SHARED_SCALE = 1.0

        def _layernorm(x, g, b, eps=1e-05):
            mu = jnp.mean(x, axis=-1, keepdims=True)
            var = jnp.mean((x - mu) ** 2, axis=-1, keepdims=True)
            return (x - mu) * jax.lax.rsqrt(var + eps) * g + b
        Bx, Sx, D = x.shape
        Tn = Bx * Sx
        h = _layernorm(x, ln_g, ln_b).reshape(Tn, D)
        logits = h @ Wr
        top_vals, top_idx = jax.lax.top_k(logits, TOP_K)
        gates = jax.nn.softmax(top_vals, axis=-1)
        idx = top_idx.T.reshape(-1)
        gat = gates.T.reshape(-1)
        tok = jnp.tile(jnp.arange(Tn), TOP_K)
        onehot = jax.nn.one_hot(idx, E_ROUTED, dtype=jnp.int32)
        pos = jnp.sum(jnp.cumsum(onehot, axis=0) * onehot, axis=-1) - 1
        keep = pos < CAPACITY
        pos_c = jnp.where(keep, pos, CAPACITY)
        xe = jnp.zeros((E_ROUTED, CAPACITY, D), h.dtype).at[idx, pos_c].set(h[tok], mode='drop')
        a = jnp.einsum('ecd,edf->ecf', xe, W1)
        b = jnp.einsum('ecd,edf->ecf', xe, W3)
        ye = jnp.einsum('ecf,efd->ecd', jax.nn.silu(a) * b, W2)
        out_slots = ye[jnp.clip(idx, 0, E_ROUTED - 1), jnp.clip(pos_c, 0, CAPACITY - 1)]
        out_slots = out_slots * (gat * keep.astype(gat.dtype))[:, None]
        routed = jnp.zeros((Tn, D), h.dtype).at[tok].add(out_slots)
        shared = jax.nn.silu(h @ W1s) * (h @ W3s) @ W2s
        out = routed + SHARED_SCALE * shared
        return out.reshape(Bx, Sx, D)
    h = _L0_tok_ref(x, L0_tok_emb_table, L0_tok_Wq, L0_tok_Wk, L0_tok_Wv, L0_tok_Wo, L0_tok_ff_w1, L0_tok_ff_b1, L0_tok_ff_w2, L0_tok_ff_b2, L0_tok_ln1_w, L0_tok_ln1_b, L0_tok_ln2_w, L0_tok_ln2_b)
    h = h + _L0_attn_ref(_layernorm(h, axis=-1), L0_attn_w_q, L0_attn_w_kv, L0_attn_w_out, L0_attn_b_out, L0_attn_sort_w)
    h = h + _L0_ffn_ref(_layernorm(h, axis=-1), L0_ffn_ln_g, L0_ffn_ln_b, L0_ffn_Wr, L0_ffn_W1, L0_ffn_W3, L0_ffn_W2, L0_ffn_W1s, L0_ffn_W3s, L0_ffn_W2s)
    return h

_drawn_inputs = setup_inputs


def setup_inputs(seed=0):
    import zlib

    import numpy as np

    out = dict(_drawn_inputs(seed))
    spreads = {'L0_tok_ff_b1': (0.0, 0.1),
     'L0_tok_ff_b2': (0.0, 0.1),
     'L0_tok_ln1_w': (1.0, 0.2),
     'L0_tok_ln1_b': (0.0, 0.1),
     'L0_tok_ln2_w': (1.0, 0.2),
     'L0_tok_ln2_b': (0.0, 0.1),
     'L0_attn_b_out': (0.0, 0.1),
     'L0_ffn_ln_g': (1.0, 0.6),
     'L0_ffn_ln_b': (0.0, 0.8)}
    factors = {'L0_attn_w_q': 4.339,
     'L0_attn_sort_w': 6.696,
     'L0_ffn_Wr': 3.856,
     'L0_ffn_W1': 3.743,
     'L0_ffn_W3': 3.804,
     'L0_ffn_W2': 3.765}
    for name, (base, spread) in spreads.items():
        noise = np.random.default_rng([zlib.crc32(name.encode()), seed]).standard_normal(out[name].shape)
        drawn = base * np.exp(spread * noise) if base else spread * noise
        out[name] = jnp.asarray(drawn.astype(out[name].dtype))
    for name, factor in factors.items():
        out[name] = (out[name] * factor).astype(out[name].dtype)
    return out
```

```python
from contextlib import ExitStack

import concourse.bass as bass
from concourse import mybir

F32 = mybir.dt.float32
F32R = mybir.dt.float32r
I32 = mybir.dt.int32
U32 = mybir.dt.uint32
ALU = mybir.AluOpType
ACT = mybir.ActivationFunctionType
AX = mybir.AxisListType

P = 128
D = 256
DC = D // P
N_TOK = 4096
G = 512
NG = N_TOK // G
GT = G // P
F = 1024
FC = F // P
LAYERS = 6
VOCAB = 8000
EPS = 1e-5


def held(eng, value):
    if not isinstance(value, int):
        value = eng.snap(value)
        eng.compute_val(value)
    return value


def tower(nc, ctx, io, x32, rows_for, acc):
    def sb(name, shape, dt=F32):
        return ctx.enter_context(nc.sbuf_tensor(name, shape, dt))

    def sem(name):
        return ctx.enter_context(nc.semaphore(name))

    w_hi = [sb(f"t_w_hi{i}", [P, NG, G], F32R) for i in range(2)]
    w_lo = [sb(f"t_w_lo{i}", [P, NG, G], F32R) for i in range(2)]
    w_stage = sb("t_w_stage", [P, 2, G])
    mix = sb("t_mix", [P, LAYERS, DC * D])
    mix_hi = sb("t_mix_hi", [P, DC, D], F32R)
    mix_lo = sb("t_mix_lo", [P, DC, D], F32R)
    x_hi = sb("t_x_hi", [P, DC, G], F32R)
    x_lo = sb("t_x_lo", [P, DC, G], F32R)
    a32 = sb("t_a32", [P, 2, DC, G])
    a_hi = sb("t_a_hi", [P, 2, DC, G], F32R)
    a_lo = sb("t_a_lo", [P, 2, DC, G], F32R)
    h32 = sb("t_h32", [P, 2, G])
    h_hi = sb("t_h_hi", [P, FC, G], F32R)
    h_lo = sb("t_h_lo", [P, FC, G], F32R)
    u2 = sb("t_u2", [P, DC, G])
    xn = [sb(f"t_xn{i}", [P, GT, D]) for i in (1, 2)]
    vec = sb("t_vec", [P, LAYERS, 14])
    b1 = sb("t_b1", [P, LAYERS, FC])
    ids = sb("t_ids", [P, N_TOK // P], I32)
    idf = sb("t_idf", [P, 3, N_TOK // P])
    idu = sb("t_idu", [P, N_TOK // P], U32)
    eye = sb("t_eye", [P, DC, D])
    stats = [sb(f"t_stats{i}", [P, GT, 6]) for i in (1, 2)]
    mv = [sb(f"t_mv{i}", [P, GT, 2]) for i in (1, 2)]
    var_eps = [sb(f"t_ve{i}", [P, GT]) for i in (1, 2)]
    std = [sb(f"t_std{i}", [P, GT]) for i in (1, 2)]
    rstd = [sb(f"t_rstd{i}", [P, GT]) for i in (1, 2)]
    nmr = [sb(f"t_nmr{i}", [P, GT]) for i in (1, 2)]
    fill = sb("t_fill", [P, REC])

    ps_tok = ctx.enter_context(nc.psum_tensor("t_ps_tok", [P, GT, D], F32))
    ps_feat = ctx.enter_context(nc.psum_tensor("t_ps_feat", [P, DC, G], F32))
    ps_h = ctx.enter_context(nc.psum_tensor("t_ps_h", [P, 2, G], F32))
    ps_y = ctx.enter_context(nc.psum_tensor("t_ps_y", [P, DC, G], F32))

    vec_loaded = sem("t_vec_loaded")
    ids_loaded = sem("t_ids_loaded")
    qo_loaded = [sem(f"t_qo_loaded{i}") for i in range(2)]
    stage_loaded = [sem(f"t_stage_loaded{i}") for i in range(2)]
    ids_ready = sem("t_ids_ready")
    ids_steps = sem("t_ids_steps")
    x_hi_done = sem("t_x_hi_done")
    rows_loaded = [sem(f"t_rows_loaded{i}") for i in range(2)]
    eye_ready = sem("t_eye_ready")
    rows_turned = sem("t_rows_turned")
    x_ready = sem("t_x_ready")
    mix_done = sem("t_mix_done")
    mix_ready = sem("t_mix_ready")
    w_split = sem("t_w_split")
    x_split = sem("t_x_split")
    z_done = sem("t_z_done")
    ff1_done = sem("t_ff1_done")
    ff2_done = sem("t_ff2_done")
    fwd_done = [sem(f"t_fwd_done{i}") for i in (1, 2)]
    back_done = sem("t_back_done")
    u2_ready = sem("t_u2_ready")
    stats_done = [sem(f"t_stats_done{i}") for i in (1, 2)]
    mv_done = [sem(f"t_mv_done{i}") for i in (1, 2)]
    ve_done = [sem(f"t_ve_done{i}") for i in (1, 2)]
    std_done = [sem(f"t_std_done{i}") for i in (1, 2)]
    rstd_done = [sem(f"t_rstd_done{i}") for i in (1, 2)]
    nmr_done = [sem(f"t_nmr_done{i}") for i in (1, 2)]
    xn_ready = [sem(f"t_xn_ready{i}") for i in (1, 2)]
    a32_ready = sem("t_a32_ready")
    a_hi_done = sem("t_a_hi_done")
    a_split = sem("t_a_split")
    h32_ready = sem("t_h32_ready")
    h_hi_ready = sem("t_h_hi_ready")
    h_lo_ready = sem("t_h_lo_ready")
    hi_written = sem("t_hi_written")
    fill_ready = sem("t_fill_ready")
    filled = sem("t_filled")

    SLOTS = LAYERS * NG
    LN1_W, LN1_B, LN2_W, LN2_B, FF_B2 = (DC * i for i in range(5))

    def slots(eng, body):
        for b in range(2):
            body(b, 0, b, 0)
        with eng.Fori(1, NG // 2) as j:
            for b in range(2):
                body(j * 2 + b, 0, b, 0)
        with eng.Fori(0, NG // 2) as j:
            for b in range(2):
                body(j * 2 + (NG + b), 1, b, 1)
        with eng.Fori(1, LAYERS // 2) as pair:
            for par in range(2):
                with eng.Fori(0, NG // 2) as j:
                    for b in range(2):
                        body(pair * (2 * NG) + j * 2 + (par * NG + b), pair * 2 + par, b, par)

    def w1(w, par, kc, m):
        at = kc * F + m * P
        return w[par][:, at // (G // 2), at % (G // 2):at % (G // 2) + P]

    def w2(w, par, k, oc):
        return w[par][:, k, G // 2 + oc * P:G // 2 + (oc + 1) * P]

    block = ctx.enter_context(nc.Block())

    @block.sync
    def _(sp):
        sp.dma_start(ids[:], io["ids"]).then_inc(ids_loaded, 16)
        sp.dma_start(vec[:, :, 0:10], io["vec"]).then_inc(vec_loaded, 16)
        sp.dma_start(b1[:], io["b1"]).then_inc(vec_loaded, 16)
        for l in range(LAYERS):
            if l >= 2:
                sp.wait_ge(mix_done, l - 1)
            sp.dma_start(a32[:, l % 2, :, :], io["wqo"][l]).then_inc(qo_loaded[l % 2], 16)
        for g in range(NG):
            if g >= 2:
                sp.wait_ge(w_split, g - 1)
            sp.dma_start(w_stage[:, g % 2, :], io["wf"][g]).then_inc(stage_loaded[g % 2], 16)
        with sp.Fori(0, SLOTS // 2) as i:
            for b in range(2):
                sp.wait_ge(w_split, i * 2 + (NG + b - 1))
                sp.dma_start(w_stage[:, b, :], io["wf"][(i * 2 + (NG + b)) % SLOTS]).then_inc(stage_loaded[b], 16)

    @block.gpsimd
    def _(pool):
        pool.memset(eye[:], 0.0).then_inc(eye_ready, 1)
        pool.wait_ge(eye_ready, 1)
        pool.affine_select(out=eye[:], in_=eye[:], compare_op=ALU.not_equal, fill=1.0, base=0,
                           pattern=[[-P, DC], [1, D]], channel_multiplier=-1).then_inc(eye_ready, 1)
        pool.memset(fill[:], 0.0).then_inc(fill_ready, 1)
        pool.wait_ge(fill_ready, 1)
        pool.iota(fill[:].bitcast(I32)[:, D:D + 1], pattern=[[0, 1]], base=N_TOK, channel_multiplier=1).then_inc(fill_ready, 1)
        pool.wait_ge(ids_ready, 1)
        for g in range(NG):
            if g >= 2:
                pool.wait_ge(rows_turned, g - 1)
            for t in range(GT):
                pool.indirect_dma_start(out=xn[g % 2][:, t, :], out_offset=None, in_=io["emb"],
                                        in_offset=bass.IndirectOffsetOnAxis(ap=idu[:, g * GT + t:g * GT + t + 1], axis=0),
                                        ).then_inc(rows_loaded[g % 2], 16)

        def body(s, l, b, par):
            for m in range(FC):
                count = held(pool, s * FC + (m + 1))
                pool.wait_ge(eye_ready, 2)
                pool.wait_ge(h32_ready, count)
                pool.tensor_copy(h_hi[:, m, :], h32[:, m % 2, :]).then_inc(h_hi_ready, 1)
        slots(pool, body)

    @block.scalar
    def _(act):
        act.wait_ge(vec_loaded, 32)
        for g in range(NG):
            act.wait_ge(rows_turned, g + 1)
            act.activation(x32[:, :, g * G:(g + 1) * G], ps_feat[:], ACT.Copy).then_inc(x_ready, 1)

        def root(n, k):
            act.wait_ge(ve_done[n], k + 1)
            act.activation(std[n][:], var_eps[n][:], ACT.Sqrt).then_inc(std_done[n], 1)

        def normalise(n, k, first, last):
            if first == 0:
                act.wait_ge(nmr_done[n], k + 1)
                if not (isinstance(k, int) and k == 0):
                    act.wait_ge(fwd_done[n], k)
                elif n == 0:
                    act.wait_ge(rows_turned, NG)
            for t in range(first, last):
                ins = act.activation(xn[n][:, t, :], ps_tok[:, t, :], ACT.Identity,
                                     scale=rstd[n][:, t:t + 1], bias=nmr[n][:, t:t + 1])
            if last == GT:
                ins.then_inc(xn_ready[n], 1)

        def scale_first(k, l, b):
            act.wait_ge(fwd_done[0], k + 1)
            if not (isinstance(k, int) and k < 2):
                act.wait_ge(u2_ready, k - 1)
            for c in range(DC):
                ins = act.activation(a32[:, b, c, :], ps_feat[:, c, :], ACT.Identity,
                                     scale=vec[:, l, LN1_W + c:LN1_W + c + 1],
                                     bias=vec[:, l, LN1_B + c:LN1_B + c + 1])
            ins.then_inc(a32_ready, 1)

        def scale_second(k, l):
            count = held(act, k + 1)
            act.wait_ge(vec_loaded, 32)
            act.wait_ge(fwd_done[1], count)
            g = k % NG
            for c in range(DC):
                ins = act.activation(x32[:, c, bass.ds(g * G, G)], ps_feat[:, c, :], ACT.Identity,
                                     scale=vec[:, l, LN2_W + c:LN2_W + c + 1],
                                     bias=vec[:, l, LN2_B + c:LN2_B + c + 1])
            ins.then_inc(x_ready, 1)

        def hidden(s, l, m):
            before = m >= 2 or not (isinstance(s, int) and s == 0)
            count = held(act, s * FC + (m + 1))
            free = held(act, s * FC + (m - 1)) if before else 0
            act.wait_ge(vec_loaded, 32)
            act.wait_ge(ff1_done, count)
            if before:
                act.wait_ge(h_lo_ready, free)
            act.activation(h32[:, m % 2, :], ps_h[:, m % 2, :], ACT.Relu,
                           bias=b1_of(l)[:, m:m + 1]).then_inc(h32_ready, 1)

        def b1_of(l):
            return b1[:, l, :]

        root(0, 0)
        normalise(0, 0, 0, GT)
        act.wait_ge(mix_ready, LAYERS)
        scale_first(0, 0, 0)
        act.wait_ge(fill_ready, 2)
        act.dma_start(acc[N_TOK:, :], fill[:, 0:D]).then_inc(filled, 16)
        by_row = rows_for.rearrange("(e r) c -> r e c", e=E)
        for t in range(ET):
            n = P if t < ET - 1 else LAST_ROWS
            act.dma_start(by_row[t * P:t * P + n], fill[0:n, :].unsqueeze(1).to_broadcast([n, E, REC])).then_inc(filled, 16)

        def body(s, l, b, par):
            two = not (isinstance(s, int) and s == 0)
            l_next, l_prev = ((s + 1) // NG) % LAYERS, (s - 1) // NG
            hidden(s, l, 0)
            hidden(s, l, 1)
            root(0, s + 1)
            normalise(0, s + 1, 0, 2)
            hidden(s, l, 2)
            normalise(0, s + 1, 2, GT)
            hidden(s, l, 3)
            hidden(s, l, 4)
            scale_first(s + 1, l_next, 1 - b)
            hidden(s, l, 5)
            hidden(s, l, 6)
            hidden(s, l, 7)
            if two:
                root(1, s - 1)
                normalise(1, s - 1, 0, GT)
                scale_second(s - 1, l_prev)
        slots(act, body)
        root(1, SLOTS - 1)
        normalise(1, SLOTS - 1, 0, GT)
        scale_second(SLOTS - 1, LAYERS - 1)
        act.wait_ge(filled, 16 * (1 + ET))

    @block.tensor
    def _(pe):
        pe.wait_ge(eye_ready, 2)
        ident_ap = eye[:, 0, 0:P]
        for l in range(LAYERS):
            pe.wait_ge(qo_loaded[l % 2], 16 * (l // 2 + 1))
            if l >= 2:
                pe.wait_ge(mix_ready, l - 1)
            for kc in range(DC):
                for hc in range(DC):
                    mm = pe.matmul(ps_h[:, l % 2, kc * D:(kc + 1) * D], a32[:, l % 2, 0, hc * D + kc * P:hc * D + (kc + 1) * P],
                                   a32[:, l % 2, 1, hc * D:(hc + 1) * D], start=(hc == 0), stop=(hc == DC - 1))
            mm.then_inc(mix_done, 1)
        for g in range(NG):
            pe.wait_ge(rows_loaded[g % 2], 16 * GT * (g // 2 + 1))
            if g >= 1:
                pe.wait_ge(x_ready, g)
            for t in range(GT):
                for c in range(DC):
                    tr = pe.transpose(ps_feat[:, c, t * P:(t + 1) * P], xn[g % 2][:, t, c * P:(c + 1) * P], ident_ap)
            tr.then_inc(rows_turned, 1)

        def passes(out, lhs, rhs, start, stop):
            pe.matmul(out, lhs[0], rhs[0], start=start, stop=False)
            pe.matmul(out, lhs[0], rhs[1], start=False, stop=False)
            return pe.matmul(out, lhs[1], rhs[0], start=False, stop=stop)

        def mixing(k):
            pe.wait_ge(x_split, k + 1)
            if isinstance(k, int) and k < 3:
                if k >= 1:
                    pe.wait_ge(xn_ready[0], k)
            else:
                pe.wait_ge(xn_ready[1], k - 2)
            for t in range(GT):
                for kc in range(DC):
                    tok = slice(t * P, (t + 1) * P)
                    mm = passes(ps_tok[:, t, :], (x_hi[:, kc, tok], x_lo[:, kc, tok]),
                                (mix_hi[:, kc, :], mix_lo[:, kc, :]), kc == 0, kc == DC - 1)
            mm.then_inc(z_done, 1)

        def forward(n, k):
            pe.wait_ge(xn_ready[n], k + 1)
            for c in range(DC):
                for t in range(GT):
                    tr = pe.transpose(ps_feat[:, c, t * P:(t + 1) * P], xn[n][:, t, c * P:(c + 1) * P], ident_ap)
            tr.then_inc(fwd_done[n], 1)

        def back(k):
            pe.wait_ge(u2_ready, k + 1)
            pe.wait_ge(xn_ready[0], k + 3)
            for t in range(GT):
                for c in range(DC):
                    tr = pe.transpose(ps_tok[:, t, c * P:(c + 1) * P], u2[:, c, t * P:(t + 1) * P], ident_ap)
            tr.then_inc(back_done, 1)

        def up(s, b, par, m):
            if m == 0:
                pe.wait_ge(a_split, s + 1)
            if not (isinstance(s, int) and s == 0 and m < 2):
                pe.wait_ge(h32_ready, s * FC + (m - 1))
            for kc in range(DC):
                mm = passes(ps_h[:, m % 2, :], (w1(w_hi, par, kc, m), w1(w_lo, par, kc, m)),
                            (a_hi[:, b, kc, :], a_lo[:, b, kc, :]), kc == 0, kc == DC - 1)
            mm.then_inc(ff1_done, 1)

        def down(s, par, k):
            if k == 0 and not (isinstance(s, int) and s == 0):
                pe.wait_ge(u2_ready, s)
            pe.wait_ge(h_hi_ready, s * FC + (k + 1))
            pe.wait_ge(h_lo_ready, s * FC + (k + 1))
            for oc in range(DC):
                mm = passes(ps_y[:, oc, :], (w2(w_hi, par, k, oc), w2(w_lo, par, k, oc)),
                            (h_hi[:, k, :], h_lo[:, k, :]), k == 0, k == FC - 1)
            if k == FC - 1:
                mm.then_inc(ff2_done, 1)

        pe.wait_ge(mix_ready, LAYERS)
        mixing(0)
        pe.wait_ge(x_ready, NG)
        forward(0, 0)

        def body(s, l, b, par):
            two = not (isinstance(s, int) and s == 0)
            mixing(s + 1)
            pe.wait_ge(w_split, l * NG + NG)
            for m in range(5):
                up(s, b, par, m)
            if isinstance(s, int) and s < 2:
                pe.wait_ge(a32_ready, s + 1)
            else:
                pe.wait_ge(x_ready, s + (NG - 1))
            forward(0, s + 1)
            for m in range(5, FC):
                up(s, b, par, m)
            if two:
                back(s - 1)
            for k in range(5):
                down(s, par, k)
            if two:
                pe.wait_ge(a32_ready, s + 2)
                forward(1, s - 1)
            for k in range(5, FC):
                down(s, par, k)
        slots(pe, body)
        pe.wait_ge(u2_ready, SLOTS)
        pe.wait_ge(xn_ready[0], SLOTS + 1)
        back_last = SLOTS - 1
        for t in range(GT):
            for c in range(DC):
                tr = pe.transpose(ps_tok[:, t, c * P:(c + 1) * P], u2[:, c, t * P:(t + 1) * P], ident_ap)
        tr.then_inc(back_done, 1)
        pe.wait_ge(x_ready, NG + SLOTS - 1)
        forward(1, back_last)

    @block.vector
    def _(dve):
        dve.wait_ge(ids_loaded, 16)
        dve.tensor_copy(idf[:, 0, :], ids[:]).then_inc(ids_steps, 1)
        dve.wait_ge(ids_steps, 1)
        dve.tensor_scalar(idf[:, 1, :], idf[:, 0, :], 0.0, float(VOCAB), ALU.is_lt, ALU.mult).then_inc(ids_steps, 1)
        dve.wait_ge(ids_steps, 2)
        dve.tensor_tensor(idf[:, 2, :], idf[:, 0, :], idf[:, 1, :], ALU.add).then_inc(ids_steps, 1)
        dve.wait_ge(ids_steps, 3)
        dve.tensor_scalar(idf[:, 0, :], idf[:, 2, :], 0.0, float(VOCAB - 1), ALU.max, ALU.min).then_inc(ids_steps, 1)
        dve.wait_ge(ids_steps, 4)
        dve.tensor_copy(idu[:], idf[:, 0, :]).then_inc(ids_ready, 1)

        def split_weights(n, par, b, g):
            dve.wait_ge(stage_loaded[b], (n // 2) * 16 + 16)
            dve.tensor_copy(w_hi[par][:, g, :], w_stage[:, b, :]).then_inc(hi_written, 1)
            return w_hi[par][:, g, :], w_lo[par][:, g, :], w_stage[:, b, :]

        for l in range(LAYERS):
            dve.wait_ge(eye_ready, 2)
            dve.wait_ge(mix_done, l + 1)
            dve.tensor_tensor(mix[:, l, :], ps_h[:, l % 2, :], eye[:].rearrange("p a b -> p (a b)"), ALU.add).then_inc(mix_ready, 1)
        for g in range(NG):
            hi, lo, raw = split_weights(g, 0, g % 2, g)
            dve.wait_ge(hi_written, g + 1)
            dve.tensor_tensor(lo, raw, hi.bitcast(F32), ALU.subtract).then_inc(w_split, 1)

        def split_x(k):
            dve.wait_ge(x_ready, k + 1)
            g, l = k % NG, (k // NG) % LAYERS
            for c in range(DC):
                dve.tensor_copy(x_hi[:, c, :], x32[:, c, bass.ds(g * G, G)])
            dve.tensor_copy(mix_hi[:].rearrange("p a b -> p (a b)"), mix[:, l, :]).then_inc(x_hi_done, 1)
            dve.wait_ge(x_hi_done, k + 1)
            for c in range(DC):
                dve.tensor_tensor(x_lo[:, c, :], x32[:, c, bass.ds(g * G, G)], x_hi[:, c, :].bitcast(F32), ALU.subtract)
            dve.tensor_tensor(mix_lo[:].rearrange("p a b -> p (a b)"), mix[:, l, :],
                              mix_hi[:].rearrange("p a b -> p (a b)").bitcast(F32), ALU.subtract).then_inc(x_split, 1)

        def statistics(n, k):
            if n == 0:
                dve.wait_ge(z_done, k + 1)
            else:
                dve.wait_ge(back_done, k + 1)
            for t in range(GT):
                ins = dve.bn_stats(stats[n][:, t, :], ps_tok[:, t, :])
            ins.then_inc(stats_done[n], 1)
            count = held(dve, k + 1)
            dve.wait_ge(eye_ready, 2)
            dve.wait_ge(stats_done[n], count)
            for t in range(GT):
                ins = dve.bn_aggr(mv[n][:, t, :], stats[n][:, t, :])
            ins.then_inc(mv_done[n], 1)
            dve.wait_ge(mv_done[n], k + 1)
            dve.tensor_scalar(var_eps[n][:], mv[n][:, :, 1], EPS, None, ALU.add).then_inc(ve_done[n], 1)

        def reciprocal(n, k):
            dve.wait_ge(std_done[n], k + 1)
            dve.reciprocal(rstd[n][:], std[n][:]).then_inc(rstd_done[n], 1)
            dve.wait_ge(rstd_done[n], k + 1)
            dve.scalar_tensor_tensor(out=nmr[n][:], in0=mv[n][:, :, 0], scalar=-1.0, in1=rstd[n][:],
                                     op0=ALU.mult, op1=ALU.mult).then_inc(nmr_done[n], 1)

        def split_a(k, b):
            dve.wait_ge(a32_ready, k + 1)
            dve.tensor_copy(a_hi[:, b], a32[:, b]).then_inc(a_hi_done, 1)
            dve.wait_ge(a_hi_done, k + 1)
            dve.tensor_tensor(a_lo[:, b], a32[:, b], a_hi[:, b].bitcast(F32), ALU.subtract).then_inc(a_split, 1)

        def residual(k, b, l):
            dve.wait_ge(ff2_done, k + 1)
            if not (isinstance(k, int) and k == 0):
                dve.wait_ge(back_done, k)
            for c in range(DC):
                ins = dve.scalar_tensor_tensor(out=u2[:, c, :], in0=ps_y[:, c, :], scalar=vec[:, l, FF_B2 + c:FF_B2 + c + 1],
                                               in1=a32[:, b, c, :], op0=ALU.add, op1=ALU.add)
            ins.then_inc(u2_ready, 1)

        def low_hidden(s, m):
            dve.wait_ge(h_hi_ready, s * FC + (m + 1))
            dve.tensor_tensor(h_lo[:, m, :], h32[:, m % 2, :], h_hi[:, m, :].bitcast(F32), ALU.subtract).then_inc(h_lo_ready, 1)

        split_x(0)
        statistics(0, 0)
        reciprocal(0, 0)
        split_x(1)
        split_a(0, 0)
        dve.wait_ge(vec_loaded, 32)

        def body(s, l, b, par):
            two = not (isinstance(s, int) and s == 0)
            if two:
                residual(s - 1, 1 - b, (s - 1) // NG)
            statistics(0, s + 1)
            low_hidden(s, 0)
            reciprocal(0, s + 1)
            low_hidden(s, 1)
            low_hidden(s, 2)
            split_x(s + 2)
            low_hidden(s, 3)
            low_hidden(s, 4)
            split_a(s + 1, 1 - b)
            for m in range(5, FC):
                low_hidden(s, m)
            if two:
                statistics(1, s - 1)
            piece(s, b, par)
            if two:
                reciprocal(1, s - 1)

        def piece(s, b, par):
            g = s % NG
            n = s + NG
            dve.wait_ge(stage_loaded[b], (n // 2) * 16 + 16)
            dve.tensor_copy(w_hi[1 - par][:, g, :], w_stage[:, b, :]).then_inc(hi_written, 1)
            dve.wait_ge(hi_written, n + 1)
            dve.tensor_tensor(w_lo[1 - par][:, g, :], w_stage[:, b, :], w_hi[1 - par][:, g, :].bitcast(F32),
                              ALU.subtract).then_inc(w_split, 1)

        slots(dve, body)
        residual(SLOTS - 1, 1, LAYERS - 1)
        statistics(1, SLOTS - 1)
        reciprocal(1, SLOTS - 1)


HEADS = 16
DH = 64
PAIRS = HEADS // 2
LOCAL_PAIRS = 2
SORT_PAIRS = PAIRS - LOCAL_PAIRS
SEQ = 2048
BATCH = N_TOK // SEQ
BK = 32
NB = SEQ // BK
BT = P // BK
ST = SEQ // P
SG = SEQ // G
NEG = -3.4028234663852886e38


def attention(nc, ctx, io, x32):
    def sb(name, shape, dt=F32):
        return ctx.enter_context(nc.sbuf_tensor("a_" + name, shape, dt))

    def sem(name):
        return ctx.enter_context(nc.semaphore("a_" + name))

    y_hi = sb("y_hi", [P, DC, N_TOK], F32R)
    y_lo = sb("y_lo", [P, DC, N_TOK], F32R)
    w_stage = sb("w_stage", [P, 4, D])
    w_hi = sb("w_hi", [P, 3, DC, P], F32R)
    w_lo = sb("w_lo", [P, 3, DC, P], F32R)
    wo_hi = sb("wo_hi", [P, D], F32R)
    wo_lo = sb("wo_lo", [P, D], F32R)
    q_t = sb("q_t", [P, SEQ])
    keys = sb("keys", [P, 2, SEQ + 2])
    v_t = sb("v_t", [P, SEQ + 2 * BK])
    k_bk = sb("k_bk", [P, BK // 2, P])
    v_bk = sb("v_bk", [P, BK // 2, P])
    v_tok = [sb(f"v_tok{i}", [P, ST, P]) for i in range(2)]
    scratch = sb("scratch", [P, 2, 1024])
    p_t = sb("p_t", [P, 2, 1024])
    att_hi = sb("att_hi", [P, SEQ], F32R)
    att_lo = sb("att_lo", [P, SEQ], F32R)
    ident = sb("ident", [P, P])
    stats = q_t[:, 0:GT * 6].rearrange("p (t n) -> p t n", t=GT)
    mv = q_t[:, 64:64 + GT * 2].rearrange("p (t n) -> p t n", t=GT)
    var_eps, std, rstd, nmr = (q_t[:, 128 + 64 * n:128 + 64 * n + GT] for n in range(4))
    b_out = sb("b_out", [P, DC])
    sort_w = sb("sort_w", [P, 2, NB])
    sums = sb("sums", [P, 2, NB])
    r_log = sb("r_log", [P, NB])
    r_two = sb("r_two", [P, 2, NB])
    r_t = sb("r_t", [P, P])
    r_small = sb("r_small", [P, 4])
    s_max = sb("s_max", [P, 16])
    s_sum = sb("s_sum", [P, 16])
    s_inv = sb("s_inv", [P, 16])
    mixed_t = scratch[:].rearrange("p a b -> p (a b)")
    v_by_t = mixed_t
    own_keys = keys[:, 0, 1:1 + SEQ]
    mixed_keys = keys[:, 1, 1:1 + SEQ]
    xn = [v_tok[i][:, 0:8, :].rearrange("p a b -> p (a b)").rearrange("p (t d) -> p t d", t=GT) for i in range(2)]
    values = {True: [v_tok[0], v_tok[1], k_bk], False: [v_tok[0], v_tok[1]]}
    probs = [p_t, v_bk[:].rearrange("p a b -> p (a b)").rearrange("p (u n) -> p u n", u=2)]

    ring = ctx.enter_context(nc.psum_tensor("a_ring", [P, 4, G], F32))
    quad = ctx.enter_context(nc.psum_tensor("a_quad", [P, 4, G], F32))

    ident_ready = sem("ident_ready")
    bias_loaded = sem("bias_loaded")
    pads_ready = sem("pads_ready")
    back_done = sem("back_done")
    norm_steps = sem("norm_steps")
    ve_done = sem("ve_done")
    std_done = sem("std_done")
    nmr_done = sem("nmr_done")
    xn_ready = sem("xn_ready")
    fwd_done = sem("fwd_done")
    y_hi_ready = sem("y_hi_ready")
    y_ready = sem("y_ready")
    bias_added = sem("bias_added")
    w_loaded = sem("w_loaded")
    w_hi_done = sem("w_hi_done")
    w_ready = sem("w_ready")
    wo_ready = sem("wo_ready")
    sort_loaded = sem("sort_loaded")
    proj_done = sem("proj_done")
    proj_read = sem("proj_read")
    sums_done = sem("sums_done")
    v_by_t_ready = sem("v_by_t_ready")
    turned = {True: sem("turned_local"), False: sem("turned_sort")}
    turned_read = {True: sem("turned_read_local"), False: sem("turned_read_sort")}
    logits_done = sem("logits_done")
    logits_read = sem("logits_read")
    r_max_done = sem("r_max_done")
    r_neg_done = sem("r_neg_done")
    r_exp_done = sem("r_exp_done")
    r_inv_done = sem("r_inv_done")
    r_two_done = sem("r_two_done")
    r_turned = sem("r_turned")
    r_ready = sem("r_ready")
    mix_done = sem("mix_done")
    mix_read = sem("mix_read")
    kinds = {True: "local", False: "sort"}
    s_done = {k: sem("s_done_" + n) for k, n in kinds.items()}
    s_read = {k: sem("s_read_" + n) for k, n in kinds.items()}
    s_masked = sem("s_masked")
    s_max_done = {k: sem("s_max_done_" + n) for k, n in kinds.items()}
    s_sub_done = {k: sem("s_sub_done_" + n) for k, n in kinds.items()}
    s_exp_done = {k: sem("s_exp_done_" + n) for k, n in kinds.items()}
    s_sum_done = {k: sem("s_sum_done_" + n) for k, n in kinds.items()}
    s_inv_done = {k: sem("s_inv_done_" + n) for k, n in kinds.items()}
    s_norm_done = {k: sem("s_norm_done_" + n) for k, n in kinds.items()}
    p_ready = {k: sem("p_ready_" + n) for k, n in kinds.items()}
    pv_done = sem("pv_done")
    att_hi_ready = sem("att_hi_ready")
    att_ready = sem("att_ready")
    out_done = sem("out_done")
    x_added = sem("x_added")

    UNITS = {True: 4, False: 2}
    TILES = {True: ST // 4, False: ST // 2}
    BLOCKS = {True: 3, False: 2}
    SCALE = {True: 1.0, False: DH ** -0.5}

    def pairs(eng, body):
        with eng.Fori(0, BATCH) as b:
            with eng.Fori(0, LOCAL_PAIRS) as c:
                body(b * PAIRS + c, b * LOCAL_PAIRS + c, True)
            with eng.Fori(0, SORT_PAIRS) as c:
                body(b * PAIRS + c + LOCAL_PAIRS, b * SORT_PAIRS + c, False)

    block = ctx.enter_context(nc.Block())

    @block.sync
    def _(sp):
        sp.dma_start(b_out[:], io["b_out"]).then_inc(bias_loaded, 16)
        sp.dma_start(w_stage[:], io["wa"][0]).then_inc(w_loaded, 16)

        def body(i, n, local):
            if not local:
                sp.wait_ge(r_max_done, n + 1)
                sp.dma_start(sort_w[:], io["sort_w"][n % SORT_PAIRS]).then_inc(sort_loaded, 16)
            sp.wait_ge(wo_ready, i + 1)
            sp.dma_start(w_stage[:], io["wa"][(i + 1) % PAIRS]).then_inc(w_loaded, 16)
        pairs(sp, body)
        sp.wait_ge(w_loaded, 16 * (BATCH * PAIRS + 1))

    @block.gpsimd
    def _(pool):
        pool.memset(ident[:], 0.0).then_inc(ident_ready, 1)
        pool.wait_ge(ident_ready, 1)
        pool.affine_select(out=ident[:], in_=ident[:], compare_op=ALU.not_equal, fill=1.0, base=0,
                           pattern=[[-1, P]], channel_multiplier=1).then_inc(ident_ready, 1)
        pool.memset(keys[:, 0, 0:1], 0.0)
        pool.memset(keys[:, 0, SEQ + 1:], 0.0)
        pool.memset(v_t[:, 0:BK], 0.0)
        pool.memset(v_t[:, BK + SEQ:], 0.0).then_inc(pads_ready, 1)

        pool.wait_ge(bias_loaded, 16)
        for g in range(NG):
            pool.wait_ge(back_done, g + 1)
            for c in range(DC):
                xs = x32[:, c, g * G:(g + 1) * G]
                ins = pool.tensor_scalar(xs, xs, b_out[:, c:c + 1], None, ALU.add)
            ins.then_inc(bias_added, 1)

        def split_weights(i):
            count = held(pool, i * 16 + 16)
            pool.wait_ge(ident_ready, 2)
            pool.wait_ge(w_loaded, count)
            pool.tensor_copy(w_hi[:].rearrange("p a b c -> p (a b c)"), w_stage[:, 0:3, :].rearrange("p a b -> p (a b)")).then_inc(w_hi_done, 1)
            pool.wait_ge(w_hi_done, i * 2 + 1)
            pool.tensor_tensor(w_lo[:].rearrange("p a b c -> p (a b c)"), w_stage[:, 0:3, :].rearrange("p a b -> p (a b)"),
                               w_hi[:].rearrange("p a b c -> p (a b c)").bitcast(F32), ALU.subtract).then_inc(w_ready, 1)

        def split_out_weights(i):
            pool.tensor_copy(wo_hi[:], w_stage[:, 3, :]).then_inc(w_hi_done, 1)
            pool.wait_ge(w_hi_done, i * 2 + 2)
            pool.tensor_tensor(wo_lo[:], w_stage[:, 3, :], wo_hi[:].bitcast(F32), ALU.subtract).then_inc(wo_ready, 1)

        split_weights(0)
        split_out_weights(0)

        def body(i, n, local):
            if not local:
                count = held(pool, i * 12 + 12)
                pool.wait_ge(ident_ready, 2)
                pool.wait_ge(proj_read, count)
                pool.tensor_copy(v_by_t.rearrange("p (t v) -> p v t", v=NB),
                                 v_t[:, BK:BK + SEQ].rearrange("p (v t) -> p v t", t=BK)).then_inc(v_by_t_ready, 1)
            pool.wait_ge(proj_done, i * 12 + 12)
            split_weights(i + 1)
            count = held(pool, i * 8 + 8)
            pool.wait_ge(ident_ready, 2)
            pool.wait_ge(out_done, count)
            split_out_weights(i + 1)
        pairs(pool, body)

    @block.scalar
    def _(act):
        for g in range(NG):
            act.wait_ge(ve_done, g + 1)
            act.activation(std, var_eps, ACT.Sqrt).then_inc(std_done, 1)
            act.wait_ge(nmr_done, g + 1)
            if g >= 2:
                act.wait_ge(fwd_done, g - 1)
            for t in range(GT):
                ins = act.activation(xn[g % 2][:, t, :], ring[:, (g % 2) * 2 + t // 2, (t % 2) * D:(t % 2 + 1) * D], ACT.Identity,
                                     scale=rstd[:, t:t + 1], bias=nmr[:, t:t + 1])
            ins.then_inc(xn_ready, 1)
            act.wait_ge(fwd_done, g + 1)
            act.activation(y_hi[:, :, g * G:(g + 1) * G], quad[:, (g % 2) * 2:(g % 2) * 2 + 2, :], ACT.Copy).then_inc(y_hi_ready, 1)

        def read_projection(i):
            for j in range(12):
                kind, g = j // SG, j % SG
                act.wait_ge(proj_done, i * 12 + (j + 1))
                src = ring[:, j % 4, :]
                if kind == 0:
                    ins = act.activation(q_t[:, g * G:(g + 1) * G], src, ACT.Copy)
                elif kind == 1:
                    nb = G // BK
                    ins = act.activation(own_keys.rearrange("p (t v) -> p v t", v=NB)[:, g * nb:(g + 1) * nb, :],
                                         src.rearrange("p (v t) -> p v t", t=BK), ACT.Copy)
                else:
                    ins = act.activation(v_t[:, BK + g * G:BK + (g + 1) * G], src, ACT.Copy)
                ins.then_inc(proj_read, 1)

        read_projection(0)

        def body(i, n, local):
            per = 12 if local else 16
            dests = values[True] if local else [k_bk, v_tok[0], v_bk]

            def read_turned(first, last):
                for c in range(first, last):
                    act.wait_ge(turned[local], n * per + (c + 1))
                    dest = dests[c // 4] if c < 12 else v_tok[1]
                    act.activation(dest[:, (c % 4) * 4:(c % 4) * 4 + 4, :].rearrange("p a b -> p (a b)"), ring[:, c % 4, :], ACT.Copy)\
                       .then_inc(turned_read[local], 1)

            read_turned(0, 12)
            if not local:
                for r in range(2):
                    act.wait_ge(logits_done, n * 2 + (r + 1))
                    act.activation(r_log[r * DH:(r + 1) * DH, :], ring[r * DH:(r + 1) * DH, r, 0:NB], ACT.Relu).then_inc(logits_read, 1)
                act.wait_ge(r_neg_done, n + 1)
                act.activation(r_log[:], r_log[:], ACT.Exp, bias=r_small[:, 1:2], accum_out=r_small[:, 2:3]).then_inc(r_exp_done, 1)
                act.wait_ge(r_turned, n + 1)
                act.activation(r_t[:], ring[:, 2, 0:P], ACT.Copy).then_inc(r_ready, 1)
                read_turned(12, 16)
            U, T, W = UNITS[local], TILES[local], BLOCKS[local] * BK

            def read_scores(u):
                act.wait_ge(s_done[local], n * U + (u + 1))
                if u >= 2:
                    act.wait_ge(p_ready[local], n * U + (u - 1))
                act.activation(scratch[:, u % 2, 0:2 * T * W].rearrange("p (r n) -> p r n", r=2),
                               quad[:, (u % 2) * 2:(u % 2) * 2 + 2, 0:T * W], ACT.Copy, scale=SCALE[local]).then_inc(s_read[local], 1)

            def exponent(u):
                act.wait_ge(s_sub_done[local], n * U + (u + 1))
                sc = scratch[:, u % 2, 0:2 * T * W]
                act.activation(sc, sc, ACT.Exp).then_inc(s_exp_done[local], 1)

            read_scores(0)
            read_scores(1)
            for u in range(U):
                exponent(u)
                if u + 2 < U:
                    read_scores(u + 2)
            read_projection(i + 1)
            for j in range(BT):
                if j == 0:
                    act.wait_ge(pv_done, i + 1)
                act.activation(att_hi[:].rearrange("p (t j q) -> p t j q", j=BT, q=BK)[:, :, j, :],
                               quad[:, j, :].rearrange("p (t q) -> p t q", q=BK), ACT.Copy).then_inc(att_hi_ready, 1)
        pairs(act, body)

    @block.tensor
    def _(pe):
        pe.wait_ge(ident_ready, 2)

        def back(g):
            if g >= 2:
                pe.wait_ge(xn_ready, g - 1)
            for t in range(GT):
                for c in range(DC):
                    tr = pe.transpose(ring[:, (g % 2) * 2 + t // 2, (t % 2) * D + c * P:(t % 2) * D + (c + 1) * P],
                                      x32[:, c, g * G + t * P:g * G + (t + 1) * P], ident[:])
            tr.then_inc(back_done, 1)

        back(0)
        for g in range(NG):
            if g + 1 < NG:
                back(g + 1)
            pe.wait_ge(xn_ready, g + 1)
            if g >= 2:
                pe.wait_ge(y_ready, g - 1)
            for c in range(DC):
                for t in range(GT):
                    tr = pe.transpose(quad[:, (g % 2) * 2 + c, t * P:(t + 1) * P], xn[g % 2][:, t, c * P:(c + 1) * P], ident[:])
            tr.then_inc(fwd_done, 1)

        def around(h, bk):
            first = keys[h, 0, bk:bk + 3]
            return bass.AP(tensor=first.tensor, offset=first.offset, ap=[first.ap[0], [1, 3], [NB, BK]])

        def passes(out, lhs, rhs, start, stop):
            pe.matmul(out, lhs[0], rhs[0], start=start, stop=False)
            pe.matmul(out, lhs[0], rhs[1], start=False, stop=False)
            return pe.matmul(out, lhs[1], rhs[0], start=False, stop=stop)

        def project(i):
            pe.wait_ge(w_ready, i + 1)
            at = ((i // PAIRS) % BATCH) * SEQ
            for j in range(12):
                kind, g = j // SG, j % SG
                if j >= 4:
                    pe.wait_ge(proj_read, i * 12 + (j - 3))
                for kc in range(DC):
                    mm = passes(ring[:, j % 4, :], (w_hi[:, kind, kc, :], w_lo[:, kind, kc, :]),
                                (y_hi[:, kc, bass.ds(at + g * G, G)], y_lo[:, kc, bass.ds(at + g * G, G)]), kc == 0, kc == DC - 1)
                mm.then_inc(proj_done, 1)

        pe.wait_ge(y_ready, NG)
        project(0)
        pe.wait_ge(pads_ready, 1)

        def body(i, n, local):
            per = 12 if local else 16
            pe.wait_ge(proj_read, i * 12 + 12)
            pe.wait_ge(x_added, i * 8 + 1)

            def turn(c, sources):
                if c >= 4:
                    pe.wait_ge(turned_read[local], n * per + (c - 3))
                for k, src in enumerate(sources):
                    tr = pe.transpose(ring[:, c % 4, k * P:(k + 1) * P], src, ident[:])
                tr.then_inc(turned[local], 1)

            if local:
                for w in range(3):
                    for c in range(4):
                        turn(4 * w + c, [v_t[:, w * BK + t * P:w * BK + (t + 1) * P] for t in range(4 * c, 4 * c + 4)])
            else:
                for c in range(4):
                    turn(c, [own_keys[:, m * P:(m + 1) * P] for m in range(4 * c, 4 * c + 4)])
                for c in range(4):
                    turn(4 + c, [v_t[:, BK + t * P:BK + (t + 1) * P] for t in range(4 * c, 4 * c + 4)])
                pe.wait_ge(v_by_t_ready, n + 1)
                for c in range(4):
                    turn(8 + c, [v_by_t[:, m * P:(m + 1) * P] for m in range(4 * c, 4 * c + 4)])
                pe.wait_ge(sums_done, n * 2 + 2)
                pe.wait_ge(sort_loaded, n * 16 + 16)
                for r in range(2):
                    count = held(pe, n * per + (9 + r))
                    pe.wait_ge(ident_ready, 2)
                    pe.wait_ge(turned_read[False], count)
                    h = slice(r * DH, (r + 1) * DH)
                    pe.matmul(ring[h, r, 0:NB], sums[h, 0, :], sort_w[h, 0, :], start=True, stop=False)
                    pe.matmul(ring[h, r, 0:NB], sums[h, 1, :], sort_w[h, 1, :], start=False, stop=True).then_inc(logits_done, 1)
                pe.wait_ge(turned_read[False], n * per + 12)
                pe.wait_ge(r_two_done, n + 1)
                pe.transpose(ring[:, 2, 0:P], r_two[:].rearrange("p a b -> p (a b)"), ident[:]).then_inc(r_turned, 1)
                pe.wait_ge(r_ready, n + 1)
                for unit in range(4):
                    src = (k_bk, v_bk)[unit // 2]
                    count = held(pe, n * 8 + (2 * unit - 2) if unit >= 2 else i * 4 + 1)
                    pe.wait_ge(ident_ready, 2)
                    if unit >= 2:
                        pe.wait_ge(mix_read, count)
                    else:
                        pe.wait_ge(att_ready, count)
                    for m in range(8):
                        for tp in range(2):
                            for r in range(2):
                                half = slice(tp * DH, (tp + 1) * DH)
                                mm = pe.matmul(quad[r * DH:(r + 1) * DH, (unit % 2) * 2 + tp, m * NB:(m + 1) * NB],
                                               src[half, (unit % 2) * 8 + m, r * DH:(r + 1) * DH],
                                               r_t[half, r * NB:(r + 1) * NB], start=True, stop=True)
                    mm.then_inc(mix_done, 1)
                pe.wait_ge(mix_read, n * 8 + 8)
                for c in range(4):
                    if c < 3:
                        pe.wait_ge(logits_read, n * 2 + 2)
                    turn(12 + c, [mixed_t[:, t * P:(t + 1) * P] for t in range(4 * c, 4 * c + 4)])
            U, T, W = UNITS[local], TILES[local], BLOCKS[local]
            for u in range(U):
                if u >= 2 or local:
                    count = held(pe, n * U + (u - 1) if u >= 2 else i * 4 + 1)
                    pe.wait_ge(ident_ready, 2)
                    pe.wait_ge(s_read[local] if u >= 2 else att_ready, count)
                for t in range(u * T, (u + 1) * T):
                    for r in range(2):
                        h = slice(r * DH, (r + 1) * DH)
                        for j in range(BT):
                            bk = t * BT + j
                            if local:
                                rhs = around(h, bk)
                            else:
                                rhs = keys[h, :, 1 + bk:1 + bk + SEQ - NB + 1:NB]
                            out = quad[j * BK:(j + 1) * BK, (u % 2) * 2 + r, (t % T) * W * BK:(t % T + 1) * W * BK]
                            mm = pe.matmul(out.rearrange("p (a b) -> p a b", b=BK), q_t[h, bk * BK:(bk + 1) * BK], rhs, start=True, stop=True)
                mm.then_inc(s_done[local], 1)
            pe.wait_ge(turned_read[local], n * per + per)
            if not local:
                pe.wait_ge(r_ready, n + 1)
            project(i + 1)
            for u in range(U):
                pe.wait_ge(p_ready[local], n * U + (u + 1))
                if u == 0:
                    pe.wait_ge(s_read[local], n * U + U)
                pt = (probs[u // 2][:, u % 2, :])[:, 0:2 * T * W * BK].rearrange("p (r t w q) -> p r t w q", r=2, t=T, w=W)
                for t in range(T):
                    for r in range(2):
                        for j in range(BT):
                            rows = slice(j * BK, (j + 1) * BK)
                            tile = u * T + t
                            for w in range(W):
                                mm = pe.matmul(quad[r * DH:(r + 1) * DH, j, tile * BK:(tile + 1) * BK],
                                               values[local][w][rows, tile, r * DH:(r + 1) * DH], pt[rows, r, t, w, :],
                                               start=(w == 0), stop=(w == W - 1))
            mm.then_inc(pv_done, 1)
            pe.wait_ge(att_ready, i * 4 + 5)
            pe.wait_ge(wo_ready, i + 1)
            for j in range(8):
                g, oc = j // 2, j % 2
                if j < 4:
                    pe.wait_ge(proj_read, i * 12 + 24)
                else:
                    pe.wait_ge(x_added, i * 8 + (j - 2))
                cols = slice(g * G, (g + 1) * G)
                passes(ring[:, j % 4, :], (wo_hi[:, oc * P:(oc + 1) * P], wo_lo[:, oc * P:(oc + 1) * P]),
                       (att_hi[:, cols], att_lo[:, cols]), True, True).then_inc(out_done, 1)
        pairs(pe, body)

    @block.vector
    def _(dve):
        for g in range(NG):
            dve.wait_ge(back_done, g + 1)
            for t in range(GT):
                ins = dve.bn_stats(stats[:, t, :], ring[:, (g % 2) * 2 + t // 2, (t % 2) * D:(t % 2 + 1) * D])
            ins.then_inc(norm_steps, 1)
            dve.wait_ge(norm_steps, 3 * g + 1)
            for t in range(GT):
                ins = dve.bn_aggr(mv[:, t, :], stats[:, t, :])
            ins.then_inc(norm_steps, 1)
            dve.wait_ge(norm_steps, 3 * g + 2)
            dve.tensor_scalar(var_eps, mv[:, :, 1], EPS, None, ALU.add).then_inc(ve_done, 1)
            dve.wait_ge(std_done, g + 1)
            if g >= 1:
                dve.wait_ge(xn_ready, g)
            dve.reciprocal(rstd, std).then_inc(norm_steps, 1)
            dve.wait_ge(norm_steps, 3 * g + 3)
            dve.scalar_tensor_tensor(out=nmr, in0=mv[:, :, 0], scalar=-1.0, in1=rstd,
                                     op0=ALU.mult, op1=ALU.mult).then_inc(nmr_done, 1)
            dve.wait_ge(y_hi_ready, g + 1)
            ys = slice(g * G, (g + 1) * G)
            dve.tensor_tensor(y_lo[:, :, ys], quad[:, (g % 2) * 2:(g % 2) * 2 + 2, :], y_hi[:, :, ys].bitcast(F32), ALU.subtract).then_inc(y_ready, 1)
        dve.memset(s_max[:], 0.0).then_inc(r_max_done, 1)
        dve.memset(s_sum[:], 0.0).then_inc(x_added, 1)
        dve.memset(s_inv[:], 0.0).then_inc(att_ready, 1)
        dve.wait_ge(bias_added, NG)

        def body(i, n, local):
            if not local:
                for k, src in enumerate((q_t[:].rearrange("p (v t) -> p v t", t=BK), own_keys.rearrange("p (t v) -> p v t", v=NB))):
                    dve.wait_ge(proj_read, i * 12 + 4 * (k + 1))
                    dve.tensor_reduce(sums[:, k, :], src, AX.X, ALU.add).then_inc(sums_done, 1)
                dve.wait_ge(logits_read, n * 2 + 2)
                dve.tensor_reduce(r_small[:, 0:1], r_log[:], AX.X, ALU.max).then_inc(r_max_done, 1)
                dve.wait_ge(r_max_done, n + 2)
                dve.tensor_scalar(r_small[:, 1:2], r_small[:, 0:1], -1.0, None, ALU.mult).then_inc(r_neg_done, 1)
                dve.wait_ge(r_exp_done, n + 1)
                dve.reciprocal(r_small[:, 3:4], r_small[:, 2:3]).then_inc(r_inv_done, 1)
                dve.wait_ge(r_inv_done, n + 1)
                for c in range(2):
                    ins = dve.tensor_scalar(r_two[:, c, :], r_log[:], r_small[:, 3:4], None, ALU.mult)
                ins.then_inc(r_two_done, 1)
                dest_k = mixed_keys.rearrange("p (t u) -> p t u", u=NB)
                dest_v = mixed_t.rearrange("p (u t) -> p t u", t=BK)
                for unit in range(4):
                    dve.wait_ge(mix_done, n * 4 + (unit + 1))
                    for tp in range(2):
                        dest = (dest_k, dest_v)[unit // 2][:, (unit % 2) * 16 + tp:(unit % 2) * 16 + 16:2, :]
                        dve.tensor_copy(dest, quad[:, (unit % 2) * 2 + tp, :].rearrange("p (m u) -> p m u", u=NB)).then_inc(mix_read, 1)
            U, T, W = UNITS[local], TILES[local], BLOCKS[local] * BK
            for u in range(U):
                k = n * U + u
                sc = scratch[:, u % 2, 0:2 * T * W]
                rows3 = sc.rearrange("p (a w) -> p a w", w=W)
                dve.wait_ge(s_read[local], k + 1)
                if local and u == 0:
                    dve.memset(sc.rearrange("p (r t w) -> p r t w", r=2, t=T)[0:BK, :, 0, 0:BK], NEG).then_inc(s_masked, 1)
                    dve.wait_ge(s_masked, n * 2 + 1)
                if local and u == U - 1:
                    dve.memset(sc.rearrange("p (r t w) -> p r t w", r=2, t=T)[P - BK:P, :, T - 1, 2 * BK:3 * BK], NEG).then_inc(s_masked, 1)
                    dve.wait_ge(s_masked, n * 2 + 2)
                mx, sm, iv = (x[:, 0:2 * T] for x in (s_max, s_sum, s_inv))
                dve.tensor_reduce(mx, rows3, AX.X, ALU.max).then_inc(s_max_done[local], 1)
                dve.wait_ge(s_max_done[local], k + 1)
                dve.tensor_tensor(rows3, rows3, mx.unsqueeze(2).to_broadcast([P, 2 * T, W]), ALU.subtract).then_inc(s_sub_done[local], 1)
                dve.wait_ge(s_exp_done[local], k + 1)
                dve.tensor_reduce(sm, rows3, AX.X, ALU.add).then_inc(s_sum_done[local], 1)
                dve.wait_ge(s_sum_done[local], k + 1)
                dve.reciprocal(iv, sm).then_inc(s_inv_done[local], 1)
                dve.wait_ge(s_inv_done[local], k + 1)
                dve.tensor_tensor(rows3, rows3, iv.unsqueeze(2).to_broadcast([P, 2 * T, W]), ALU.mult).then_inc(s_norm_done[local], 1)
                dve.wait_ge(s_norm_done[local], k + 1)
                dve.transpose(probs[u // 2][:, u % 2, 0:2 * T * W], sc).then_inc(p_ready[local], 1)
            for j in range(BT):
                dve.wait_ge(att_hi_ready, i * 4 + (j + 1))
                tj = "p (t j q) -> p t j q"
                dve.tensor_tensor(att_lo[:].rearrange(tj, j=BT, q=BK)[:, :, j, :], quad[:, j, :].rearrange("p (t q) -> p t q", q=BK),
                                  att_hi[:].bitcast(F32).rearrange(tj, j=BT, q=BK)[:, :, j, :], ALU.subtract).then_inc(att_ready, 1)
            at = (i // PAIRS) * SEQ
            for j in range(8):
                g, oc = j // 2, j % 2
                dve.wait_ge(out_done, i * 8 + (j + 1))
                xs = x32[:, oc, bass.ds(at + g * G, G)]
                dve.tensor_tensor(xs, ring[:, j % 4, :], xs, ALU.add).then_inc(x_added, 1)
        pairs(dve, body)


E = 7
CAP = 732
ET = -(-CAP // P)
LAST_ROWS = CAP - (ET - 1) * P
HALF = CAP // 2
REC = D + 4
NT = N_TOK // P
ES = 8
WC = 3 * D
SKIP = 1.0e6


def experts(nc, ctx, io, x32, rows_for, acc):
    def sb(name, shape, dt=F32):
        return ctx.enter_context(nc.sbuf_tensor("e_" + name, shape, dt))

    def sem(name):
        return ctx.enter_context(nc.semaphore("e_" + name))

    rec = sb("rec", [P, NT, REC])
    w_hi = sb("w_hi", [P, FC, WC], F32R)
    w_lo = sb("w_lo", [P, FC, WC], F32R)
    w_stage = sb("w_stage", [P, 2, WC])
    f_hi = sb("f_hi", [P, 2, DC, 768], F32R)
    f_lo = sb("f_lo", [P, 2, DC, 768], F32R)
    f32 = sb("f32", [P, DC, 768])
    xr = sb("xr", [P, ET, REC])
    s32 = sb("s32", [P, 2, G])
    g32 = sb("g32", [P, 768])
    g_hi = sb("g_hi", [P, 2, 768], F32R)
    g_lo = sb("g_lo", [P, 2, 768], F32R)
    yo = sb("yo", [P, ET, D])
    xn = [yo[:, 0:GT, :], f32[:].rearrange("p c n -> p (c n)")[:, 0:GT * D].rearrange("p (t d) -> p t d", t=GT)]
    ht = sb("ht", [P, 2, GT, D])
    ident = sb("ident", [P, P])
    below = sb("below", [P, P])
    ones = sb("ones", [P, P])
    ln_g = sb("ln_g", [P, DC])
    ln_b = sb("ln_b", [P, DC])
    w_r = sb("w_r", [P, DC, E])
    stats = sb("stats", [P, GT, 6])
    mv = sb("mv", [P, GT, 2])
    var_eps = sb("ve", [P, GT])
    std = sb("std", [P, GT])
    rstd = sb("rstd", [P, GT])
    nmr = sb("nmr", [P, GT])
    iot = sb("iot", [P, 3, ES], I32)
    cst = sb("cst", [P, 3, ES])
    lg = sb("lg", [P, NT, ES])
    eq = sb("eq", [P, NT, ES])
    hot = sb("hot", [P, 2, NT, ES])
    top = sb("top", [P, 2, NT])
    which = sb("which", [P, 2, NT])
    small = sb("small", [P, 4, NT])
    tot = sb("tot", [P, ES])
    before = sb("before", [DH, 2 * NT, ES])
    at_pos = sb("at_pos", [P, 2 * NT, ES])
    place = sb("place", [P, 4, 2 * NT])
    place_u = sb("place_u", [P, 2 * NT], U32)
    gate = sb("gate", [P, ET])
    gtmp = sb("gtmp", [P, 2, ET])
    tok = sb("tok", [P, ET], I32)

    ps = ctx.enter_context(nc.psum_tensor("e_ps", [P, 8, G], F32))

    consts_ready = sem("consts_ready")
    iota_done = sem("iota_done")
    cst_done = sem("cst_done")
    small_loaded = sem("small_loaded")
    back_done = sem("back_done")
    norm_steps = sem("norm_steps")
    ve_done = sem("ve_done")
    std_done = sem("std_done")
    nmr_done = sem("nmr_done")
    xn_ready = sem("xn_ready")
    ht_ready = sem("ht_ready")
    ht_sent = [sem(f"ht_sent{i}") for i in range(2)]
    rec_ready = sem("rec_ready")
    fwd_done = sem("fwd_done")
    feat_ready = sem("feat_ready")
    logits_done = sem("logits_done")
    route = sem("route")
    gap_ready = sem("gap_ready")
    gate_exp_done = sem("gate_exp_done")
    hot_ready = sem("hot_ready")
    tot_done = sem("tot_done")
    before_ready = sem("before_ready")
    pos_done = sem("pos_done")
    place_ready = sem("place_ready")
    dispatched = sem("dispatched")
    w_loaded = [sem(f"w_loaded{i}") for i in range(2)]
    w_hi_done = sem("w_hi_done")
    w_ready = sem("w_ready")
    f_hi_done = sem("f_hi_done")
    f_ready = sem("f_ready")
    xr_loaded = sem("xr_loaded")
    xr_zeroed = sem("xr_zeroed")
    turned = sem("turned")
    f32_ready = sem("f32_ready")
    up_done = sem("up_done")
    silu_done = sem("silu_done")
    prod_done = sem("prod_done")
    g_hi_ready = sem("g_hi_ready")
    g_lo_ready = sem("g_lo_ready")
    down_done = sem("down_done")
    y_read = sem("y_read")
    y_sent = sem("y_sent")
    tok_done = sem("tok_done")
    gate_steps = sem("gate_steps")
    gate_ready = sem("gate_ready")

    JS = NG

    def jobs(eng, body):
        for g in (0, 1):
            body(g, g, None)
        with eng.Fori(1, JS // 2 - 1) as i:
            for b in range(2):
                body(i * 2 + b, b, None)
        for g in (JS - 2, JS - 1):
            body(g, g % 2, None)
        with eng.Fori(0, E - 1) as e:
            body(e + JS, None, e)
        body(JS + E - 1, (E - 1) % 2, E - 1)

    def is_first(j):
        return isinstance(j, int) and j == 0

    def is_last_shared(j):
        return isinstance(j, int) and j == JS - 1

    def has_next(j, e):
        return is_last_shared(j) if e is None else not isinstance(j, int)

    def part(j, e, m, h=0):
        return j * FC + m if e is None else e * (2 * FC) + (JS * FC + 2 * m + h)

    def w1(w, m, kc):
        return w[:, m, kc * P:(kc + 1) * P]

    def w3(w, m, kc):
        return w[:, m, D + kc * P:D + (kc + 1) * P]

    def w2(w, m):
        return w[:, m, 2 * D:3 * D]

    block = ctx.enter_context(nc.Block())

    @block.sync
    def _(sp):
        sp.dma_start(ln_g[:], io["ffn_g"]).then_inc(small_loaded, 16)
        sp.dma_start(ln_b[:], io["ffn_b"]).then_inc(small_loaded, 16)
        sp.dma_start(w_r[:], io["w_r"]).then_inc(small_loaded, 16)
        for q in range(FC):
            if q >= 2:
                sp.wait_ge(w_ready, q - 1)
            sp.dma_start(w_stage[:, q % 2, :], io["we"][q]).then_inc(w_loaded[q % 2], 16)
        for g in range(NG):
            sp.wait_ge(ht_ready, g + 1)
            sp.dma_start(acc[g * G:(g + 1) * G, :].rearrange("(t p) d -> p t d", p=P), ht[:, g % 2, :, :]).then_inc(ht_sent[g % 2], 16)

        def load_weights(e, q0):
            for m in range(FC):
                sp.wait_ge(w_ready, q0 + (m - 1))
                sp.dma_start(w_stage[:, m % 2, :], io["we"][q0 + m]).then_inc(w_loaded[m % 2], 16)

        def load_rows(e):
            full = (ET - 1) * P
            sp.dma_start(xr[:, 0:ET - 1, :], rows_for[bass.ds(e * CAP, full), :].rearrange("(t p) c -> p t c", p=P)).then_inc(xr_loaded, 16)
            sp.dma_start(xr[0:LAST_ROWS, ET - 1, :], rows_for[bass.ds(e * CAP + full, LAST_ROWS), :]).then_inc(xr_loaded, 16)

        sp.wait_ge(xr_zeroed, 1)
        sp.wait_ge(dispatched, 16 * 2 * NT)
        load_rows(0)
        load_weights(0, FC)
        with sp.Fori(0, E - 1) as e:
            sp.wait_ge(tok_done, e + 1)
            sp.wait_ge(gate_ready, e + 1)
            sp.wait_ge(turned, e * 3 + 3)
            load_rows(e + 1)
            load_weights(e + 1, e * FC + 2 * FC)
        sp.wait_ge(y_sent, 16 * (JS + E * ET))

    @block.gpsimd
    def _(pool):
        pool.memset(ident[:], 0.0).then_inc(iota_done, 1)
        pool.memset(below[:], 1.0).then_inc(iota_done, 1)
        pool.memset(xr[:], 0.0).then_inc(xr_zeroed, 1)
        pool.memset(ones[:], 1.0)
        pool.wait_ge(iota_done, 2)
        pool.affine_select(out=ident[:], in_=ident[:], compare_op=ALU.not_equal, fill=1.0, base=0,
                           pattern=[[-1, P]], channel_multiplier=1)
        pool.affine_select(out=below[:], in_=below[:], compare_op=ALU.is_gt, fill=0.0, base=0,
                           pattern=[[1, P]], channel_multiplier=-1).then_inc(consts_ready, 1)
        pool.iota(iot[:, 0, :], pattern=[[-1, ES]], base=ES, channel_multiplier=0)
        pool.iota(iot[:, 1, :], pattern=[[CAP, ES]], base=0, channel_multiplier=0)
        pool.iota(iot[:, 2, :], pattern=[[1, ES]], base=0, channel_multiplier=0)
        pool.iota(rec[:].bitcast(I32)[:, :, D], pattern=[[P, NT]], base=0, channel_multiplier=1).then_inc(consts_ready, 1)

        def split_weights(q, m):
            count = held(pool, (q // 2) * 16 + 16)
            pool.wait_ge(iota_done, 2)
            pool.wait_ge(w_loaded[m % 2], count)
            pool.tensor_copy(w_hi[:, m, :], w_stage[:, m % 2, :]).then_inc(w_hi_done, 1)
            pool.wait_ge(w_hi_done, q + 1)
            pool.tensor_tensor(w_lo[:, m, :], w_stage[:, m % 2, :], w_hi[:, m, :].bitcast(F32), ALU.subtract).then_inc(w_ready, 1)

        for m in range(FC):
            split_weights(m, m)
        for k in range(2):
            pool.wait_ge(place_ready, 1)
            for t in range(NT):
                pool.indirect_dma_start(out=rows_for[:, :], in_=rec[:, t, :], in_offset=None,
                                        out_offset=bass.IndirectOffsetOnAxis(ap=place_u[:, k * NT + t:k * NT + t + 1], axis=0),
                                        bounds_check=E * CAP - 1, oob_is_err=False).then_inc(dispatched, 16)

        def body(j, b, e):
            if has_next(j, e):
                first = FC if e is None else e * FC + 2 * FC
                for m in range(FC):
                    pool.wait_ge(down_done, j * FC + (m + 1))
                    split_weights(first + m, m)
            if e is None:
                pool.wait_ge(y_read, j + 1)
                if is_first(j):
                    for i in range(2):
                        pool.wait_ge(ht_sent[i], 16 * NG // 2)
                pool.dma_start(acc[bass.ds(j * G, G), :].rearrange("(t p) d -> p t d", p=P), yo[:, 0:GT, :],
                               accum_op=ALU.add).then_inc(y_sent, 16)
            else:
                pool.wait_ge(y_read, j + 1)
                for t in range(ET):
                    count = held(pool, e * (16 * ET) + 16 * (JS + t))
                    pool.wait_ge(iota_done, 2)
                    pool.wait_ge(y_sent, count)
                    n = P if t < ET - 1 else LAST_ROWS
                    pool.indirect_dma_start(out=acc[:, :], in_=yo[0:n, t, :], in_offset=None,
                                            out_offset=bass.IndirectOffsetOnAxis(ap=tok[0:n, t:t + 1].bitcast(U32), axis=0),
                                            compute_op=ALU.add).then_inc(y_sent, 16)
        jobs(pool, body)

    @block.scalar
    def _(act):
        for g in range(NG):
            act.wait_ge(back_done, g + 1)
            tok_bank = ps[:, (g % 2) * 2:(g % 2) * 2 + 2, :]
            for n in range(2):
                k = 2 * g + n
                act.wait_ge(ve_done, k + 1)
                act.activation(std[:], var_eps[:], ACT.Sqrt).then_inc(std_done, 1)
                if n == 0:
                    if g >= 2:
                        act.wait_ge(ht_sent[g % 2], 16 * (g // 2))
                    act.activation(ht[:, g % 2, :, :].rearrange("p t d -> p (t d)"), tok_bank.rearrange("p a b -> p (a b)"), ACT.Copy).then_inc(ht_ready, 1)
                act.wait_ge(nmr_done, k + 1)
                for t in range(GT):
                    src = ps[:, (g % 2) * 2 + t // 2, (t % 2) * D:(t % 2 + 1) * D] if n == 0 else xn[g % 2][:, t, :]
                    dst = xn[g % 2][:, t, :] if n == 0 else rec[:, g * GT + t, 0:D]
                    ins = act.activation(dst, src, ACT.Identity, scale=rstd[:, t:t + 1], bias=nmr[:, t:t + 1])
                ins.then_inc((xn_ready, rec_ready)[n], 1)
            if g == 0:
                act.wait_ge(small_loaded, 48)
            act.wait_ge(fwd_done, g + 1)
            for c in range(DC):
                ins = act.activation(x32[:, c, g * G:(g + 1) * G], ps[:, 4 + c, :], ACT.Identity,
                                     scale=ln_g[:, c:c + 1], bias=ln_b[:, c:c + 1])
            ins.then_inc(feat_ready, 1)
        act.wait_ge(gap_ready, 1)
        act.activation(small[:, 1, :], small[:, 0, :], ACT.Exp).then_inc(gate_exp_done, 1)

        def read_turned(e, q):
            act.wait_ge(turned, e * 3 + (q + 1))
            n = 2 * P if q < 2 else CAP - 4 * P
            for c in range(DC):
                ins = act.activation(f32[:, c, q * 2 * P:q * 2 * P + n], ps[:, 7, c * 2 * P:c * 2 * P + n], ACT.Identity,
                                     scale=ln_g[:, c:c + 1], bias=ln_b[:, c:c + 1])
            ins.then_inc(f32_ready, 1)

        def body(j, b, e):
            for m in range(FC):
                k = j * FC + m
                if e is None:
                    act.wait_ge(up_done, part(j, e, m + 1))
                    if not (is_first(j) and m < 2):
                        act.wait_ge(prod_done, part(j, e, m - 1))
                    act.activation(s32[:, m % 2, :], ps[:, (m % 2) * 2, :], ACT.Silu).then_inc(silu_done, 1)
                else:
                    for h in range(2):
                        act.wait_ge(up_done, part(j, e, m, h + 1))
                        act.wait_ge(prod_done, part(j, e, m, h - 1))
                        act.activation(s32[:, h, 0:HALF], ps[:, 2 * h, 0:HALF], ACT.Silu).then_inc(silu_done, 1)
                act.wait_ge(prod_done, part(j, e, m + 1))
                if not (is_first(j) and m < 2):
                    act.wait_ge(down_done, k - 1)
                n = G if e is None else CAP
                act.activation(g_hi[:, m % 2, 0:n], g32[:, 0:n], ACT.Copy).then_inc(g_hi_ready, 1)
                if has_next(j, e) and 4 <= m < 7:
                    if m == 4 and not isinstance(j, int):
                        act.wait_ge(f_ready, j + 1)
                    read_turned(0 if e is None else e + 1, m - 4)
            act.wait_ge(down_done, j * FC + FC)
            if e is None:
                if not is_first(j):
                    act.wait_ge(y_sent, j * 16)
                act.activation(yo[:, 0:GT, :].rearrange("p t d -> p (t d)"), ps[:, 4:6, :].rearrange("p a b -> p (a b)"), ACT.Copy).then_inc(y_read, 1)
            else:
                act.wait_ge(gate_ready, e + 1)
                act.wait_ge(y_sent, 16 * JS + (16 * ET) * e)
                for t in range(ET):
                    n = P if t < ET - 1 else LAST_ROWS
                    ins = act.activation(yo[0:n, t, :], ps[0:n, 4 + t // 2, (t % 2) * D:(t % 2 + 1) * D], ACT.Copy, scale=gate[0:n, t:t + 1])
                ins.then_inc(y_read, 1)
        jobs(act, body)

    @block.tensor
    def _(pe):
        pe.wait_ge(consts_ready, 1)

        def back(g):
            if g >= 2:
                pe.wait_ge(xn_ready, g - 1)
                pe.wait_ge(ht_ready, g - 1)
            for t in range(GT):
                for c in range(DC):
                    tr = pe.transpose(ps[:, (g % 2) * 2 + t // 2, (t % 2) * D + c * P:(t % 2) * D + (c + 1) * P],
                                      x32[:, c, g * G + t * P:g * G + (t + 1) * P], ident[:])
            tr.then_inc(back_done, 1)

        back(0)
        for g in range(NG):
            if g + 1 < NG:
                back(g + 1)
            pe.wait_ge(rec_ready, g + 1)
            if g >= 1:
                pe.wait_ge(feat_ready, g)
            for c in range(DC):
                for t in range(GT):
                    tr = pe.transpose(ps[:, 4 + c, t * P:(t + 1) * P], rec[:, g * GT + t, c * P:(c + 1) * P], ident[:])
            tr.then_inc(fwd_done, 1)
            pe.wait_ge(feat_ready, g + 1)
            pe.wait_ge(small_loaded, 48)
            for t in range(GT):
                for c in range(DC):
                    at = (g * GT + t) * ES
                    mm = pe.matmul(ps[:, 6, at:at + E], x32[:, c, g * G + t * P:g * G + (t + 1) * P], w_r[:, c, :],
                                   start=(c == 0), stop=(c == DC - 1))
            mm.then_inc(logits_done, 1)

        def passes(out, lhs, rhs, start, stop, check=False):
            pe.matmul(out, lhs[0], rhs[0], start=start, stop=False, skip_group_check=check)
            pe.matmul(out, lhs[0], rhs[1], start=False, stop=False, skip_group_check=check)
            return pe.matmul(out, lhs[1], rhs[0], start=False, stop=stop, skip_group_check=check)

        def up(j, b, e, m):
            if m == 0:
                pe.wait_ge(f_ready, j + 1)
            if e is None:
                if is_first(j):
                    pe.wait_ge(w_ready, m + 1)
                if not (is_first(j) and m < 2):
                    pe.wait_ge(prod_done, part(j, e, m - 1))
                elif m == 0:
                    pe.wait_ge(xn_ready, NG)
                    pe.wait_ge(ht_ready, NG)
                halves = [((m % 2) * 2, 0, G)]
            else:
                pe.wait_ge(w_ready, e * FC + (FC + m + 1))
                halves = [(2 * h, h * HALF, HALF) for h in range(2)]
            for h, (bank, at, n) in enumerate(halves):
                if e is not None:
                    pe.wait_ge(prod_done, part(j, e, m, h - 1))
                par = b if b is not None else e % 2
                for which_w, w in enumerate((w1, w3)):
                    for kc in range(DC):
                        rhs = [f[:, par, kc, at:at + n] for f in (f_hi, f_lo)]
                        mm = passes(ps[:, bank + which_w, 0:n], (w(w_hi, m, kc), w(w_lo, m, kc)), rhs, kc == 0, kc == DC - 1)
                mm.then_inc(up_done, 1)

        def down(j, e, m):
            k = j * FC + m
            pe.wait_ge(g_hi_ready, k + 1)
            pe.wait_ge(g_lo_ready, k + 1)
            if m == 0:
                if is_first(j):
                    pe.wait_ge(feat_ready, NG)
                else:
                    pe.wait_ge(y_read, j)
            for t in range(GT if e is None else ET):
                n = P if t < ET - 1 else LAST_ROWS
                g = [x[:, m % 2, t * P:t * P + n] for x in (g_hi, g_lo)]
                mm = passes(ps[0:n, 4 + t // 2, (t % 2) * D:(t % 2 + 1) * D], g, (w2(w_hi, m), w2(w_lo, m)),
                            m == 0 and t % 2 == 0, m == FC - 1, True)
            mm.then_inc(down_done, 1)

        def turn(e, q):
            if q == 0:
                pe.wait_ge(xr_loaded, e * 32 + 32)
                if isinstance(e, int) and e == 0:
                    pe.wait_ge(place_ready, 1)
                else:
                    pe.wait_ge(f32_ready, e * 3)
            else:
                pe.wait_ge(f32_ready, e * 3 + q)
            for c in range(DC):
                for t in (2 * q, 2 * q + 1):
                    n = P if t < ET - 1 else LAST_ROWS
                    tr = pe.transpose(ps[:, 7, c * 2 * P + (t % 2) * P:c * 2 * P + (t % 2) * P + n], xr[0:n, t, c * P:(c + 1) * P], ident[0:n, 0:n])
            tr.then_inc(turned, 1)

        def body(j, b, e):
            for m in range(FC):
                up(j, b, e, m)
                if m >= 1:
                    down(j, e, m - 1)
                if has_next(j, e) and 4 <= m < 7:
                    turn(0 if e is None else e + 1, m - 4)
            down(j, e, FC - 1)
            if is_first(j):
                pe.wait_ge(hot_ready, 1)
                for x in range(ES):
                    mm = pe.matmul(ps[0:2 * NT, 7, x:x + 1], hot[:].rearrange("p k t x -> p (k t) x")[:, :, x], ones[:, 0:1], start=True, stop=True)
                mm.then_inc(tot_done, 1)
                pe.wait_ge(before_ready, 1)
                pe.matmul(ps[:, 7, :], below[:], hot[:].rearrange("p k t x -> p (k t x)"), start=True, stop=False)
                pe.matmul(ps[:, 7, :], ones[0:2 * NT, :], before[:].rearrange("p k x -> p (k x)"), start=False, stop=True).then_inc(pos_done, 1)
        jobs(pe, body)

    @block.vector
    def _(dve):
        dve.wait_ge(consts_ready, 2)
        dve.tensor_copy(cst[:], iot[:]).then_inc(cst_done, 1)
        for g in range(NG):
            dve.wait_ge(back_done, g + 1)
            for n in range(2):
                k = 2 * g + n
                if n == 1:
                    dve.wait_ge(xn_ready, g + 1)
                for t in range(GT):
                    src = ps[:, (g % 2) * 2 + t // 2, (t % 2) * D:(t % 2 + 1) * D] if n == 0 else xn[g % 2][:, t, :]
                    ins = dve.bn_stats(stats[:, t, :], src)
                ins.then_inc(norm_steps, 1)
                dve.wait_ge(norm_steps, 3 * k + 1)
                for t in range(GT):
                    ins = dve.bn_aggr(mv[:, t, :], stats[:, t, :])
                ins.then_inc(norm_steps, 1)
                dve.wait_ge(norm_steps, 3 * k + 2)
                dve.tensor_scalar(var_eps[:], mv[:, :, 1], EPS, None, ALU.add).then_inc(ve_done, 1)
                dve.wait_ge(std_done, k + 1)
                if k >= 1:
                    dve.wait_ge((xn_ready, rec_ready)[(k - 1) % 2], (k - 1) // 2 + 1)
                dve.reciprocal(rstd[:], std[:]).then_inc(norm_steps, 1)
                dve.wait_ge(norm_steps, 3 * k + 3)
                dve.scalar_tensor_tensor(out=nmr[:], in0=mv[:, :, 0], scalar=-1.0, in1=rstd[:],
                                         op0=ALU.mult, op1=ALU.mult).then_inc(nmr_done, 1)

        def split_block(g, b):
            xs = x32[:, :, bass.ds(g * G, G)]
            if isinstance(g, int):
                dve.wait_ge(feat_ready, g + 1)
            dve.tensor_copy(f_hi[:, b, :, 0:G], xs).then_inc(f_hi_done, 1)
            dve.wait_ge(f_hi_done, g + 1)
            dve.tensor_tensor(f_lo[:, b, :, 0:G], xs, f_hi[:, b, :, 0:G].bitcast(F32), ALU.subtract).then_inc(f_ready, 1)

        def split_expert(e):
            par = e % 2
            dve.wait_ge(f32_ready, e * 3 + 3)
            hi, lo = (f[:, bass.ds(par, 1), :, 0:CAP].rearrange("p a c n -> p (a c) n") for f in (f_hi, f_lo))
            dve.tensor_copy(hi, f32[:, :, 0:CAP]).then_inc(f_hi_done, 1)
            dve.wait_ge(f_hi_done, e + (JS + 1))
            dve.tensor_tensor(lo, f32[:, :, 0:CAP], hi.bitcast(F32), ALU.subtract).then_inc(f_ready, 1)

        steps = [0]

        def step(ins):
            steps[0] += 1
            ins.then_inc(route, 1)
            dve.wait_ge(route, steps[0])

        def by_expert(x):
            return cst[:, x, :].unsqueeze(1).to_broadcast([P, NT, ES])

        def wide(x):
            return x.unsqueeze(2).to_broadcast([P, NT, ES])

        def choices():
            dve.memset(lg[:, :, E:ES], NEG)
            step(dve.tensor_copy(lg[:, :, 0:E], ps[:, 6, 0:NT * ES].rearrange("p (t x) -> p t x", x=ES)[:, :, 0:E]))
            for k in range(2):
                step(dve.tensor_reduce(top[:, k, :], lg[:], AX.X, ALU.max))
                step(dve.tensor_tensor(eq[:], lg[:], wide(top[:, k, :]), ALU.is_equal))
                step(dve.tensor_tensor(eq[:], eq[:], by_expert(0), ALU.mult))
                step(dve.tensor_reduce(which[:, k, :], eq[:], AX.X, ALU.max))
                step(dve.tensor_tensor(hot[:, k], by_expert(0), wide(which[:, k, :]), ALU.is_equal))
                if k == 0:
                    step(dve.scalar_tensor_tensor(out=lg[:], in0=hot[:, 0], scalar=NEG, in1=lg[:], op0=ALU.mult, op1=ALU.add))
            dve.tensor_tensor(small[:, 0, :], top[:, 1, :], top[:, 0, :], ALU.subtract).then_inc(gap_ready, 1)
            step(dve.tensor_scalar(rec[:, :, D + 2], which[:, 0, :], -1.0, float(ES), ALU.mult, ALU.add))
            dve.memset(tot[:], 0.0).then_inc(hot_ready, 1)
            dve.wait_ge(gate_exp_done, 1)
            step(dve.tensor_scalar(small[:, 2, :], small[:, 1, :], 1.0, None, ALU.add))
            step(dve.reciprocal(small[:, 3, :], small[:, 2, :]))
            dve.tensor_copy(rec[:, :, D + 1], small[:, 3, :])
            step(dve.tensor_tensor(rec[:, :, D + 3], small[:, 1, :], small[:, 3, :], ALU.mult))

        def places():
            dve.wait_ge(tot_done, 1)
            step(dve.tensor_copy(tot[0:2 * NT, :], ps[0:2 * NT, 7, 0:ES]))
            n = 2 * NT
            dve.tensor_tensor(before[:], tot[0:n, :].unsqueeze(1).to_broadcast([n, n, ES]),
                              below[0:n, 0:n].unsqueeze(2).to_broadcast([n, n, ES]), ALU.mult).then_inc(before_ready, 1)
            dve.wait_ge(pos_done, 1)
            hots = hot[:].rearrange("p k t x -> p (k t) x")
            caps = cst[:, 1, :].unsqueeze(1).to_broadcast([P, n, ES])
            step(dve.tensor_tensor(at_pos[:], ps[:, 7, :].rearrange("p (k x) -> p k x", x=ES), hots, ALU.mult))
            step(dve.tensor_reduce(place[:, 0, :], at_pos[:], AX.X, ALU.add))
            step(dve.tensor_tensor(at_pos[:], hots, caps, ALU.mult))
            dve.tensor_scalar(place[:, 2, :], place[:, 0, :], float(CAP), SKIP, ALU.is_ge, ALU.mult)
            step(dve.tensor_reduce(place[:, 1, :], at_pos[:], AX.X, ALU.add))
            step(dve.tensor_tensor(place[:, 3, :], place[:, 0, :], place[:, 1, :], ALU.add))
            step(dve.tensor_tensor(place[:, 3, :], place[:, 3, :], place[:, 2, :], ALU.add))
            dve.tensor_copy(place_u[:], place[:, 3, :]).then_inc(place_ready, 1)

        split_block(0, 0)
        dve.wait_ge(logits_done, NG)
        dve.wait_ge(cst_done, 1)
        choices()

        def gates(e):
            dve.wait_ge(xr_loaded, e * 32 + 32)
            dve.wait_ge(y_sent, 16 * JS + (16 * ET) * e)
            dve.tensor_copy(tok[:], xr[:].bitcast(I32)[:, :, D]).then_inc(tok_done, 1)
            first, eid, second = (xr[:, :, D + 1 + n] for n in range(3))
            dve.tensor_scalar(gtmp[:, 0, :], eid, cst[:, 2, bass.ds(e, 1)], None, ALU.is_equal)
            dve.tensor_tensor(gtmp[:, 1, :], first, second, ALU.subtract).then_inc(gate_steps, 1)
            dve.wait_ge(gate_steps, e * 2 + 1)
            dve.tensor_tensor(gtmp[:, 0, :], gtmp[:, 0, :], gtmp[:, 1, :], ALU.mult).then_inc(gate_steps, 1)
            dve.wait_ge(gate_steps, e * 2 + 2)
            dve.tensor_tensor(gate[:], gtmp[:, 0, :], second, ALU.add).then_inc(gate_ready, 1)

        def body(j, b, e):
            for m in range(FC):
                k = j * FC + m
                if not (is_first(j) and m == 0):
                    dve.wait_ge(g_hi_ready, k)
                    dve.wait_ge(g_lo_ready, k)
                if e is None:
                    dve.wait_ge(silu_done, part(j, e, m + 1))
                    dve.tensor_tensor(g32[:, 0:G], s32[:, m % 2, :], ps[:, (m % 2) * 2 + 1, :], ALU.mult).then_inc(prod_done, 1)
                    n = G
                else:
                    for h in range(2):
                        dve.wait_ge(silu_done, part(j, e, m, h + 1))
                        dve.tensor_tensor(g32[:, h * HALF:(h + 1) * HALF], s32[:, h, 0:HALF], ps[:, 2 * h + 1, 0:HALF], ALU.mult).then_inc(prod_done, 1)
                    n = CAP
                dve.wait_ge(g_hi_ready, k + 1)
                dve.tensor_tensor(g_lo[:, m % 2, 0:n], g32[:, 0:n], g_hi[:, m % 2, 0:n].bitcast(F32), ALU.subtract).then_inc(g_lo_ready, 1)
                if m == 1:
                    if e is not None:
                        gates(e)
                    elif not is_last_shared(j):
                        split_block(j + 1, 1 - b)
            if is_first(j):
                places()
            if has_next(j, e):
                split_expert(0 if e is None else e + 1)
        jobs(dve, body)


def program(nc, io, acc):
    rows_for = nc.dram_tensor("rows_for", (E * CAP, REC), F32, kind="Internal").ap()
    with ExitStack() as ctx:
        x32 = ctx.enter_context(nc.sbuf_tensor("x32", [P, DC, N_TOK], F32))
        with ExitStack() as stage:
            tower(nc, stage, io, x32, rows_for, acc)
        with ExitStack() as stage:
            attention(nc, stage, io, x32)
        with ExitStack() as stage:
            experts(nc, stage, io, x32, rows_for, acc)


def expert_weights(a):
    import numpy as np

    def up(w):
        return w.reshape(DC, P, FC, P).transpose(2, 1, 0, 3).reshape(FC, P, D)

    parts = []
    for e in range(-1, E):
        w1, w3, w2 = (a("L0_ffn_" + n + "s") if e < 0 else a("L0_ffn_" + n)[e] for n in ("W1", "W3", "W2"))
        parts.append(np.concatenate([up(w1), up(w3), w2.reshape(FC, P, D)], 2))
    return np.concatenate(parts)


def attention_weights(a, rows):
    import numpy as np

    wq, wkv, wo = a("L0_attn_w_q"), a("L0_attn_w_kv"), a("L0_attn_w_out")
    h = HEADS * DH
    parts = []
    for p in range(PAIRS):
        at = p * P
        parts.append(np.stack([rows(wq[:, at:at + P], DC), rows(wkv[:, at:at + P], DC),
                               rows(wkv[:, h + at:h + at + P], DC), wo[at:at + P]], 1))
    return np.stack(parts)


def layout(i):
    import numpy as np

    def a(name):
        return np.asarray(i[name])

    def rows(w, chunks):
        return w.reshape(chunks, P, -1).transpose(1, 0, 2).reshape(P, -1)

    def cols(v):
        return np.moveaxis(v.reshape(v.shape[:-1] + (-1, P)), -1, 0)

    wqo, wf = [], []
    for l in range(LAYERS):
        wqo.append(np.stack([rows(a("L0_tok_Wq")[l].reshape(D, D), DC), rows(a("L0_tok_Wo")[l].T, DC)], 1))
        w1 = rows(a("L0_tok_ff_w1")[l].T, DC).reshape(P, NG, G // 2)
        w2 = rows(a("L0_tok_ff_w2")[l].T, FC).reshape(P, NG, G // 2)
        wf.append(np.concatenate([w1, w2], 2).transpose(1, 0, 2))
    return {
        "ids": np.ascontiguousarray(a("x").reshape(-1, P).T),
        "emb": a("L0_tok_emb_table"),
        "wqo": np.ascontiguousarray(np.stack(wqo)),
        "wf": np.ascontiguousarray(np.concatenate(wf)),
        "vec": np.ascontiguousarray(np.concatenate([cols(a("L0_tok_" + n)) for n in ("ln1_w", "ln1_b", "ln2_w", "ln2_b", "ff_b2")], 2)),
        "wa": np.ascontiguousarray(attention_weights(a, rows)),
        "b_out": np.ascontiguousarray(cols(a("L0_attn_b_out"))),
        "sort_w": np.ascontiguousarray(a("L0_attn_sort_w")[0].reshape(SORT_PAIRS, 2, 2, DH, NB)
                                       .transpose(0, 1, 3, 2, 4).reshape(SORT_PAIRS, P, 2, NB)),
        "ffn_g": np.ascontiguousarray(cols(a("L0_ffn_ln_g"))),
        "ffn_b": np.ascontiguousarray(cols(a("L0_ffn_ln_b"))),
        "w_r": np.ascontiguousarray(a("L0_ffn_Wr").reshape(DC, P, E).transpose(1, 0, 2)),
        "we": np.ascontiguousarray(expert_weights(a)),
        "b1": np.ascontiguousarray(cols(a("L0_tok_ff_b1"))),
    }


def kernel(**inputs):
    import numpy as np
    import concourse.bacc as bacc
    from concourse.bass_utils import run_bass_kernel_spmd

    arrays = {"in_" + name: v for name, v in layout(inputs).items()}
    nc = bacc.Bacc("TRN2", target_bir_lowering=False, num_devices=1)
    io = {name[3:]: nc.dram_tensor(name, v.shape, mybir.dt.from_np(v.dtype), kind="ExternalInput").ap()
          for name, v in arrays.items()}
    acc = nc.dram_tensor("out", (N_TOK + P, D), F32, kind="ExternalOutput").ap()
    program(nc, io, acc)
    got = run_bass_kernel_spmd(nc, [arrays], core_ids=[0]).results[0]["out"]
    return got[:N_TOK].reshape(2, N_TOK // 2, D)
```

```python
from contextlib import ExitStack

import concourse.bass as bass
from concourse import mybir

F32 = mybir.dt.float32
F32R = mybir.dt.float32r
I32 = mybir.dt.int32
U32 = mybir.dt.uint32
ALU = mybir.AluOpType
ACT = mybir.ActivationFunctionType
AX = mybir.AxisListType

P = 128
D = 256
DC = D // P
N_TOK = 4096
G = 512
NG = N_TOK // G
GT = G // P
F = 1024
FC = F // P
LAYERS = 6
VOCAB = 8000
EPS = 1e-5


def held(eng, value):
    if not isinstance(value, int):
        value = eng.snap(value)
        eng.compute_val(value)
    return value


def tower(nc, ctx, io, x32, rows_for, acc):
    def sb(name, shape, dt=F32):
        return ctx.enter_context(nc.sbuf_tensor(name, shape, dt))

    def sem(name):
        return ctx.enter_context(nc.semaphore(name))

    w_hi = [sb(f"t_w_hi{i}", [P, NG, G], F32R) for i in range(2)]
    w_lo = [sb(f"t_w_lo{i}", [P, NG, G], F32R) for i in range(2)]
    w_stage = sb("t_w_stage", [P, 2, G])
    mix = sb("t_mix", [P, LAYERS, DC * D])
    mix_hi = sb("t_mix_hi", [P, DC, D], F32R)
    mix_lo = sb("t_mix_lo", [P, DC, D], F32R)
    x_hi = sb("t_x_hi", [P, DC, G], F32R)
    x_lo = sb("t_x_lo", [P, DC, G], F32R)
    a32 = sb("t_a32", [P, 2, DC, G])
    a_hi = sb("t_a_hi", [P, 2, DC, G], F32R)
    a_lo = sb("t_a_lo", [P, 2, DC, G], F32R)
    h32 = sb("t_h32", [P, 2, G])
    h_hi = sb("t_h_hi", [P, FC, G], F32R)
    h_lo = sb("t_h_lo", [P, FC, G], F32R)
    u2 = sb("t_u2", [P, DC, G])
    xn = [sb(f"t_xn{i}", [P, GT, D]) for i in (1, 2)]
    vec = sb("t_vec", [P, LAYERS, 14])
    b1 = sb("t_b1", [P, LAYERS, FC])
    ids = sb("t_ids", [P, N_TOK // P], I32)
    idf = sb("t_idf", [P, 3, N_TOK // P])
    idu = sb("t_idu", [P, N_TOK // P], U32)
    eye = sb("t_eye", [P, DC, D])
    stats = [sb(f"t_stats{i}", [P, GT, 6]) for i in (1, 2)]
    mv = [sb(f"t_mv{i}", [P, GT, 2]) for i in (1, 2)]
    var_eps = [sb(f"t_ve{i}", [P, GT]) for i in (1, 2)]
    std = [sb(f"t_std{i}", [P, GT]) for i in (1, 2)]
    rstd = [sb(f"t_rstd{i}", [P, GT]) for i in (1, 2)]
    nmr = [sb(f"t_nmr{i}", [P, GT]) for i in (1, 2)]
    fill = sb("t_fill", [P, REC])

    ps_tok = ctx.enter_context(nc.psum_tensor("t_ps_tok", [P, GT, D], F32))
    ps_feat = ctx.enter_context(nc.psum_tensor("t_ps_feat", [P, DC, G], F32))
    ps_h = ctx.enter_context(nc.psum_tensor("t_ps_h", [P, 2, G], F32))
    ps_y = ctx.enter_context(nc.psum_tensor("t_ps_y", [P, DC, G], F32))

    vec_loaded = sem("t_vec_loaded")
    ids_loaded = sem("t_ids_loaded")
    qo_loaded = [sem(f"t_qo_loaded{i}") for i in range(2)]
    stage_loaded = [sem(f"t_stage_loaded{i}") for i in range(2)]
    ids_ready = sem("t_ids_ready")
    ids_steps = sem("t_ids_steps")
    x_hi_done = sem("t_x_hi_done")
    rows_loaded = [sem(f"t_rows_loaded{i}") for i in range(2)]
    eye_ready = sem("t_eye_ready")
    rows_turned = sem("t_rows_turned")
    x_ready = sem("t_x_ready")
    mix_done = sem("t_mix_done")
    mix_ready = sem("t_mix_ready")
    w_split = sem("t_w_split")
    x_split = sem("t_x_split")
    z_done = sem("t_z_done")
    ff1_done = sem("t_ff1_done")
    ff2_done = sem("t_ff2_done")
    fwd_done = [sem(f"t_fwd_done{i}") for i in (1, 2)]
    back_done = sem("t_back_done")
    u2_ready = sem("t_u2_ready")
    stats_done = [sem(f"t_stats_done{i}") for i in (1, 2)]
    mv_done = [sem(f"t_mv_done{i}") for i in (1, 2)]
    ve_done = [sem(f"t_ve_done{i}") for i in (1, 2)]
    std_done = [sem(f"t_std_done{i}") for i in (1, 2)]
    rstd_done = [sem(f"t_rstd_done{i}") for i in (1, 2)]
    nmr_done = [sem(f"t_nmr_done{i}") for i in (1, 2)]
    xn_ready = [sem(f"t_xn_ready{i}") for i in (1, 2)]
    a32_ready = sem("t_a32_ready")
    a_hi_done = sem("t_a_hi_done")
    a_split = sem("t_a_split")
    h_hi_ready = sem("t_h_hi_ready")
    h_lo_ready = sem("t_h_lo_ready")
    hi_written = sem("t_hi_written")
    fill_ready = sem("t_fill_ready")
    filled = sem("t_filled")

    SLOTS = LAYERS * NG
    LN1_W, LN1_B, LN2_W, LN2_B, FF_B2 = (DC * i for i in range(5))

    def slots(eng, body):
        for b in range(2):
            body(b, 0, b, 0)
        with eng.Fori(1, NG // 2) as j:
            for b in range(2):
                body(j * 2 + b, 0, b, 0)
        with eng.Fori(0, NG // 2) as j:
            for b in range(2):
                body(j * 2 + (NG + b), 1, b, 1)
        with eng.Fori(1, LAYERS // 2) as pair:
            for par in range(2):
                with eng.Fori(0, NG // 2) as j:
                    for b in range(2):
                        body(pair * (2 * NG) + j * 2 + (par * NG + b), pair * 2 + par, b, par)

    def w1(w, par, kc, m):
        at = kc * F + m * P
        return w[par][:, at // (G // 2), at % (G // 2):at % (G // 2) + P]

    def w2(w, par, k, oc):
        return w[par][:, k, G // 2 + oc * P:G // 2 + (oc + 1) * P]

    block = ctx.enter_context(nc.Block())

    @block.sync
    def _(sp):
        sp.dma_start(ids[:], io["ids"]).then_inc(ids_loaded, 16)
        sp.dma_start(vec[:, :, 0:10], io["vec"]).then_inc(vec_loaded, 16)
        sp.dma_start(b1[:], io["b1"]).then_inc(vec_loaded, 16)
        for l in range(LAYERS):
            if l >= 2:
                sp.wait_ge(mix_done, l - 1)
            sp.dma_start(a32[:, l % 2, :, :], io["wqo"][l]).then_inc(qo_loaded[l % 2], 16)
        for g in range(NG):
            if g >= 2:
                sp.wait_ge(w_split, g - 1)
            sp.dma_start(w_stage[:, g % 2, :], io["wf"][g]).then_inc(stage_loaded[g % 2], 16)
        with sp.Fori(0, SLOTS // 2) as i:
            for b in range(2):
                sp.wait_ge(w_split, i * 2 + (NG + b - 1))
                sp.dma_start(w_stage[:, b, :], io["wf"][(i * 2 + (NG + b)) % SLOTS]).then_inc(stage_loaded[b], 16)

    @block.gpsimd
    def _(pool):
        pool.memset(eye[:], 0.0).then_inc(eye_ready, 1)
        pool.wait_ge(eye_ready, 1)
        pool.affine_select(out=eye[:], in_=eye[:], compare_op=ALU.not_equal, fill=1.0, base=0,
                           pattern=[[-P, DC], [1, D]], channel_multiplier=-1).then_inc(eye_ready, 1)
        pool.memset(fill[:], 0.0).then_inc(fill_ready, 1)
        pool.wait_ge(fill_ready, 1)
        pool.iota(fill[:].bitcast(I32)[:, D:D + 1], pattern=[[0, 1]], base=N_TOK, channel_multiplier=1).then_inc(fill_ready, 1)
        pool.wait_ge(ids_ready, 1)
        for g in range(NG):
            if g >= 2:
                pool.wait_ge(rows_turned, g - 1)
            for t in range(GT):
                pool.indirect_dma_start(out=xn[g % 2][:, t, :], out_offset=None, in_=io["emb"],
                                        in_offset=bass.IndirectOffsetOnAxis(ap=idu[:, g * GT + t:g * GT + t + 1], axis=0),
                                        ).then_inc(rows_loaded[g % 2], 16)

    @block.scalar
    def _(act):
        act.wait_ge(vec_loaded, 32)
        for g in range(NG):
            act.wait_ge(rows_turned, g + 1)
            act.activation(x32[:, :, g * G:(g + 1) * G], ps_feat[:], ACT.Copy).then_inc(x_ready, 1)

        def root(n, k):
            act.wait_ge(ve_done[n], k + 1)
            act.activation(std[n][:], var_eps[n][:], ACT.Sqrt).then_inc(std_done[n], 1)

        def normalise(n, k, first, last):
            if first == 0:
                act.wait_ge(nmr_done[n], k + 1)
                if not (isinstance(k, int) and k == 0):
                    act.wait_ge(fwd_done[n], k)
                elif n == 0:
                    act.wait_ge(rows_turned, NG)
            for t in range(first, last):
                ins = act.activation(xn[n][:, t, :], ps_tok[:, t, :], ACT.Identity,
                                     scale=rstd[n][:, t:t + 1], bias=nmr[n][:, t:t + 1])
            if last == GT:
                ins.then_inc(xn_ready[n], 1)

        def scale_first(k, l, b):
            act.wait_ge(fwd_done[0], k + 1)
            if not (isinstance(k, int) and k < 2):
                act.wait_ge(u2_ready, k - 1)
            for c in range(DC):
                ins = act.activation(a32[:, b, c, :], ps_feat[:, c, :], ACT.Identity,
                                     scale=vec[:, l, LN1_W + c:LN1_W + c + 1],
                                     bias=vec[:, l, LN1_B + c:LN1_B + c + 1])
            ins.then_inc(a32_ready, 1)

        def scale_second(k, l):
            count = held(act, k + 1)
            act.wait_ge(vec_loaded, 32)
            act.wait_ge(fwd_done[1], count)
            g = k % NG
            for c in range(DC):
                ins = act.activation(x32[:, c, bass.ds(g * G, G)], ps_feat[:, c, :], ACT.Identity,
                                     scale=vec[:, l, LN2_W + c:LN2_W + c + 1],
                                     bias=vec[:, l, LN2_B + c:LN2_B + c + 1])
            ins.then_inc(x_ready, 1)

        def hidden(s, l, m):
            before = m >= 2 or not (isinstance(s, int) and s == 0)
            count = held(act, s * FC + (m + 1))
            free = held(act, s * FC + (m - 1)) if before else 0
            act.wait_ge(vec_loaded, 32)
            act.wait_ge(ff1_done, count)
            if before:
                act.wait_ge(h_lo_ready, free)
            act.activation(h32[:, m % 2, :], ps_h[:, m % 2, :], ACT.Relu, bias=b1[:, l, m:m + 1])
            act.activation(h_hi[:, m, :], ps_h[:, m % 2, :], ACT.Relu, bias=b1[:, l, m:m + 1]).then_inc(h_hi_ready, 1)

        root(0, 0)
        normalise(0, 0, 0, GT)
        act.wait_ge(mix_ready, LAYERS)
        scale_first(0, 0, 0)
        act.wait_ge(fill_ready, 2)
        act.dma_start(acc[N_TOK:, :], fill[:, 0:D]).then_inc(filled, 16)
        by_row = rows_for.rearrange("(e r) c -> r e c", e=E)
        for t in range(ET):
            n = P if t < ET - 1 else LAST_ROWS
            act.dma_start(by_row[t * P:t * P + n], fill[0:n, :].unsqueeze(1).to_broadcast([n, E, REC])).then_inc(filled, 16)

        def body(s, l, b, par):
            two = not (isinstance(s, int) and s == 0)
            l_next, l_prev = ((s + 1) // NG) % LAYERS, (s - 1) // NG
            hidden(s, l, 0)
            hidden(s, l, 1)
            root(0, s + 1)
            hidden(s, l, 2)
            normalise(0, s + 1, 0, GT)
            hidden(s, l, 3)
            scale_first(s + 1, l_next, 1 - b)
            hidden(s, l, 4)
            hidden(s, l, 5)
            hidden(s, l, 6)
            if two:
                root(1, s - 1)
                normalise(1, s - 1, 0, GT)
            hidden(s, l, 7)
            if two:
                scale_second(s - 1, l_prev)
        slots(act, body)
        root(1, SLOTS - 1)
        normalise(1, SLOTS - 1, 0, GT)
        scale_second(SLOTS - 1, LAYERS - 1)
        act.wait_ge(filled, 16 * (1 + ET))

    @block.tensor
    def _(pe):
        pe.wait_ge(eye_ready, 2)
        ident_ap = eye[:, 0, 0:P]
        for l in range(LAYERS):
            pe.wait_ge(qo_loaded[l % 2], 16 * (l // 2 + 1))
            if l >= 2:
                pe.wait_ge(mix_ready, l - 1)
            for kc in range(DC):
                for hc in range(DC):
                    mm = pe.matmul(ps_h[:, l % 2, kc * D:(kc + 1) * D], a32[:, l % 2, 0, hc * D + kc * P:hc * D + (kc + 1) * P],
                                   a32[:, l % 2, 1, hc * D:(hc + 1) * D], start=(hc == 0), stop=(hc == DC - 1))
            mm.then_inc(mix_done, 1)
        for g in range(NG):
            pe.wait_ge(rows_loaded[g % 2], 16 * GT * (g // 2 + 1))
            if g >= 1:
                pe.wait_ge(x_ready, g)
            for t in range(GT):
                for c in range(DC):
                    tr = pe.transpose(ps_feat[:, c, t * P:(t + 1) * P], xn[g % 2][:, t, c * P:(c + 1) * P], ident_ap)
            tr.then_inc(rows_turned, 1)

        def passes(out, lhs, rhs, start, stop):
            pe.matmul(out, lhs[0], rhs[0], start=start, stop=False)
            pe.matmul(out, lhs[0], rhs[1], start=False, stop=False)
            return pe.matmul(out, lhs[1], rhs[0], start=False, stop=stop)

        def mixing(k):
            pe.wait_ge(x_split, k + 1)
            if isinstance(k, int) and k < 3:
                if k >= 1:
                    pe.wait_ge(xn_ready[0], k)
            else:
                pe.wait_ge(xn_ready[1], k - 2)
            for t in range(GT):
                for kc in range(DC):
                    tok = slice(t * P, (t + 1) * P)
                    mm = passes(ps_tok[:, t, :], (x_hi[:, kc, tok], x_lo[:, kc, tok]),
                                (mix_hi[:, kc, :], mix_lo[:, kc, :]), kc == 0, kc == DC - 1)
            mm.then_inc(z_done, 1)

        def forward(n, k):
            pe.wait_ge(xn_ready[n], k + 1)
            for c in range(DC):
                for t in range(GT):
                    tr = pe.transpose(ps_feat[:, c, t * P:(t + 1) * P], xn[n][:, t, c * P:(c + 1) * P], ident_ap)
            tr.then_inc(fwd_done[n], 1)

        def back(k):
            pe.wait_ge(u2_ready, k + 1)
            pe.wait_ge(xn_ready[0], k + 3)
            for t in range(GT):
                for c in range(DC):
                    tr = pe.transpose(ps_tok[:, t, c * P:(c + 1) * P], u2[:, c, t * P:(t + 1) * P], ident_ap)
            tr.then_inc(back_done, 1)

        def up(s, b, par, m):
            if m == 0:
                pe.wait_ge(a_split, s + 1)
            if not (isinstance(s, int) and s == 0 and m < 2):
                pe.wait_ge(h_hi_ready, s * FC + (m - 1))
            for kc in range(DC):
                mm = passes(ps_h[:, m % 2, :], (w1(w_hi, par, kc, m), w1(w_lo, par, kc, m)),
                            (a_hi[:, b, kc, :], a_lo[:, b, kc, :]), kc == 0, kc == DC - 1)
            mm.then_inc(ff1_done, 1)

        def down(s, par, k):
            if k == 0 and not (isinstance(s, int) and s == 0):
                pe.wait_ge(u2_ready, s)
            pe.wait_ge(h_hi_ready, s * FC + (k + 1))
            pe.wait_ge(h_lo_ready, s * FC + (k + 1))
            for oc in range(DC):
                mm = passes(ps_y[:, oc, :], (w2(w_hi, par, k, oc), w2(w_lo, par, k, oc)),
                            (h_hi[:, k, :], h_lo[:, k, :]), k == 0, k == FC - 1)
            if k == FC - 1:
                mm.then_inc(ff2_done, 1)

        pe.wait_ge(mix_ready, LAYERS)
        mixing(0)
        pe.wait_ge(x_ready, NG)
        forward(0, 0)

        def body(s, l, b, par):
            two = not (isinstance(s, int) and s == 0)
            mixing(s + 1)
            pe.wait_ge(w_split, l * NG + NG)
            up(s, b, par, 0)
            up(s, b, par, 1)
            for m in range(2, FC):
                up(s, b, par, m)
                down(s, par, m - 2)
                if m == 3:
                    if isinstance(s, int) and s < 2:
                        pe.wait_ge(a32_ready, s + 1)
                    else:
                        pe.wait_ge(x_ready, s + (NG - 1))
                    forward(0, s + 1)
                if m == 5 and two:
                    back(s - 1)
            down(s, par, FC - 2)
            if two:
                pe.wait_ge(a32_ready, s + 2)
                forward(1, s - 1)
            down(s, par, FC - 1)
        slots(pe, body)
        pe.wait_ge(u2_ready, SLOTS)
        pe.wait_ge(xn_ready[0], SLOTS + 1)
        back_last = SLOTS - 1
        for t in range(GT):
            for c in range(DC):
                tr = pe.transpose(ps_tok[:, t, c * P:(c + 1) * P], u2[:, c, t * P:(t + 1) * P], ident_ap)
        tr.then_inc(back_done, 1)
        pe.wait_ge(x_ready, NG + SLOTS - 1)
        forward(1, back_last)

    @block.vector
    def _(dve):
        dve.wait_ge(ids_loaded, 16)
        dve.tensor_copy(idf[:, 0, :], ids[:]).then_inc(ids_steps, 1)
        dve.wait_ge(ids_steps, 1)
        dve.tensor_scalar(idf[:, 1, :], idf[:, 0, :], 0.0, float(VOCAB), ALU.is_lt, ALU.mult).then_inc(ids_steps, 1)
        dve.wait_ge(ids_steps, 2)
        dve.tensor_tensor(idf[:, 2, :], idf[:, 0, :], idf[:, 1, :], ALU.add).then_inc(ids_steps, 1)
        dve.wait_ge(ids_steps, 3)
        dve.tensor_scalar(idf[:, 0, :], idf[:, 2, :], 0.0, float(VOCAB - 1), ALU.max, ALU.min).then_inc(ids_steps, 1)
        dve.wait_ge(ids_steps, 4)
        dve.tensor_copy(idu[:], idf[:, 0, :]).then_inc(ids_ready, 1)

        def split_weights(n, par, b, g):
            dve.wait_ge(stage_loaded[b], (n // 2) * 16 + 16)
            dve.tensor_copy(w_hi[par][:, g, :], w_stage[:, b, :]).then_inc(hi_written, 1)
            return w_hi[par][:, g, :], w_lo[par][:, g, :], w_stage[:, b, :]

        for l in range(LAYERS):
            dve.wait_ge(eye_ready, 2)
            dve.wait_ge(mix_done, l + 1)
            dve.tensor_tensor(mix[:, l, :], ps_h[:, l % 2, :], eye[:].rearrange("p a b -> p (a b)"), ALU.add).then_inc(mix_ready, 1)
        for g in range(NG):
            hi, lo, raw = split_weights(g, 0, g % 2, g)
            dve.wait_ge(hi_written, g + 1)
            dve.tensor_tensor(lo, raw, hi.bitcast(F32), ALU.subtract).then_inc(w_split, 1)

        def split_x(k):
            dve.wait_ge(x_ready, k + 1)
            g, l = k % NG, (k // NG) % LAYERS
            for c in range(DC):
                dve.tensor_copy(x_hi[:, c, :], x32[:, c, bass.ds(g * G, G)])
            dve.tensor_copy(mix_hi[:].rearrange("p a b -> p (a b)"), mix[:, l, :]).then_inc(x_hi_done, 1)
            dve.wait_ge(x_hi_done, k + 1)
            for c in range(DC):
                dve.tensor_tensor(x_lo[:, c, :], x32[:, c, bass.ds(g * G, G)], x_hi[:, c, :].bitcast(F32), ALU.subtract)
            dve.tensor_tensor(mix_lo[:].rearrange("p a b -> p (a b)"), mix[:, l, :],
                              mix_hi[:].rearrange("p a b -> p (a b)").bitcast(F32), ALU.subtract).then_inc(x_split, 1)

        def statistics(n, k):
            if n == 0:
                dve.wait_ge(z_done, k + 1)
            else:
                dve.wait_ge(back_done, k + 1)
            for t in range(GT):
                ins = dve.bn_stats(stats[n][:, t, :], ps_tok[:, t, :])
            ins.then_inc(stats_done[n], 1)
            count = held(dve, k + 1)
            dve.wait_ge(eye_ready, 2)
            dve.wait_ge(stats_done[n], count)
            for t in range(GT):
                ins = dve.bn_aggr(mv[n][:, t, :], stats[n][:, t, :])
            ins.then_inc(mv_done[n], 1)
            dve.wait_ge(mv_done[n], k + 1)
            dve.tensor_scalar(var_eps[n][:], mv[n][:, :, 1], EPS, None, ALU.add).then_inc(ve_done[n], 1)

        def reciprocal(n, k):
            dve.wait_ge(std_done[n], k + 1)
            dve.reciprocal(rstd[n][:], std[n][:]).then_inc(rstd_done[n], 1)
            dve.wait_ge(rstd_done[n], k + 1)
            dve.scalar_tensor_tensor(out=nmr[n][:], in0=mv[n][:, :, 0], scalar=-1.0, in1=rstd[n][:],
                                     op0=ALU.mult, op1=ALU.mult).then_inc(nmr_done[n], 1)

        def split_a(k, b):
            dve.wait_ge(a32_ready, k + 1)
            dve.tensor_copy(a_hi[:, b], a32[:, b]).then_inc(a_hi_done, 1)
            dve.wait_ge(a_hi_done, k + 1)
            dve.tensor_tensor(a_lo[:, b], a32[:, b], a_hi[:, b].bitcast(F32), ALU.subtract).then_inc(a_split, 1)

        def residual(k, b, l):
            dve.wait_ge(ff2_done, k + 1)
            if not (isinstance(k, int) and k == 0):
                dve.wait_ge(back_done, k)
            for c in range(DC):
                ins = dve.scalar_tensor_tensor(out=u2[:, c, :], in0=ps_y[:, c, :], scalar=vec[:, l, FF_B2 + c:FF_B2 + c + 1],
                                               in1=a32[:, b, c, :], op0=ALU.add, op1=ALU.add)
            ins.then_inc(u2_ready, 1)

        def low_hidden(s, m):
            dve.wait_ge(h_hi_ready, s * FC + (m + 1))
            dve.tensor_tensor(h_lo[:, m, :], h32[:, m % 2, :], h_hi[:, m, :].bitcast(F32), ALU.subtract).then_inc(h_lo_ready, 1)

        split_x(0)
        statistics(0, 0)
        reciprocal(0, 0)
        split_x(1)
        split_a(0, 0)
        dve.wait_ge(vec_loaded, 32)

        def body(s, l, b, par):
            two = not (isinstance(s, int) and s == 0)
            if two:
                residual(s - 1, 1 - b, (s - 1) // NG)
            statistics(0, s + 1)
            low_hidden(s, 0)
            reciprocal(0, s + 1)
            low_hidden(s, 1)
            low_hidden(s, 2)
            split_x(s + 2)
            low_hidden(s, 3)
            split_a(s + 1, 1 - b)
            low_hidden(s, 4)
            low_hidden(s, 5)
            if two:
                statistics(1, s - 1)
            low_hidden(s, 6)
            if two:
                reciprocal(1, s - 1)
            piece(s, b, par)
            low_hidden(s, 7)

        def piece(s, b, par):
            g = s % NG
            n = s + NG
            dve.wait_ge(stage_loaded[b], (n // 2) * 16 + 16)
            dve.tensor_copy(w_hi[1 - par][:, g, :], w_stage[:, b, :]).then_inc(hi_written, 1)
            dve.wait_ge(hi_written, n + 1)
            dve.tensor_tensor(w_lo[1 - par][:, g, :], w_stage[:, b, :], w_hi[1 - par][:, g, :].bitcast(F32),
                              ALU.subtract).then_inc(w_split, 1)

        slots(dve, body)
        residual(SLOTS - 1, 1, LAYERS - 1)
        statistics(1, SLOTS - 1)
        reciprocal(1, SLOTS - 1)


HEADS = 16
DH = 64
PAIRS = HEADS // 2
LOCAL_PAIRS = 2
SORT_PAIRS = PAIRS - LOCAL_PAIRS
SEQ = 2048
BATCH = N_TOK // SEQ
BK = 32
NB = SEQ // BK
BT = P // BK
ST = SEQ // P
SG = SEQ // G
NEG = -3.4028234663852886e38


def attention(nc, ctx, io, x32):
    def sb(name, shape, dt=F32):
        return ctx.enter_context(nc.sbuf_tensor("a_" + name, shape, dt))

    def sem(name):
        return ctx.enter_context(nc.semaphore("a_" + name))

    y_hi = sb("y_hi", [P, DC, SEQ], F32R)
    y_lo = sb("y_lo", [P, DC, SEQ], F32R)
    w_stage = sb("w_stage", [P, 4, D])
    w_hi = sb("w_hi", [P, 3, DC, P], F32R)
    w_lo = sb("w_lo", [P, 3, DC, P], F32R)
    wo_hi = sb("wo_hi", [P, D], F32R)
    wo_lo = sb("wo_lo", [P, D], F32R)
    q_t = sb("q_t", [P, SEQ])
    keys = sb("keys", [P, 2, SEQ + 2])
    v_t = sb("v_t", [P, SEQ + 2 * BK])
    v_by_t = sb("v_by_t", [P, SEQ])
    k_bk = sb("k_bk", [P, BK // 2, P])
    v_bk = sb("v_bk", [P, BK // 2, P])
    v_tok = [sb(f"v_tok{i}", [P, ST, P]) for i in range(2)]
    scratch = sb("scratch", [P, 2, 1024])
    p_diag = sb("p_diag", [P, 2, 32, P])
    att_hi = sb("att_hi", [P, SEQ], F32R)
    att_lo = sb("att_lo", [P, SEQ], F32R)
    ident = sb("ident", [P, P])
    stats = q_t[:, 0:GT * 6].rearrange("p (t n) -> p t n", t=GT)
    mv = q_t[:, 64:64 + GT * 2].rearrange("p (t n) -> p t n", t=GT)
    var_eps, std, rstd, nmr = (q_t[:, 128 + 64 * n:128 + 64 * n + GT] for n in range(4))
    b_out = sb("b_out", [P, DC])
    sort_w = sb("sort_w", [P, 2, NB])
    sums = sb("sums", [P, 2, NB])
    r_log = sb("r_log", [P, NB])
    r_two = sb("r_two", [P, 2, NB])
    r_diag = sb("r_diag", [P, 2, P])
    r_small = sb("r_small", [P, 4])
    s_max = sb("s_max", [P, 16])
    s_sum = sb("s_sum", [P, 16])
    s_inv = sb("s_inv", [P, 16])
    mixed_t = scratch[:].rearrange("p a b -> p (a b)")
    x_static = scratch[:].rearrange("p a (c n) -> p a c n", c=DC)
    own_keys = keys[:, 0, 1:1 + SEQ]
    mixed_keys = keys[:, 1, 1:1 + SEQ]
    xn = [v_tok[i][:, 0:8, :].rearrange("p a b -> p (a b)").rearrange("p (t d) -> p t d", t=GT) for i in range(2)]
    values = {True: [v_tok[0], v_tok[1], k_bk], False: [v_tok[0], v_tok[1]]}

    ring = ctx.enter_context(nc.psum_tensor("a_ring", [P, 4, G], F32))
    quad = ctx.enter_context(nc.psum_tensor("a_quad", [P, 4, G], F32))

    ident_ready = sem("ident_ready")
    bias_loaded = sem("bias_loaded")
    pads_ready = sem("pads_ready")
    back_done = sem("back_done")
    norm_steps = sem("norm_steps")
    ve_done = sem("ve_done")
    std_done = sem("std_done")
    nmr_done = sem("nmr_done")
    xn_ready = sem("xn_ready")
    fwd_done = sem("fwd_done")
    y_hi_ready = sem("y_hi_ready")
    y_ready = sem("y_ready")
    bias_added = sem("bias_added")
    w_loaded = sem("w_loaded")
    w_hi_done = sem("w_hi_done")
    w_ready = sem("w_ready")
    wo_ready = sem("wo_ready")
    sort_loaded = sem("sort_loaded")
    proj_done = sem("proj_done")
    proj_read = sem("proj_read")
    sums_done = sem("sums_done")
    turned = {True: sem("turned_local"), False: sem("turned_sort")}
    turned_read = {True: sem("turned_read_local"), False: sem("turned_read_sort")}
    logits_done = sem("logits_done")
    logits_read = sem("logits_read")
    r_max_done = sem("r_max_done")
    r_neg_done = sem("r_neg_done")
    r_exp_done = sem("r_exp_done")
    r_inv_done = sem("r_inv_done")
    r_two_done = sem("r_two_done")
    r_turned = sem("r_turned")
    r_ready = sem("r_ready")
    mix_done = sem("mix_done")
    mix_read = sem("mix_read")
    kinds = {True: "local", False: "sort"}
    s_done = {k: sem("s_done_" + n) for k, n in kinds.items()}
    s_read = {k: sem("s_read_" + n) for k, n in kinds.items()}
    s_masked = sem("s_masked")
    s_max_done = {k: sem("s_max_done_" + n) for k, n in kinds.items()}
    s_sub_done = {k: sem("s_sub_done_" + n) for k, n in kinds.items()}
    s_exp_done = {k: sem("s_exp_done_" + n) for k, n in kinds.items()}
    s_sum_done = {k: sem("s_sum_done_" + n) for k, n in kinds.items()}
    s_inv_done = {k: sem("s_inv_done_" + n) for k, n in kinds.items()}
    s_norm_done = {k: sem("s_norm_done_" + n) for k, n in kinds.items()}
    p_ready = {k: sem("p_ready_" + n) for k, n in kinds.items()}
    v_by_t_ready = sem("v_by_t_ready")
    x_staged = sem("x_staged")
    pv_done = {k: sem("pv_done_" + n) for k, n in kinds.items()}
    att_hi_ready = sem("att_hi_ready")
    att_ready = sem("att_ready")
    out_done = sem("out_done")
    x_added = sem("x_added")

    UNITS = {True: 4, False: 2}
    TILES = {True: ST // 4, False: ST // 2}
    BLOCKS = {True: 3, False: 2}
    SCALE = {True: 1.0, False: DH ** -0.5}

    def pairs(eng, start, body):
        with eng.Fori(0, BATCH) as b:
            start(b)
            with eng.Fori(0, LOCAL_PAIRS) as c:
                body(b * PAIRS + c, b * LOCAL_PAIRS + c, True, True)
            with eng.Fori(0, SORT_PAIRS - 1) as c:
                body(b * PAIRS + c + LOCAL_PAIRS, b * SORT_PAIRS + c, False, True)
            body(b * PAIRS + (PAIRS - 1), b * SORT_PAIRS + (SORT_PAIRS - 1), False, False)

    block = ctx.enter_context(nc.Block())

    @block.sync
    def _(sp):
        sp.dma_start(b_out[:], io["b_out"]).then_inc(bias_loaded, 16)
        sp.dma_start(w_stage[:], io["wa"][0]).then_inc(w_loaded, 16)

        def start(b):
            pass

        def body(i, n, local, more):
            if not local:
                sp.wait_ge(r_max_done, n + 1)
                sp.dma_start(sort_w[:], io["sort_w"][n % SORT_PAIRS]).then_inc(sort_loaded, 16)
            sp.wait_ge(wo_ready, i + 1)
            sp.dma_start(w_stage[:], io["wa"][(i + 1) % PAIRS]).then_inc(w_loaded, 16)
        pairs(sp, start, body)
        sp.wait_ge(w_loaded, 16 * (BATCH * PAIRS + 1))

    @block.gpsimd
    def _(pool):
        pool.memset(ident[:], 0.0).then_inc(ident_ready, 1)
        pool.wait_ge(ident_ready, 1)
        pool.affine_select(out=ident[:], in_=ident[:], compare_op=ALU.not_equal, fill=1.0, base=0,
                           pattern=[[-1, P]], channel_multiplier=1).then_inc(ident_ready, 1)
        for i in range(2):
            pool.memset(p_diag[:, i], 0.0)
        pool.memset(r_diag[:], 0.0)
        pool.memset(keys[:, 0, 0:1], 0.0)
        pool.memset(keys[:, 0, SEQ + 1:], 0.0)
        pool.memset(v_t[:, 0:BK], 0.0)
        pool.memset(v_t[:, BK + SEQ:], 0.0).then_inc(pads_ready, 1)

        pool.wait_ge(bias_loaded, 16)

        def split_weights(i):
            count = held(pool, i * 16 + 16)
            pool.wait_ge(ident_ready, 2)
            pool.wait_ge(w_loaded, count)
            pool.tensor_copy(w_hi[:].rearrange("p a b c -> p (a b c)"), w_stage[:, 0:3, :].rearrange("p a b -> p (a b)")).then_inc(w_hi_done, 1)
            pool.wait_ge(w_hi_done, i * 2 + 1)
            pool.tensor_tensor(w_lo[:].rearrange("p a b c -> p (a b c)"), w_stage[:, 0:3, :].rearrange("p a b -> p (a b)"),
                               w_hi[:].rearrange("p a b c -> p (a b c)").bitcast(F32), ALU.subtract).then_inc(w_ready, 1)

        def split_out_weights(i):
            pool.tensor_copy(wo_hi[:], w_stage[:, 3, :]).then_inc(w_hi_done, 1)
            pool.wait_ge(w_hi_done, i * 2 + 2)
            pool.tensor_tensor(wo_lo[:], w_stage[:, 3, :], wo_hi[:].bitcast(F32), ALU.subtract).then_inc(wo_ready, 1)

        split_weights(0)
        split_out_weights(0)

        def start(b):
            pass

        def body(i, n, local, more):
            pool.wait_ge(proj_done, i * 12 + 12)
            split_weights(i + 1)
            if more:
                count = held(pool, i * 12 + 24)
                pool.wait_ge(ident_ready, 2)
                pool.wait_ge(proj_read, count)
                pool.tensor_copy(v_by_t[:].rearrange("p (t v) -> p v t", v=NB),
                                 v_t[:, BK:BK + SEQ].rearrange("p (v t) -> p v t", t=BK)).then_inc(v_by_t_ready, 1)
            count = held(pool, i * 8 + 8)
            pool.wait_ge(ident_ready, 2)
            pool.wait_ge(out_done, count)
            split_out_weights(i + 1)
        pairs(pool, start, body)

    @block.scalar
    def _(act):
        act.wait_ge(pads_ready, 1)

        def start(b):
            for g in range(SG):
                k = b * SG + g
                act.wait_ge(ve_done, k + 1)
                act.activation(std, var_eps, ACT.Sqrt).then_inc(std_done, 1)
                act.wait_ge(nmr_done, k + 1)
                if g >= 2:
                    act.wait_ge(fwd_done, k - 1)
                for t in range(GT):
                    ins = act.activation(xn[g % 2][:, t, :], ring[:, (g % 2) * 2 + t // 2, (t % 2) * D:(t % 2 + 1) * D], ACT.Identity,
                                         scale=rstd[:, t:t + 1], bias=nmr[:, t:t + 1])
                ins.then_inc(xn_ready, 1)
                act.wait_ge(fwd_done, k + 1)
                act.activation(y_hi[:, :, g * G:(g + 1) * G], quad[:, (g % 2) * 2:(g % 2) * 2 + 2, :], ACT.Copy).then_inc(y_hi_ready, 1)
            read_projection(b * PAIRS)

        def read_projection(i, parts=(0, 1, 2)):
            for j in [4 * part + g for part in parts for g in range(SG)]:
                kind, g = j // SG, j % SG
                act.wait_ge(proj_done, i * 12 + (j + 1))
                src = ring[:, j % 4, :]
                if kind == 0:
                    ins = act.activation(q_t[:, g * G:(g + 1) * G], src, ACT.Copy)
                elif kind == 1:
                    nb = G // BK
                    ins = act.activation(own_keys.rearrange("p (t v) -> p v t", v=NB)[:, g * nb:(g + 1) * nb, :],
                                         src.rearrange("p (v t) -> p v t", t=BK), ACT.Copy)
                else:
                    ins = act.activation(v_t[:, BK + g * G:BK + (g + 1) * G], src, ACT.Copy)
                ins.then_inc(proj_read, 1)

        def body(i, n, local, more):
            per = 12 if local else 16
            dests = values[True] if local else [k_bk, v_tok[0], v_bk]

            def read_turned(first, last):
                for c in range(first, last):
                    act.wait_ge(turned[local], n * per + (c + 1))
                    dest = dests[c // 4] if c < 12 else v_tok[1]
                    act.activation(dest[:, (c % 4) * 4:(c % 4) * 4 + 4, :].rearrange("p a b -> p (a b)"), ring[:, c % 4, :], ACT.Copy)\
                       .then_inc(turned_read[local], 1)

            read_turned(0, 12)
            if not local:
                for r in range(2):
                    act.wait_ge(logits_done, n * 2 + (r + 1))
                    act.activation(r_log[r * DH:(r + 1) * DH, :], ring[r * DH:(r + 1) * DH, r, 0:NB], ACT.Relu).then_inc(logits_read, 1)
                act.wait_ge(r_neg_done, n + 1)
                act.activation(r_log[:], r_log[:], ACT.Exp, bias=r_small[:, 1:2], accum_out=r_small[:, 2:3]).then_inc(r_exp_done, 1)
                act.wait_ge(r_turned, n + 1)
                for copy in range(2):
                    rows = slice(copy * NB, (copy + 1) * NB)
                    ins = act.activation(r_diag[rows, :, rows], ring[rows, 2, 0:P].rearrange("p (r u) -> p r u", r=2), ACT.Copy)
                ins.then_inc(r_ready, 1)
                read_turned(12, 16)
            U, T, W = UNITS[local], TILES[local], BLOCKS[local] * BK

            def read_scores(u):
                act.wait_ge(s_done[local], n * U + (u + 1))
                if u >= 2:
                    act.wait_ge(p_ready[local], n * U + (u - 1))
                act.activation(scratch[:, u % 2, 0:2 * T * W].rearrange("p (r n) -> p r n", r=2),
                               quad[:, (u % 2) * 2:(u % 2) * 2 + 2, 0:T * W], ACT.Copy, scale=SCALE[local]).then_inc(s_read[local], 1)

            def exponent(u):
                act.wait_ge(s_sub_done[local], n * U + (u + 1))
                sc = scratch[:, u % 2, 0:2 * T * W]
                act.activation(sc, sc, ACT.Exp).then_inc(s_exp_done[local], 1)

            read_scores(0)
            read_scores(1)
            for u in range(U):
                exponent(u)
                if u + 2 < U:
                    read_scores(u + 2)
                if more and u >= U - 2:
                    read_projection(i + 1, (0,) if u == U - 2 else (1, 2))
            for g in range(SG):
                act.wait_ge(pv_done[local], n * U + (g * U // SG + 1))
                act.activation(att_hi[:, g * G:(g + 1) * G], quad[:, g, :], ACT.Copy).then_inc(att_hi_ready, 1)
        pairs(act, start, body)

    @block.tensor
    def _(pe):
        pe.wait_ge(ident_ready, 2)
        pe.wait_ge(pads_ready, 1)

        def start(b):
            def back(g):
                pe.wait_ge(x_staged, b * SG + (g + 1))
                if g >= 2:
                    pe.wait_ge(xn_ready, b * SG + (g - 1))
                else:
                    pe.wait_ge(x_added, b * (PAIRS * 8) + 1)
                for t in range(GT):
                    for c in range(DC):
                        tr = pe.transpose(ring[:, (g % 2) * 2 + t // 2, (t % 2) * D + c * P:(t % 2) * D + (c + 1) * P],
                                          x_static[:, g % 2, c, t * P:(t + 1) * P], ident[:])
                tr.then_inc(back_done, 1)

            back(0)
            for g in range(SG):
                if g + 1 < SG:
                    back(g + 1)
                pe.wait_ge(xn_ready, b * SG + (g + 1))
                if g >= 2:
                    pe.wait_ge(y_ready, b * SG + (g - 1))
                else:
                    pe.wait_ge(att_ready, b * (PAIRS * 4) + 1)
                for c in range(DC):
                    for t in range(GT):
                        tr = pe.transpose(quad[:, (g % 2) * 2 + c, t * P:(t + 1) * P], xn[g % 2][:, t, c * P:(c + 1) * P], ident[:])
                tr.then_inc(fwd_done, 1)
            pe.wait_ge(y_ready, b * SG + SG)
            project(b * PAIRS)

        def around(h, bk):
            first = keys[h, 0, bk:bk + 3]
            return bass.AP(tensor=first.tensor, offset=first.offset, ap=[first.ap[0], [1, 3], [NB, BK]])

        def passes(out, lhs, rhs, start, stop):
            pe.matmul(out, lhs[0], rhs[0], start=start, stop=False)
            pe.matmul(out, lhs[0], rhs[1], start=False, stop=False)
            return pe.matmul(out, lhs[1], rhs[0], start=False, stop=stop)

        def project(i, parts=(0, 1, 2)):
            if parts[0] == 0:
                pe.wait_ge(w_ready, i + 1)
            for j in [4 * part + g for part in parts for g in range(SG)]:
                kind, g = j // SG, j % SG
                if j >= 4:
                    pe.wait_ge(proj_read, i * 12 + (j - 3))
                for kc in range(DC):
                    mm = passes(ring[:, j % 4, :], (w_hi[:, kind, kc, :], w_lo[:, kind, kc, :]),
                                (y_hi[:, kc, g * G:(g + 1) * G], y_lo[:, kc, g * G:(g + 1) * G]), kc == 0, kc == DC - 1)
                mm.then_inc(proj_done, 1)

        def body(i, n, local, more):
            per = 12 if local else 16
            pe.wait_ge(proj_read, i * 12 + 12)
            pe.wait_ge(x_added, i * 8 + 1)

            def turn(c, sources):
                if c >= 4:
                    pe.wait_ge(turned_read[local], n * per + (c - 3))
                for k, src in enumerate(sources):
                    tr = pe.transpose(ring[:, c % 4, k * P:(k + 1) * P], src, ident[:])
                tr.then_inc(turned[local], 1)

            if local:
                for w in range(3):
                    for c in range(4):
                        turn(4 * w + c, [v_t[:, w * BK + t * P:w * BK + (t + 1) * P] for t in range(4 * c, 4 * c + 4)])
            else:
                for c in range(4):
                    turn(c, [own_keys[:, m * P:(m + 1) * P] for m in range(4 * c, 4 * c + 4)])
                for c in range(4):
                    turn(4 + c, [v_t[:, BK + t * P:BK + (t + 1) * P] for t in range(4 * c, 4 * c + 4)])
                pe.wait_ge(v_by_t_ready, n + n // SORT_PAIRS + LOCAL_PAIRS)
                for c in range(4):
                    turn(8 + c, [v_by_t[:, m * P:(m + 1) * P] for m in range(4 * c, 4 * c + 4)])
                pe.wait_ge(sums_done, n * 2 + 2)
                pe.wait_ge(sort_loaded, n * 16 + 16)
                for r in range(2):
                    count = held(pe, n * per + (9 + r))
                    pe.wait_ge(ident_ready, 2)
                    pe.wait_ge(turned_read[False], count)
                    h = slice(r * DH, (r + 1) * DH)
                    pe.matmul(ring[h, r, 0:NB], sums[h, 0, :], sort_w[h, 0, :], start=True, stop=False)
                    pe.matmul(ring[h, r, 0:NB], sums[h, 1, :], sort_w[h, 1, :], start=False, stop=True).then_inc(logits_done, 1)
                pe.wait_ge(turned_read[False], n * per + 12)
                pe.wait_ge(r_two_done, n + 1)
                pe.transpose(ring[:, 2, 0:P], r_two[:].rearrange("p a b -> p (a b)"), ident[:]).then_inc(r_turned, 1)
                pe.wait_ge(r_ready, n + 1)
                for unit in range(4):
                    src = (k_bk, v_bk)[unit // 2]
                    count = held(pe, n * 4 + (unit - 1) if unit >= 2 else i * 4 + 1)
                    pe.wait_ge(ident_ready, 2)
                    if unit >= 2:
                        pe.wait_ge(mix_read, count)
                    else:
                        pe.wait_ge(att_ready, count)
                    for m in range(8):
                        for r in range(2):
                            at = (m % 4) * P
                            mm = pe.matmul(quad[r * DH:(r + 1) * DH, (unit % 2) * 2 + m // 4, at:at + P],
                                           src[:, (unit % 2) * 8 + m, r * DH:(r + 1) * DH], r_diag[:, r, :], start=True, stop=True)
                    mm.then_inc(mix_done, 1)
                pe.wait_ge(mix_read, n * 4 + 4)
                for c in range(4):
                    if c < 3:
                        pe.wait_ge(logits_read, n * 2 + 2)
                    turn(12 + c, [mixed_t[:, t * P:(t + 1) * P] for t in range(4 * c, 4 * c + 4)])
            U, T, W = UNITS[local], TILES[local], BLOCKS[local]
            for u in range(U):
                if u >= 2 or local:
                    count = held(pe, n * U + (u - 1) if u >= 2 else i * 4 + 1)
                    pe.wait_ge(ident_ready, 2)
                    pe.wait_ge(s_read[local] if u >= 2 else att_ready, count)
                for t in range(u * T, (u + 1) * T):
                    for r in range(2):
                        h = slice(r * DH, (r + 1) * DH)
                        for j in range(BT):
                            bk = t * BT + j
                            if local:
                                rhs = around(h, bk)
                            else:
                                rhs = keys[h, :, 1 + bk:1 + bk + SEQ - NB + 1:NB]
                            out = quad[j * BK:(j + 1) * BK, (u % 2) * 2 + r, (t % T) * W * BK:(t % T + 1) * W * BK]
                            mm = pe.matmul(out.rearrange("p (a b) -> p a b", b=BK), q_t[h, bk * BK:(bk + 1) * BK], rhs, start=True, stop=True)
                mm.then_inc(s_done[local], 1)
            pe.wait_ge(turned_read[local], n * per + per)
            if not local:
                pe.wait_ge(r_ready, n + 1)
            if more:
                project(i + 1, (0,) if local else (0, 1))
            for u in range(U):
                count = held(pe, n * U + (u + 1))
                if local:
                    pe.wait_ge(s_read[local], n * U + min(u + 3, U))
                else:
                    pe.wait_ge(s_read[local], n * U + (u + 1))
                pe.wait_ge(ident_ready, 2)
                pe.wait_ge(p_ready[local], count)
                for t in range(T):
                    tile = u * T + t
                    for r in range(2):
                        for w in range(W):
                            mm = pe.matmul(quad[r * DH:(r + 1) * DH, tile // GT, (tile % GT) * P:(tile % GT + 1) * P],
                                           values[local][w][:, tile, r * DH:(r + 1) * DH], p_diag[:, u % 2, (r * T + t) * W + w, :],
                                           start=(w == 0), stop=(w == W - 1))
                mm.then_inc(pv_done[local], 1)
                if more and u < U - 1 - local:
                    project(i + 1, (u + 1 if local else 2,))
            pe.wait_ge(att_ready, i * 4 + 5)
            pe.wait_ge(wo_ready, i + 1)
            for j in range(8):
                g, oc = j // 2, j % 2
                if j < 4:
                    if more:
                        pe.wait_ge(proj_read, i * 12 + 24)
                else:
                    pe.wait_ge(x_added, i * 8 + (j - 2))
                cols = slice(g * G, (g + 1) * G)
                passes(ring[:, j % 4, :], (wo_hi[:, oc * P:(oc + 1) * P], wo_lo[:, oc * P:(oc + 1) * P]),
                       (att_hi[:, cols], att_lo[:, cols]), True, True).then_inc(out_done, 1)
        pairs(pe, start, body)

    @block.vector
    def _(dve):
        dve.memset(s_max[:], 0.0).then_inc(r_max_done, 1)
        dve.memset(s_sum[:], 0.0).then_inc(x_added, 1)
        dve.memset(s_inv[:], 0.0).then_inc(att_ready, 1)
        dve.wait_ge(bias_loaded, 16)
        dve.wait_ge(pads_ready, 1)

        def start(b):
            def stage(g):
                if g >= 2:
                    dve.wait_ge(back_done, b * SG + (g - 1))
                dve.tensor_copy(x_static[:, g % 2], x32[:, :, bass.ds(b * SEQ + g * G, G)]).then_inc(x_staged, 1)

            stage(0)
            stage(1)
            for g in range(SG):
                k = b * SG + g
                dve.wait_ge(back_done, k + 1)
                if g + 2 < SG:
                    stage(g + 2)
                for t in range(GT):
                    ins = dve.bn_stats(stats[:, t, :], ring[:, (g % 2) * 2 + t // 2, (t % 2) * D:(t % 2 + 1) * D])
                ins.then_inc(norm_steps, 1)
                count = held(dve, k * 3 + 1)
                dve.wait_ge(ident_ready, 2)
                dve.wait_ge(norm_steps, count)
                for t in range(GT):
                    ins = dve.bn_aggr(mv[:, t, :], stats[:, t, :])
                ins.then_inc(norm_steps, 1)
                dve.wait_ge(norm_steps, k * 3 + 2)
                dve.tensor_scalar(var_eps, mv[:, :, 1], EPS, None, ALU.add).then_inc(ve_done, 1)
                dve.wait_ge(std_done, k + 1)
                if g >= 1:
                    dve.wait_ge(xn_ready, k)
                dve.reciprocal(rstd, std).then_inc(norm_steps, 1)
                dve.wait_ge(norm_steps, k * 3 + 3)
                dve.scalar_tensor_tensor(out=nmr, in0=mv[:, :, 0], scalar=-1.0, in1=rstd,
                                         op0=ALU.mult, op1=ALU.mult).then_inc(nmr_done, 1)
                dve.wait_ge(y_hi_ready, k + 1)
                ys = slice(g * G, (g + 1) * G)
                dve.tensor_tensor(y_lo[:, :, ys], quad[:, (g % 2) * 2:(g % 2) * 2 + 2, :], y_hi[:, :, ys].bitcast(F32), ALU.subtract).then_inc(y_ready, 1)
                for c in range(DC):
                    xs = x32[:, c, bass.ds(b * SEQ + g * G, G)]
                    ins = dve.tensor_scalar(xs, xs, b_out[:, c:c + 1], None, ALU.add)
                ins.then_inc(bias_added, 1)

        def body(i, n, local, more):
            if not local:
                for k, src in enumerate((q_t[:].rearrange("p (v t) -> p v t", t=BK), own_keys.rearrange("p (t v) -> p v t", v=NB))):
                    dve.wait_ge(proj_read, i * 12 + 4 * (k + 1))
                    dve.tensor_reduce(sums[:, k, :], src, AX.X, ALU.add).then_inc(sums_done, 1)
                dve.wait_ge(logits_read, n * 2 + 2)
                dve.tensor_reduce(r_small[:, 0:1], r_log[:], AX.X, ALU.max).then_inc(r_max_done, 1)
                dve.wait_ge(r_max_done, n + 2)
                dve.tensor_scalar(r_small[:, 1:2], r_small[:, 0:1], -1.0, None, ALU.mult).then_inc(r_neg_done, 1)
                dve.wait_ge(r_exp_done, n + 1)
                dve.reciprocal(r_small[:, 3:4], r_small[:, 2:3]).then_inc(r_inv_done, 1)
                dve.wait_ge(r_inv_done, n + 1)
                for c in range(2):
                    ins = dve.tensor_scalar(r_two[:, c, :], r_log[:], r_small[:, 3:4], None, ALU.mult)
                ins.then_inc(r_two_done, 1)
                dest_k = mixed_keys.rearrange("p (t u) -> p t u", u=NB)
                dest_v = mixed_t.rearrange("p (u t) -> p t u", t=BK)
                for unit in range(4):
                    dve.wait_ge(mix_done, n * 4 + (unit + 1))
                    for half in range(2):
                        at = (unit % 2) * 16 + half * 8
                        ins = dve.tensor_copy((dest_k, dest_v)[unit // 2][:, at:at + 8, :],
                                              quad[:, (unit % 2) * 2 + half, :].rearrange("p (t u) -> p t u", u=NB))
                    ins.then_inc(mix_read, 1)
            U, T, W = UNITS[local], TILES[local], BLOCKS[local] * BK
            for u in range(U):
                k = n * U + u
                sc = scratch[:, u % 2, 0:2 * T * W]
                rows3 = sc.rearrange("p (a w) -> p a w", w=W)
                dve.wait_ge(s_read[local], k + 1)
                if local and u == 0:
                    dve.memset(sc.rearrange("p (r t w) -> p r t w", r=2, t=T)[0:BK, :, 0, 0:BK], NEG).then_inc(s_masked, 1)
                    dve.wait_ge(s_masked, n * 2 + 1)
                if local and u == U - 1:
                    dve.memset(sc.rearrange("p (r t w) -> p r t w", r=2, t=T)[P - BK:P, :, T - 1, 2 * BK:3 * BK], NEG).then_inc(s_masked, 1)
                    dve.wait_ge(s_masked, n * 2 + 2)
                mx, sm, iv = (x[:, 0:2 * T] for x in (s_max, s_sum, s_inv))
                dve.tensor_reduce(mx, rows3, AX.X, ALU.max).then_inc(s_max_done[local], 1)
                dve.wait_ge(s_max_done[local], k + 1)
                dve.tensor_tensor(rows3, rows3, mx.unsqueeze(2).to_broadcast([P, 2 * T, W]), ALU.subtract).then_inc(s_sub_done[local], 1)
                dve.wait_ge(s_exp_done[local], k + 1)
                dve.tensor_reduce(sm, rows3, AX.X, ALU.add).then_inc(s_sum_done[local], 1)
                dve.wait_ge(s_sum_done[local], k + 1)
                dve.reciprocal(iv, sm).then_inc(s_inv_done[local], 1)
                dve.wait_ge(s_inv_done[local], k + 1)
                dve.tensor_tensor(rows3, rows3, iv.unsqueeze(2).to_broadcast([P, 2 * T, W]), ALU.mult).then_inc(s_norm_done[local], 1)
                dve.wait_ge(s_norm_done[local], k + 1)
                if u >= 2:
                    dve.wait_ge(pv_done[local], n * U + (u - 1))
                for j in range(BT):
                    rows = slice(j * BK, (j + 1) * BK)
                    ins = dve.transpose(p_diag[rows, u % 2, 0:2 * T * BLOCKS[local], rows], sc[rows, :].rearrange("p (n k) -> p n k", k=BK))
                ins.then_inc(p_ready[local], 1)
            for g in range(SG):
                dve.wait_ge(att_hi_ready, i * 4 + (g + 1))
                cols = slice(g * G, (g + 1) * G)
                dve.tensor_tensor(att_lo[:, cols], quad[:, g, :], att_hi[:, cols].bitcast(F32), ALU.subtract).then_inc(att_ready, 1)
            at = (i // PAIRS) * SEQ
            dve.wait_ge(bias_added, (i // PAIRS) * SG + SG)
            for j in range(8):
                g, oc = j // 2, j % 2
                dve.wait_ge(out_done, i * 8 + (j + 1))
                xs = x32[:, oc, bass.ds(at + g * G, G)]
                dve.tensor_tensor(xs, ring[:, j % 4, :], xs, ALU.add).then_inc(x_added, 1)
        pairs(dve, start, body)


E = 7
CAP = 732
ET = -(-CAP // P)
LAST_ROWS = CAP - (ET - 1) * P
HALF = CAP // 2
REC = D + 4
NT = N_TOK // P
ES = 8
WC = 3 * D
SKIP = 1.0e6


def experts(nc, ctx, io, x32, rows_for, acc):
    def sb(name, shape, dt=F32):
        return ctx.enter_context(nc.sbuf_tensor("e_" + name, shape, dt))

    def sem(name):
        return ctx.enter_context(nc.semaphore("e_" + name))

    rec = sb("rec", [P, NT, REC])
    w_hi = sb("w_hi", [P, FC, WC], F32R)
    w_lo = sb("w_lo", [P, FC, WC], F32R)
    w_stage = sb("w_stage", [P, 2, WC])
    f_hi = sb("f_hi", [P, 2, DC, 768], F32R)
    f_lo = sb("f_lo", [P, 2, DC, 768], F32R)
    f32 = sb("f32", [P, DC, 768])
    xr = sb("xr", [P, ET, REC])
    s32 = sb("s32", [P, 2, G])
    g32 = sb("g32", [P, 768])
    g_hi = sb("g_hi", [P, 2, 768], F32R)
    g_lo = sb("g_lo", [P, 2, 768], F32R)
    yo = sb("yo", [P, ET, D])
    ht = sb("ht", [P, 2, GT, D])
    ident = sb("ident", [P, P])
    below = sb("below", [P, P])
    ones = sb("ones", [P, P])
    ln_g = sb("ln_g", [P, DC])
    ln_b = sb("ln_b", [P, DC])
    w_r = sb("w_r", [P, DC, E])
    stats = sb("stats", [P, 2, GT, 6])
    mv = sb("mv", [P, 2, GT, 2])
    var_eps = sb("ve", [P, 2, GT])
    std = sb("std", [P, 2, GT])
    rstd = sb("rstd", [P, 2, GT])
    nmr = sb("nmr", [P, 2, GT])
    iot = sb("iot", [P, 3, ES], I32)
    cst = sb("cst", [P, 3, ES])
    lg = sb("lg", [P, NT, ES])
    eq = sb("eq", [P, NT, ES])
    hot = sb("hot", [P, 2, NT, ES])
    top = sb("top", [P, 2, NT])
    which = sb("which", [P, 2, NT])
    small = sb("small", [P, 4, NT])
    tot = sb("tot", [P, ES])
    before = sb("before", [DH, 2 * NT, ES])
    at_pos = sb("at_pos", [P, 2 * NT, ES])
    place = sb("place", [P, 4, 2 * NT])
    place_u = sb("place_u", [P, 2 * NT], U32)
    gate = sb("gate", [P, ET])
    gate_next = sb("gate_next", [P, ET])
    tok_next = sb("tok_next", [P, ET], I32)
    gtmp = sb("gtmp", [P, 2, ET])
    tok = sb("tok", [P, ET], I32)

    ps = ctx.enter_context(nc.psum_tensor("e_ps", [P, 8, G], F32))

    consts_ready = sem("consts_ready")
    iota_done = sem("iota_done")
    cst_done = sem("cst_done")
    small_loaded = sem("small_loaded")
    back_done = sem("back_done")
    norm_steps = sem("norm_steps")
    ve_done = sem("ve_done")
    std_done = sem("std_done")
    nmr_done = sem("nmr_done")
    ht_ready = sem("ht_ready")
    ht_sent = [sem(f"ht_sent{i}") for i in range(2)]
    rec_ready = sem("rec_ready")
    fwd_done = sem("fwd_done")
    feat_ready = sem("feat_ready")
    logits_done = sem("logits_done")
    route = sem("route")
    gap_ready = sem("gap_ready")
    gate_exp_done = sem("gate_exp_done")
    hot_ready = sem("hot_ready")
    tot_done = sem("tot_done")
    before_ready = sem("before_ready")
    pos_done = sem("pos_done")
    place_ready = sem("place_ready")
    dispatched = sem("dispatched")
    w_loaded = [sem(f"w_loaded{i}") for i in range(2)]
    w_hi_done = sem("w_hi_done")
    w_ready = sem("w_ready")
    f_hi_done = sem("f_hi_done")
    f_ready = sem("f_ready")
    xr_loaded = sem("xr_loaded")
    xr_zeroed = sem("xr_zeroed")
    turned = sem("turned")
    f32_ready = sem("f32_ready")
    up_done = sem("up_done")
    silu_done = sem("silu_done")
    prod_done = sem("prod_done")
    g_hi_ready = sem("g_hi_ready")
    g_lo_ready = sem("g_lo_ready")
    down_done = sem("down_done")
    y_read = sem("y_read")
    y_sent = sem("y_sent")
    tok_done = sem("tok_done")
    gate_steps = sem("gate_steps")
    gate_ready = sem("gate_ready")

    JS = NG

    def jobs(eng, body):
        body(0, 0, None, None)
        body(1, 1, None, (0, 0, None))
        with eng.Fori(1, JS // 2 - 1) as i:
            for b in range(2):
                body(i * 2 + b, b, None, (i * 2 + (b - 1), 1 - b, None))
        for g in (JS - 2, JS - 1):
            body(g, g % 2, None, (g - 1, (g - 1) % 2, None))
        body(JS, None, 0, (JS - 1, (JS - 1) % 2, None))
        with eng.Fori(1, E - 1) as e:
            body(e + JS, None, e, (e + (JS - 1), None, e - 1))
        body(JS + E - 1, None, E - 1, (JS + E - 2, None, E - 2))

    def is_first(j):
        return isinstance(j, int) and j == 0

    def is_last_shared(j):
        return isinstance(j, int) and j == JS - 1

    def has_next(j, e):
        return is_last_shared(j) if e is None else not isinstance(e, int) or e < E - 1

    def part(j, e, m, h=0):
        return j * FC + m if e is None else e * (2 * FC) + (JS * FC + 2 * m + h)

    def y_bank(j, b, e):
        return 6 if e is None and b == 1 and not is_last_shared(j) else 4

    def w1(w, m, kc):
        return w[:, m, kc * P:(kc + 1) * P]

    def w3(w, m, kc):
        return w[:, m, D + kc * P:D + (kc + 1) * P]

    def w2(w, m):
        return w[:, m, 2 * D:3 * D]

    block = ctx.enter_context(nc.Block())

    @block.sync
    def _(sp):
        sp.dma_start(ln_g[:], io["ffn_g"]).then_inc(small_loaded, 16)
        sp.dma_start(ln_b[:], io["ffn_b"]).then_inc(small_loaded, 16)
        sp.dma_start(w_r[:], io["w_r"]).then_inc(small_loaded, 16)
        def send_rows(g):
            sp.wait_ge(ht_ready, g + 1)
            sp.dma_start(acc[g * G:(g + 1) * G, :].rearrange("(t p) d -> p t d", p=P), ht[:, g % 2, :, :]).then_inc(ht_sent[g % 2], 16)

        for q in range(FC):
            if q >= 2:
                sp.wait_ge(w_ready, q - 1)
            sp.dma_start(w_stage[:, q % 2, :], io["we"][q]).then_inc(w_loaded[q % 2], 16)
            send_rows(q)

        def load_weights(e, q0):
            for m in range(FC):
                sp.wait_ge(w_ready, q0 + (m - 1))
                sp.dma_start(w_stage[:, m % 2, :], io["we"][q0 + m]).then_inc(w_loaded[m % 2], 16)

        def load_rows(e):
            full = (ET - 1) * P
            sp.dma_start(xr[:, 0:ET - 1, :], rows_for[bass.ds(e * CAP, full), :].rearrange("(t p) c -> p t c", p=P)).then_inc(xr_loaded, 16)
            sp.dma_start(xr[0:LAST_ROWS, ET - 1, :], rows_for[bass.ds(e * CAP + full, LAST_ROWS), :]).then_inc(xr_loaded, 16)

        sp.wait_ge(xr_zeroed, 1)
        sp.wait_ge(dispatched, 16 * 2 * NT)
        load_rows(0)
        load_weights(0, FC)
        with sp.Fori(0, E - 1) as e:
            sp.wait_ge(tok_done, e + 1)
            sp.wait_ge(gate_steps, e * 3 + 3)
            sp.wait_ge(turned, e * 3 + 3)
            load_rows(e + 1)
            load_weights(e + 1, e * FC + 2 * FC)
        sp.wait_ge(y_sent, 16 * (JS + E * ET))

    @block.gpsimd
    def _(pool):
        pool.memset(ident[:], 0.0).then_inc(iota_done, 1)
        pool.memset(below[:], 1.0).then_inc(iota_done, 1)
        pool.memset(xr[:], 0.0).then_inc(xr_zeroed, 1)
        pool.memset(ones[:], 1.0)
        pool.wait_ge(iota_done, 2)
        pool.affine_select(out=ident[:], in_=ident[:], compare_op=ALU.not_equal, fill=1.0, base=0,
                           pattern=[[-1, P]], channel_multiplier=1)
        pool.affine_select(out=below[:], in_=below[:], compare_op=ALU.is_gt, fill=0.0, base=0,
                           pattern=[[1, P]], channel_multiplier=-1).then_inc(consts_ready, 1)
        pool.iota(iot[:, 0, :], pattern=[[-1, ES]], base=ES, channel_multiplier=0)
        pool.iota(iot[:, 1, :], pattern=[[CAP, ES]], base=0, channel_multiplier=0)
        pool.iota(iot[:, 2, :], pattern=[[1, ES]], base=0, channel_multiplier=0)
        pool.iota(rec[:].bitcast(I32)[:, :, D], pattern=[[P, NT]], base=0, channel_multiplier=1).then_inc(consts_ready, 1)

        for m in range(FC):
            pool.wait_ge(w_loaded[m % 2], (m // 2) * 16 + 16)
            pool.tensor_copy(w_hi[:, m, :], w_stage[:, m % 2, :]).then_inc(w_hi_done, 1)
            pool.wait_ge(w_hi_done, m + 1)
            pool.tensor_tensor(w_lo[:, m, :], w_stage[:, m % 2, :], w_hi[:, m, :].bitcast(F32), ALU.subtract).then_inc(w_ready, 1)

        def low_weights(q, m):
            pool.wait_ge(w_hi_done, q + 1)
            pool.tensor_tensor(w_lo[:, m, :], w_stage[:, m % 2, :], w_hi[:, m, :].bitcast(F32), ALU.subtract).then_inc(w_ready, 1)

        pool.wait_ge(place_ready, 1)
        for i in range(2):
            pool.wait_ge(ht_sent[i], 16 * NG // 2)
        sends = [(k, t) for k in range(2) for t in range(NT)]
        per = -(-len(sends) // (JS - 2))
        for j in range(JS):
            for k, t in sends[j * per:(j + 1) * per]:
                pool.indirect_dma_start(out=rows_for[:, :], in_=rec[:, t, :], in_offset=None,
                                        out_offset=bass.IndirectOffsetOnAxis(ap=place_u[:, k * NT + t:k * NT + t + 1], axis=0),
                                        bounds_check=E * CAP - 1, oob_is_err=False).then_inc(dispatched, 16)
            if j == JS - 1:
                for m in range(FC):
                    low_weights(FC + m, m)
            pool.wait_ge(y_read, j + 1)
            pool.dma_start(acc[j * G:(j + 1) * G, :].rearrange("(t p) d -> p t d", p=P), yo[:, 0:GT, :],
                           accum_op=ALU.add).then_inc(y_sent, 16)

        def body(e, more):
            if more:
                for m in range(FC):
                    low_weights(e * FC + (2 * FC + m), m)
            pool.wait_ge(y_read, e + (JS + 1))
            for t in range(ET):
                count = held(pool, e * (16 * ET) + 16 * (JS + t))
                pool.wait_ge(iota_done, 2)
                pool.wait_ge(y_sent, count)
                n = P if t < ET - 1 else LAST_ROWS
                pool.indirect_dma_start(out=acc[:, :], in_=yo[0:n, t, :], in_offset=None,
                                        out_offset=bass.IndirectOffsetOnAxis(ap=tok[0:n, t:t + 1].bitcast(U32), axis=0),
                                        compute_op=ALU.add).then_inc(y_sent, 16)
        with pool.Fori(0, E - 1) as e:
            body(e, True)
        body(E - 1, False)

    @block.scalar
    def _(act):
        act.wait_ge(small_loaded, 48)

        def root(g):
            act.wait_ge(ve_done, g + 1)
            act.activation(std[:, g % 2], var_eps[:, g % 2], ACT.Sqrt).then_inc(std_done, 1)

        root(0)
        for g in range(NG):
            act.wait_ge(nmr_done, g + 1)
            for t in range(GT):
                ins = act.activation(rec[:, g * GT + t, 0:D], ps[:, (g % 2) * 2 + t // 2, (t % 2) * D:(t % 2 + 1) * D], ACT.Identity,
                                     scale=rstd[:, g % 2, t:t + 1], bias=nmr[:, g % 2, t:t + 1])
            ins.then_inc(rec_ready, 1)
            if g + 1 < NG:
                root(g + 1)
            act.wait_ge(fwd_done, g + 1)
            for c in range(DC):
                ins = act.activation(x32[:, c, g * G:(g + 1) * G], ps[:, 4 + c, :], ACT.Identity,
                                     scale=ln_g[:, c:c + 1], bias=ln_b[:, c:c + 1])
            ins.then_inc(feat_ready, 1)
        act.wait_ge(gap_ready, 1)
        act.activation(small[:, 1, :], small[:, 0, :], ACT.Exp).then_inc(gate_exp_done, 1)

        def read_turned(e, q):
            act.wait_ge(turned, e * 3 + (q + 1))
            n = 2 * P if q < 2 else CAP - 4 * P
            for c in range(DC):
                ins = act.activation(f32[:, c, q * 2 * P:q * 2 * P + n], ps[:, 7, c * 2 * P:c * 2 * P + n], ACT.Identity,
                                     scale=ln_g[:, c:c + 1], bias=ln_b[:, c:c + 1])
            ins.then_inc(f32_ready, 1)

        def high_weights(j, e, m):
            first = FC if e is None else e * FC + 2 * FC
            act.wait_ge(w_loaded[m % 2], (first + m) // 2 * 16 + 16)
            act.wait_ge(down_done, j * FC + (m + 1))
            act.activation(w_hi[:, m, :], w_stage[:, m % 2, :], ACT.Copy).then_inc(w_hi_done, 1)

        def result(j, b, e):
            act.wait_ge(down_done, j * FC + FC)
            if e is None:
                if not is_first(j):
                    act.wait_ge(y_sent, j * 16)
                bank = y_bank(j, b, e)
                act.activation(yo[:, 0:GT, :].rearrange("p t d -> p (t d)"), ps[:, bank:bank + 2, :].rearrange("p a b -> p (a b)"), ACT.Copy).then_inc(y_read, 1)
            else:
                act.wait_ge(gate_ready, e + 2)
                act.wait_ge(y_sent, 16 * JS + (16 * ET) * e)
                for t in range(ET):
                    n = P if t < ET - 1 else LAST_ROWS
                    ins = act.activation(yo[0:n, t, :], ps[0:n, 4 + t // 2, (t % 2) * D:(t % 2 + 1) * D], ACT.Copy, scale=gate[0:n, t:t + 1])
                ins.then_inc(y_read, 1)
            if has_next(j, e):
                high_weights(j, e, FC - 1)

        def body(j, b, e, last):
            for m in range(FC):
                k = j * FC + m
                if e is None:
                    act.wait_ge(up_done, part(j, e, m + 1))
                    if not (is_first(j) and m < 2):
                        act.wait_ge(prod_done, part(j, e, m - 1))
                    act.activation(s32[:, m % 2, :], ps[:, (m % 2) * 2, :], ACT.Silu).then_inc(silu_done, 1)
                else:
                    for h in range(2):
                        act.wait_ge(up_done, part(j, e, m, h + 1))
                        act.wait_ge(prod_done, part(j, e, m, h - 1))
                        act.activation(s32[:, h, 0:HALF], ps[:, 2 * h, 0:HALF], ACT.Silu).then_inc(silu_done, 1)
                if m == 0 and last:
                    result(*last)
                act.wait_ge(prod_done, part(j, e, m + 1))
                if not (is_first(j) and m < 2):
                    act.wait_ge(down_done, k - 1)
                n = G if e is None else CAP
                act.activation(g_hi[:, m % 2, 0:n], g32[:, 0:n], ACT.Copy).then_inc(g_hi_ready, 1)
                if has_next(j, e) and m >= 1:
                    high_weights(j, e, m - 1)
                if has_next(j, e) and 4 <= m < 7:
                    if m == 4 and e is not None:
                        act.wait_ge(f_ready, j + 1)
                    read_turned(0 if e is None else e + 1, m - 4)
        jobs(act, body)
        result(JS + E - 1, None, E - 1)

    @block.tensor
    def _(pe):
        pe.wait_ge(consts_ready, 1)

        def back(g):
            if g >= 2:
                pe.wait_ge(rec_ready, g - 1)
                pe.wait_ge(ht_ready, g - 1)
            for t in range(GT):
                for c in range(DC):
                    tr = pe.transpose(ps[:, (g % 2) * 2 + t // 2, (t % 2) * D + c * P:(t % 2) * D + (c + 1) * P],
                                      x32[:, c, g * G + t * P:g * G + (t + 1) * P], ident[:])
            tr.then_inc(back_done, 1)

        def logits(g):
            pe.wait_ge(feat_ready, g + 1)
            pe.wait_ge(small_loaded, 48)
            for t in range(GT):
                for c in range(DC):
                    at = (g * GT + t) * ES
                    mm = pe.matmul(ps[:, 6, at:at + E], x32[:, c, g * G + t * P:g * G + (t + 1) * P], w_r[:, c, :],
                                   start=(c == 0), stop=(c == DC - 1))
            mm.then_inc(logits_done, 1)

        back(0)
        for g in range(NG):
            if g + 1 < NG:
                back(g + 1)
            pe.wait_ge(rec_ready, g + 1)
            if g >= 1:
                pe.wait_ge(feat_ready, g)
            for c in range(DC):
                for t in range(GT):
                    tr = pe.transpose(ps[:, 4 + c, t * P:(t + 1) * P], rec[:, g * GT + t, c * P:(c + 1) * P], ident[:])
            tr.then_inc(fwd_done, 1)
            if g >= 1:
                logits(g - 1)
        logits(NG - 1)

        def passes(out, lhs, rhs, start, stop, check=False):
            pe.matmul(out, lhs[0], rhs[0], start=start, stop=False, skip_group_check=check)
            pe.matmul(out, lhs[0], rhs[1], start=False, stop=False, skip_group_check=check)
            return pe.matmul(out, lhs[1], rhs[0], start=False, stop=stop, skip_group_check=check)

        def up(j, b, e, m):
            if m == 0:
                pe.wait_ge(f_ready, j + 1)
            if e is None:
                if is_first(j):
                    pe.wait_ge(w_ready, m + 1)
                if not (is_first(j) and m < 2):
                    pe.wait_ge(prod_done, part(j, e, m - 1))
                elif m == 0:
                    pe.wait_ge(rec_ready, NG)
                    pe.wait_ge(ht_ready, NG)
                halves = [((m % 2) * 2, 0, G)]
            else:
                pe.wait_ge(w_ready, e * FC + (FC + m + 1))
                halves = [(2 * h, h * HALF, HALF) for h in range(2)]
            for h, (bank, at, n) in enumerate(halves):
                if e is not None:
                    pe.wait_ge(prod_done, part(j, e, m, h - 1))
                par = b if b is not None else e % 2
                for which_w, w in enumerate((w1, w3)):
                    for kc in range(DC):
                        rhs = [f[:, par, kc, at:at + n] for f in (f_hi, f_lo)]
                        mm = passes(ps[:, bank + which_w, 0:n], (w(w_hi, m, kc), w(w_lo, m, kc)), rhs, kc == 0, kc == DC - 1)
                mm.then_inc(up_done, 1)

        def down(j, b, e, m):
            k = j * FC + m
            pe.wait_ge(g_hi_ready, k + 1)
            pe.wait_ge(g_lo_ready, k + 1)
            if m == 0:
                if is_first(j):
                    pe.wait_ge(feat_ready, NG)
                elif e is None and isinstance(j, int) and j == 1:
                    pe.wait_ge(place_ready, 1)
                elif e is None and not is_last_shared(j):
                    pe.wait_ge(y_read, j - 1)
                else:
                    pe.wait_ge(y_read, j)
            for t in range(GT if e is None else ET):
                n = P if t < ET - 1 else LAST_ROWS
                g = [x[:, m % 2, t * P:t * P + n] for x in (g_hi, g_lo)]
                mm = passes(ps[0:n, y_bank(j, b, e) + t // 2, (t % 2) * D:(t % 2 + 1) * D], g, (w2(w_hi, m), w2(w_lo, m)),
                            m == 0 and t % 2 == 0, m == FC - 1, True)
            mm.then_inc(down_done, 1)

        def turn(e, q):
            if q == 0:
                pe.wait_ge(xr_loaded, e * 32 + 32)
                if isinstance(e, int) and e == 0:
                    pe.wait_ge(y_read, JS - 2)
                else:
                    pe.wait_ge(f32_ready, e * 3)
            else:
                pe.wait_ge(f32_ready, e * 3 + q)
            for c in range(DC):
                for t in (2 * q, 2 * q + 1):
                    n = P if t < ET - 1 else LAST_ROWS
                    tr = pe.transpose(ps[:, 7, c * 2 * P + (t % 2) * P:c * 2 * P + (t % 2) * P + n], xr[0:n, t, c * P:(c + 1) * P], ident[0:n, 0:n])
            tr.then_inc(turned, 1)

        def body(j, b, e, last):
            for m in range(FC):
                up(j, b, e, m)
                if m >= 1:
                    down(j, b, e, m - 1)
                elif last:
                    down(*last, FC - 1)
                if has_next(j, e) and 4 <= m < 7:
                    turn(0 if e is None else e + 1, m - 4)
            if is_first(j):
                pe.wait_ge(hot_ready, 1)
                for x in range(ES):
                    mm = pe.matmul(ps[0:2 * NT, 7, x:x + 1], hot[:].rearrange("p k t x -> p (k t) x")[:, :, x], ones[:, 0:1], start=True, stop=True)
                mm.then_inc(tot_done, 1)
                pe.wait_ge(before_ready, 1)
                pe.matmul(ps[:, 7, :], below[:], hot[:].rearrange("p k t x -> p (k t x)"), start=True, stop=False)
                pe.matmul(ps[:, 7, :], ones[0:2 * NT, :], before[:].rearrange("p k x -> p (k x)"), start=False, stop=True).then_inc(pos_done, 1)
        jobs(pe, body)
        down(JS + E - 1, None, E - 1, FC - 1)

    @block.vector
    def _(dve):
        dve.wait_ge(consts_ready, 2)
        dve.tensor_copy(cst[:], iot[:]).then_inc(cst_done, 1)
        for g in range(NG):
            b = g % 2
            dve.wait_ge(back_done, g + 1)
            for t in range(GT):
                ins = dve.bn_stats(stats[:, b, t, :], ps[:, b * 2 + t // 2, (t % 2) * D:(t % 2 + 1) * D])
            ins.then_inc(norm_steps, 1)
            dve.wait_ge(norm_steps, 3 * g + 1)
            for t in range(GT):
                ins = dve.bn_aggr(mv[:, b, t, :], stats[:, b, t, :])
            ins.then_inc(norm_steps, 1)
            dve.wait_ge(norm_steps, 3 * g + 2)
            dve.tensor_scalar(var_eps[:, b], mv[:, b, :, 1], 1.0 + EPS, EPS * EPS, ALU.mult, ALU.add).then_inc(ve_done, 1)
            if g >= 2:
                dve.wait_ge(ht_sent[b], 16 * (g // 2))
            dve.tensor_copy(ht[:, b], ps[:, b * 2:b * 2 + 2, :].rearrange("p a (t d) -> p (a t) d", d=D)).then_inc(ht_ready, 1)
            dve.wait_ge(std_done, g + 1)
            dve.reciprocal(rstd[:, b], std[:, b]).then_inc(norm_steps, 1)
            dve.wait_ge(norm_steps, 3 * g + 3)
            if g >= 2:
                dve.wait_ge(rec_ready, g - 1)
            dve.scalar_tensor_tensor(out=nmr[:, b], in0=mv[:, b, :, 0], scalar=-1.0, in1=rstd[:, b],
                                     op0=ALU.mult, op1=ALU.mult).then_inc(nmr_done, 1)

        def split_block(g, b):
            xs = x32[:, :, bass.ds(g * G, G)]
            if isinstance(g, int):
                dve.wait_ge(feat_ready, g + 1)
            dve.tensor_copy(f_hi[:, b, :, 0:G], xs).then_inc(f_hi_done, 1)
            dve.wait_ge(f_hi_done, g + 1)
            dve.tensor_tensor(f_lo[:, b, :, 0:G], xs, f_hi[:, b, :, 0:G].bitcast(F32), ALU.subtract).then_inc(f_ready, 1)

        def split_expert(e):
            par = e % 2
            dve.wait_ge(f32_ready, e * 3 + 3)
            hi, lo = (f[:, bass.ds(par, 1), :, 0:CAP].rearrange("p a c n -> p (a c) n") for f in (f_hi, f_lo))
            dve.tensor_copy(hi, f32[:, :, 0:CAP]).then_inc(f_hi_done, 1)
            dve.wait_ge(f_hi_done, e + (JS + 1))
            dve.tensor_tensor(lo, f32[:, :, 0:CAP], hi.bitcast(F32), ALU.subtract).then_inc(f_ready, 1)

        steps = [0]

        def step(ins):
            steps[0] += 1
            ins.then_inc(route, 1)
            dve.wait_ge(route, steps[0])

        def by_expert(x):
            return cst[:, x, :].unsqueeze(1).to_broadcast([P, NT, ES])

        def wide(x):
            return x.unsqueeze(2).to_broadcast([P, NT, ES])

        def choices():
            dve.memset(lg[:, :, E:ES], NEG)
            step(dve.tensor_copy(lg[:, :, 0:E], ps[:, 6, 0:NT * ES].rearrange("p (t x) -> p t x", x=ES)[:, :, 0:E]))
            for k in range(2):
                step(dve.tensor_reduce(top[:, k, :], lg[:], AX.X, ALU.max))
                step(dve.tensor_tensor(eq[:], lg[:], wide(top[:, k, :]), ALU.is_equal))
                step(dve.tensor_tensor(eq[:], eq[:], by_expert(0), ALU.mult))
                step(dve.tensor_reduce(which[:, k, :], eq[:], AX.X, ALU.max))
                step(dve.tensor_tensor(hot[:, k], by_expert(0), wide(which[:, k, :]), ALU.is_equal))
                if k == 0:
                    step(dve.scalar_tensor_tensor(out=lg[:], in0=hot[:, 0], scalar=NEG, in1=lg[:], op0=ALU.mult, op1=ALU.add))
            dve.tensor_tensor(small[:, 0, :], top[:, 1, :], top[:, 0, :], ALU.subtract).then_inc(gap_ready, 1)
            step(dve.tensor_scalar(rec[:, :, D + 2], which[:, 0, :], -1.0, float(ES), ALU.mult, ALU.add))
            dve.memset(tot[:], 0.0).then_inc(hot_ready, 1)
            dve.wait_ge(gate_exp_done, 1)
            step(dve.tensor_scalar(small[:, 2, :], small[:, 1, :], 1.0, None, ALU.add))
            step(dve.reciprocal(small[:, 3, :], small[:, 2, :]))
            dve.tensor_copy(rec[:, :, D + 1], small[:, 3, :])
            step(dve.tensor_tensor(rec[:, :, D + 3], small[:, 1, :], small[:, 3, :], ALU.mult))

        def places():
            dve.wait_ge(tot_done, 1)
            step(dve.tensor_copy(tot[0:2 * NT, :], ps[0:2 * NT, 7, 0:ES]))
            n = 2 * NT
            dve.tensor_tensor(before[:], tot[0:n, :].unsqueeze(1).to_broadcast([n, n, ES]),
                              below[0:n, 0:n].unsqueeze(2).to_broadcast([n, n, ES]), ALU.mult).then_inc(before_ready, 1)
            dve.wait_ge(pos_done, 1)
            hots = hot[:].rearrange("p k t x -> p (k t) x")
            caps = cst[:, 1, :].unsqueeze(1).to_broadcast([P, n, ES])
            step(dve.tensor_tensor(at_pos[:], ps[:, 7, :].rearrange("p (k x) -> p k x", x=ES), hots, ALU.mult))
            step(dve.tensor_reduce(place[:, 0, :], at_pos[:], AX.X, ALU.add))
            step(dve.tensor_tensor(at_pos[:], hots, caps, ALU.mult))
            dve.tensor_scalar(place[:, 2, :], place[:, 0, :], float(CAP), SKIP, ALU.is_ge, ALU.mult)
            step(dve.tensor_reduce(place[:, 1, :], at_pos[:], AX.X, ALU.add))
            step(dve.tensor_tensor(place[:, 3, :], place[:, 0, :], place[:, 1, :], ALU.add))
            step(dve.tensor_tensor(place[:, 3, :], place[:, 3, :], place[:, 2, :], ALU.add))
            dve.tensor_copy(place_u[:], place[:, 3, :]).then_inc(place_ready, 1)

        split_block(0, 0)
        dve.wait_ge(logits_done, NG)
        dve.wait_ge(cst_done, 1)
        choices()

        dve.memset(gate_next[:], 0.0).then_inc(gate_ready, 1)

        def gates(e):
            dve.wait_ge(xr_loaded, e * 32 + 32)
            dve.wait_ge(gate_ready, e + 1)
            dve.tensor_copy(tok_next[:], xr[:].bitcast(I32)[:, :, D]).then_inc(tok_done, 1)
            first, eid, second = (xr[:, :, D + 1 + n] for n in range(3))
            dve.tensor_scalar(gtmp[:, 0, :], eid, cst[:, 2, bass.ds(e, 1)], None, ALU.is_equal)
            dve.tensor_tensor(gtmp[:, 1, :], first, second, ALU.subtract).then_inc(gate_steps, 1)
            dve.wait_ge(gate_steps, e * 3 + 1)
            dve.tensor_tensor(gtmp[:, 0, :], gtmp[:, 0, :], gtmp[:, 1, :], ALU.mult).then_inc(gate_steps, 1)
            dve.wait_ge(gate_steps, e * 3 + 2)
            dve.tensor_tensor(gate_next[:], gtmp[:, 0, :], second, ALU.add).then_inc(gate_steps, 1)

        def pass_gates(e):
            dve.wait_ge(y_sent, 16 * JS + (16 * ET) * e)
            dve.wait_ge(tok_done, e + 1)
            dve.wait_ge(gate_steps, e * 3 + 3)
            dve.tensor_copy(tok[:], tok_next[:])
            dve.tensor_copy(gate[:], gate_next[:]).then_inc(gate_ready, 1)

        def body(j, b, e, last):
            for m in range(FC):
                k = j * FC + m
                if not (is_first(j) and m == 0):
                    dve.wait_ge(g_hi_ready, k)
                    dve.wait_ge(g_lo_ready, k)
                if e is None:
                    dve.wait_ge(silu_done, part(j, e, m + 1))
                    dve.tensor_tensor(g32[:, 0:G], s32[:, m % 2, :], ps[:, (m % 2) * 2 + 1, :], ALU.mult).then_inc(prod_done, 1)
                    n = G
                else:
                    for h in range(2):
                        dve.wait_ge(silu_done, part(j, e, m, h + 1))
                        dve.tensor_tensor(g32[:, h * HALF:(h + 1) * HALF], s32[:, h, 0:HALF], ps[:, 2 * h + 1, 0:HALF], ALU.mult).then_inc(prod_done, 1)
                    n = CAP
                dve.wait_ge(g_hi_ready, k + 1)
                dve.tensor_tensor(g_lo[:, m % 2, 0:n], g32[:, 0:n], g_hi[:, m % 2, 0:n].bitcast(F32), ALU.subtract).then_inc(g_lo_ready, 1)
                if m == 6 and has_next(j, e):
                    split_expert(0 if e is None else e + 1)
                if m == 1:
                    if e is not None:
                        gates(e)
                    elif not is_last_shared(j):
                        split_block(j + 1, 1 - b)
                if m == 5 and e is not None:
                    pass_gates(e)
            if is_first(j):
                places()
        jobs(dve, body)


def program(nc, io, acc):
    rows_for = nc.dram_tensor("rows_for", (E * CAP, REC), F32, kind="Internal").ap()
    with ExitStack() as ctx:
        x32 = ctx.enter_context(nc.sbuf_tensor("x32", [P, DC, N_TOK], F32))
        with ExitStack() as stage:
            tower(nc, stage, io, x32, rows_for, acc)
        with ExitStack() as stage:
            attention(nc, stage, io, x32)
        with ExitStack() as stage:
            experts(nc, stage, io, x32, rows_for, acc)


def expert_weights(a):
    import numpy as np

    def up(w):
        return w.reshape(DC, P, FC, P).transpose(2, 1, 0, 3).reshape(FC, P, D)

    parts = []
    for e in range(-1, E):
        w1, w3, w2 = (a("L0_ffn_" + n + "s") if e < 0 else a("L0_ffn_" + n)[e] for n in ("W1", "W3", "W2"))
        parts.append(np.concatenate([up(w1), up(w3), w2.reshape(FC, P, D)], 2))
    return np.concatenate(parts)


def attention_weights(a, rows):
    import numpy as np

    wq, wkv, wo = a("L0_attn_w_q"), a("L0_attn_w_kv"), a("L0_attn_w_out")
    h = HEADS * DH
    parts = []
    for p in range(PAIRS):
        at = p * P
        parts.append(np.stack([rows(wq[:, at:at + P], DC), rows(wkv[:, at:at + P], DC),
                               rows(wkv[:, h + at:h + at + P], DC), wo[at:at + P]], 1))
    return np.stack(parts)


def layout(i):
    import numpy as np

    def a(name):
        return np.asarray(i[name])

    def rows(w, chunks):
        return w.reshape(chunks, P, -1).transpose(1, 0, 2).reshape(P, -1)

    def cols(v):
        return np.moveaxis(v.reshape(v.shape[:-1] + (-1, P)), -1, 0)

    wqo, wf = [], []
    for l in range(LAYERS):
        wqo.append(np.stack([rows(a("L0_tok_Wq")[l].reshape(D, D), DC), rows(a("L0_tok_Wo")[l].T, DC)], 1))
        w1 = rows(a("L0_tok_ff_w1")[l].T, DC).reshape(P, NG, G // 2)
        w2 = rows(a("L0_tok_ff_w2")[l].T, FC).reshape(P, NG, G // 2)
        wf.append(np.concatenate([w1, w2], 2).transpose(1, 0, 2))
    return {
        "ids": np.ascontiguousarray(a("x").reshape(-1, P).T),
        "emb": a("L0_tok_emb_table"),
        "wqo": np.ascontiguousarray(np.stack(wqo)),
        "wf": np.ascontiguousarray(np.concatenate(wf)),
        "vec": np.ascontiguousarray(np.concatenate([cols(a("L0_tok_" + n)) for n in ("ln1_w", "ln1_b", "ln2_w", "ln2_b", "ff_b2")], 2)),
        "wa": np.ascontiguousarray(attention_weights(a, rows)),
        "b_out": np.ascontiguousarray(cols(a("L0_attn_b_out"))),
        "sort_w": np.ascontiguousarray(a("L0_attn_sort_w")[0].reshape(SORT_PAIRS, 2, 2, DH, NB)
                                       .transpose(0, 1, 3, 2, 4).reshape(SORT_PAIRS, P, 2, NB)),
        "ffn_g": np.ascontiguousarray(cols(a("L0_ffn_ln_g"))),
        "ffn_b": np.ascontiguousarray(cols(a("L0_ffn_ln_b"))),
        "w_r": np.ascontiguousarray(a("L0_ffn_Wr").reshape(DC, P, E).transpose(1, 0, 2)),
        "we": np.ascontiguousarray(expert_weights(a)),
        "b1": np.ascontiguousarray(cols(a("L0_tok_ff_b1"))),
    }


def kernel(**inputs):
    import numpy as np
    import concourse.bacc as bacc
    from concourse.bass_utils import run_bass_kernel_spmd

    arrays = {"in_" + name: v for name, v in layout(inputs).items()}
    nc = bacc.Bacc("TRN2", target_bir_lowering=False, num_devices=1)
    io = {name[3:]: nc.dram_tensor(name, v.shape, mybir.dt.from_np(v.dtype), kind="ExternalInput").ap()
          for name, v in arrays.items()}
    acc = nc.dram_tensor("out", (N_TOK + P, D), F32, kind="ExternalOutput").ap()
    program(nc, io, acc)
    got = run_bass_kernel_spmd(nc, [arrays], core_ids=[0]).results[0]["out"]
    return got[:N_TOK].reshape(2, N_TOK // 2, D)
```

```python
from contextlib import ExitStack

import concourse.bass as bass
from concourse import mybir

F32 = mybir.dt.float32
F32R = mybir.dt.float32r
I32 = mybir.dt.int32
U32 = mybir.dt.uint32
ALU = mybir.AluOpType
ACT = mybir.ActivationFunctionType
AX = mybir.AxisListType

P = 128
D = 256
DC = D // P
N_TOK = 4096
G = 512
NG = N_TOK // G
GT = G // P
F = 1024
FC = F // P
LAYERS = 6
VOCAB = 8000
EPS = 1e-5


def held(eng, value):
    if not isinstance(value, int):
        value = eng.snap(value)
        eng.compute_val(value)
    return value


def tower(nc, ctx, io, x32, rows_for, acc):
    def sb(name, shape, dt=F32):
        return ctx.enter_context(nc.sbuf_tensor(name, shape, dt))

    def sem(name):
        return ctx.enter_context(nc.semaphore(name))

    w_hi = [sb(f"t_w_hi{i}", [P, NG, G], F32R) for i in range(2)]
    w_lo = [sb(f"t_w_lo{i}", [P, NG, G], F32R) for i in range(2)]
    w_stage = sb("t_w_stage", [P, 2, G])
    mix = sb("t_mix", [P, LAYERS, DC * D])
    mix_hi = sb("t_mix_hi", [P, DC, D], F32R)
    mix_lo = sb("t_mix_lo", [P, DC, D], F32R)
    x_hi = sb("t_x_hi", [P, DC, G], F32R)
    x_lo = sb("t_x_lo", [P, DC, G], F32R)
    a32 = sb("t_a32", [P, 2, DC, G])
    a_hi = sb("t_a_hi", [P, 2, DC, G], F32R)
    a_lo = sb("t_a_lo", [P, 2, DC, G], F32R)
    h32 = sb("t_h32", [P, 2, G])
    h_hi = sb("t_h_hi", [P, FC, G], F32R)
    h_lo = sb("t_h_lo", [P, FC, G], F32R)
    u2 = sb("t_u2", [P, DC, G])
    xn = [sb(f"t_xn{i}", [P, GT, D]) for i in (1, 2)]
    vec = sb("t_vec", [P, LAYERS, 5 * DC])
    b1 = sb("t_b1", [P, LAYERS, FC])
    ids = sb("t_ids", [P, N_TOK // P], I32)
    idf = sb("t_idf", [P, 3, N_TOK // P])
    idu = sb("t_idu", [P, N_TOK // P], U32)
    eye = sb("t_eye", [P, DC, D])
    stats = [sb(f"t_stats{i}", [P, GT, 6]) for i in (1, 2)]
    mv = [sb(f"t_mv{i}", [P, GT, 2]) for i in (1, 2)]
    var_eps = [sb(f"t_ve{i}", [P, GT]) for i in (1, 2)]
    std = [sb(f"t_std{i}", [P, GT]) for i in (1, 2)]
    rstd = [sb(f"t_rstd{i}", [P, GT]) for i in (1, 2)]
    nmr = [sb(f"t_nmr{i}", [P, GT]) for i in (1, 2)]
    fill = sb("t_fill", [P, REC])

    ps_tok = ctx.enter_context(nc.psum_tensor("t_ps_tok", [P, GT, D], F32))
    ps_feat = ctx.enter_context(nc.psum_tensor("t_ps_feat", [P, DC, G], F32))
    ps_h = ctx.enter_context(nc.psum_tensor("t_ps_h", [P, 2, G], F32))
    ps_y = ctx.enter_context(nc.psum_tensor("t_ps_y", [P, DC, G], F32))

    vec_loaded = sem("t_vec_loaded")
    ids_loaded = sem("t_ids_loaded")
    qo_loaded = [sem(f"t_qo_loaded{i}") for i in range(2)]
    stage_loaded = [sem(f"t_stage_loaded{i}") for i in range(2)]
    ids_ready = sem("t_ids_ready")
    ids_steps = sem("t_ids_steps")
    x_hi_done = sem("t_x_hi_done")
    rows_loaded = [sem(f"t_rows_loaded{i}") for i in range(2)]
    eye_ready = sem("t_eye_ready")
    rows_turned = sem("t_rows_turned")
    x_ready = sem("t_x_ready")
    mix_done = sem("t_mix_done")
    mix_ready = sem("t_mix_ready")
    w_split = sem("t_w_split")
    x_split = sem("t_x_split")
    z_done = sem("t_z_done")
    ff1_done = sem("t_ff1_done")
    ff2_done = sem("t_ff2_done")
    fwd_done = [sem(f"t_fwd_done{i}") for i in (1, 2)]
    back_done = sem("t_back_done")
    u2_ready = sem("t_u2_ready")
    stats_done = [sem(f"t_stats_done{i}") for i in (1, 2)]
    mv_done = [sem(f"t_mv_done{i}") for i in (1, 2)]
    ve_done = [sem(f"t_ve_done{i}") for i in (1, 2)]
    std_done = [sem(f"t_std_done{i}") for i in (1, 2)]
    rstd_done = [sem(f"t_rstd_done{i}") for i in (1, 2)]
    nmr_done = [sem(f"t_nmr_done{i}") for i in (1, 2)]
    xn_ready = [sem(f"t_xn_ready{i}") for i in (1, 2)]
    a32_ready = sem("t_a32_ready")
    a_hi_done = sem("t_a_hi_done")
    a_split = sem("t_a_split")
    h_hi_ready = sem("t_h_hi_ready")
    h_lo_ready = sem("t_h_lo_ready")
    hi_written = sem("t_hi_written")
    fill_ready = sem("t_fill_ready")
    filled = sem("t_filled")

    SLOTS = LAYERS * NG
    LN1_W, LN1_B, LN2_W, LN2_B, FF_B2 = (DC * i for i in range(5))

    def slots(eng, body):
        for b in range(2):
            body(b, 0, b, 0)
        with eng.Fori(1, NG // 2) as j:
            for b in range(2):
                body(j * 2 + b, 0, b, 0)
        with eng.Fori(0, NG // 2) as j:
            for b in range(2):
                body(j * 2 + (NG + b), 1, b, 1)
        with eng.Fori(1, LAYERS // 2) as pair:
            for par in range(2):
                with eng.Fori(0, NG // 2) as j:
                    for b in range(2):
                        body(pair * (2 * NG) + j * 2 + (par * NG + b), pair * 2 + par, b, par)

    def w1(w, par, kc, m):
        at = kc * F + m * P
        return w[par][:, at // (G // 2), at % (G // 2):at % (G // 2) + P]

    def w2(w, par, k, oc):
        return w[par][:, k, G // 2 + oc * P:G // 2 + (oc + 1) * P]

    block = ctx.enter_context(nc.Block())

    @block.sync
    def _(sp):
        sp.dma_start(ids[:], io["ids"]).then_inc(ids_loaded, 16)
        sp.dma_start(vec[:], io["vec"]).then_inc(vec_loaded, 16)
        sp.dma_start(b1[:], io["b1"]).then_inc(vec_loaded, 16)
        for g in range(NG):
            if g < LAYERS:
                if g >= 2:
                    sp.wait_ge(mix_done, g - 1)
                sp.dma_start(a32[:, g % 2, :, :], io["wqo"][g]).then_inc(qo_loaded[g % 2], 16)
            if g >= 2:
                sp.wait_ge(w_split, g - 1)
            sp.dma_start(w_stage[:, g % 2, :], io["wf"][g]).then_inc(stage_loaded[g % 2], 16)
        with sp.Fori(0, SLOTS // 2) as i:
            for b in range(2):
                sp.wait_ge(w_split, i * 2 + (NG + b - 1))
                sp.dma_start(w_stage[:, b, :], io["wf"][(i * 2 + (NG + b)) % SLOTS]).then_inc(stage_loaded[b], 16)

    @block.gpsimd
    def _(pool):
        pool.memset(eye[:], 0.0).then_inc(eye_ready, 1)
        pool.wait_ge(eye_ready, 1)
        pool.affine_select(out=eye[:], in_=eye[:], compare_op=ALU.not_equal, fill=1.0, base=0,
                           pattern=[[-P, DC], [1, D]], channel_multiplier=-1).then_inc(eye_ready, 1)
        pool.memset(fill[:], 0.0).then_inc(fill_ready, 1)
        pool.wait_ge(fill_ready, 1)
        pool.iota(fill[:].bitcast(I32)[:, D:D + 1], pattern=[[0, 1]], base=N_TOK, channel_multiplier=1).then_inc(fill_ready, 1)
        pool.wait_ge(ids_ready, 1)
        for g in range(NG):
            if g >= 2:
                pool.wait_ge(rows_turned, g - 1)
            for t in range(GT):
                pool.indirect_dma_start(out=xn[g % 2][:, t, :], out_offset=None, in_=io["emb"],
                                        in_offset=bass.IndirectOffsetOnAxis(ap=idu[:, g * GT + t:g * GT + t + 1], axis=0),
                                        ).then_inc(rows_loaded[g % 2], 16)

    @block.scalar
    def _(act):
        act.wait_ge(vec_loaded, 32)
        for g in range(NG):
            act.wait_ge(rows_turned, g + 1)
            act.activation(x32[:, :, g * G:(g + 1) * G], ps_feat[:], ACT.Copy).then_inc(x_ready, 1)

        def root(n, k):
            act.wait_ge(ve_done[n], k + 1)
            act.activation(std[n][:], var_eps[n][:], ACT.Sqrt).then_inc(std_done[n], 1)

        def normalise(n, k, first, last):
            if first == 0:
                act.wait_ge(nmr_done[n], k + 1)
                if not (isinstance(k, int) and k == 0):
                    act.wait_ge(fwd_done[n], k)
                elif n == 0:
                    act.wait_ge(rows_turned, NG)
            for t in range(first, last):
                ins = act.activation(xn[n][:, t, :], ps_tok[:, t, :], ACT.Identity,
                                     scale=rstd[n][:, t:t + 1], bias=nmr[n][:, t:t + 1])
            if last == GT:
                ins.then_inc(xn_ready[n], 1)

        def scale_first(k, l, b):
            act.wait_ge(fwd_done[0], k + 1)
            if not (isinstance(k, int) and k < 2):
                act.wait_ge(u2_ready, k - 1)
            for c in range(DC):
                ins = act.activation(a32[:, b, c, :], ps_feat[:, c, :], ACT.Identity,
                                     scale=vec[:, l, LN1_W + c:LN1_W + c + 1],
                                     bias=vec[:, l, LN1_B + c:LN1_B + c + 1])
            ins.then_inc(a32_ready, 1)

        def scale_second(k, l):
            count = held(act, k + 1)
            act.wait_ge(vec_loaded, 32)
            act.wait_ge(fwd_done[1], count)
            g = k % NG
            for c in range(DC):
                ins = act.activation(x32[:, c, bass.ds(g * G, G)], ps_feat[:, c, :], ACT.Identity,
                                     scale=vec[:, l, LN2_W + c:LN2_W + c + 1],
                                     bias=vec[:, l, LN2_B + c:LN2_B + c + 1])
            ins.then_inc(x_ready, 1)

        def hidden(s, l, m):
            before = m >= 2 or not (isinstance(s, int) and s == 0)
            count = held(act, s * FC + (m + 1))
            free = held(act, s * FC + (m - 1)) if before else 0
            act.wait_ge(vec_loaded, 32)
            act.wait_ge(ff1_done, count)
            if before:
                act.wait_ge(h_lo_ready, free)
            act.activation(h32[:, m % 2, :], ps_h[:, m % 2, :], ACT.Relu, bias=b1[:, l, m:m + 1])
            act.activation(h_hi[:, m, :], ps_h[:, m % 2, :], ACT.Relu, bias=b1[:, l, m:m + 1]).then_inc(h_hi_ready, 1)

        root(0, 0)
        normalise(0, 0, 0, GT)
        act.wait_ge(mix_ready, LAYERS)
        scale_first(0, 0, 0)
        act.wait_ge(fill_ready, 2)
        act.dma_start(acc[N_TOK:, :], fill[:, 0:D]).then_inc(filled, 16)
        by_row = rows_for.rearrange("(e r) c -> r e c", e=E)
        for t in range(ET):
            n = P if t < ET - 1 else LAST_ROWS
            act.dma_start(by_row[t * P:t * P + n], fill[0:n, :].unsqueeze(1).to_broadcast([n, E, REC])).then_inc(filled, 16)

        def body(s, l, b, par):
            two = not (isinstance(s, int) and s == 0)
            l_next, l_prev = ((s + 1) // NG) % LAYERS, (s - 1) // NG
            hidden(s, l, 0)
            hidden(s, l, 1)
            root(0, s + 1)
            hidden(s, l, 2)
            normalise(0, s + 1, 0, GT)
            hidden(s, l, 3)
            scale_first(s + 1, l_next, 1 - b)
            hidden(s, l, 4)
            hidden(s, l, 5)
            hidden(s, l, 6)
            if two:
                root(1, s - 1)
                normalise(1, s - 1, 0, GT)
            hidden(s, l, 7)
            if two:
                scale_second(s - 1, l_prev)
        slots(act, body)
        root(1, SLOTS - 1)
        normalise(1, SLOTS - 1, 0, GT)
        scale_second(SLOTS - 1, LAYERS - 1)
        act.wait_ge(filled, 16 * (1 + ET))

    @block.tensor
    def _(pe):
        pe.wait_ge(eye_ready, 2)
        ident_ap = eye[:, 0, 0:P]
        for g in range(NG):
            pe.wait_ge(rows_loaded[g % 2], 16 * GT * (g // 2 + 1))
            if g >= 1:
                pe.wait_ge(x_ready, g)
            for t in range(GT):
                for c in range(DC):
                    tr = pe.transpose(ps_feat[:, c, t * P:(t + 1) * P], xn[g % 2][:, t, c * P:(c + 1) * P], ident_ap)
            tr.then_inc(rows_turned, 1)
            if g >= LAYERS:
                continue
            pe.wait_ge(qo_loaded[g % 2], 16 * (g // 2 + 1))
            if g >= 2:
                pe.wait_ge(mix_ready, g - 1)
            for kc in range(DC):
                for hc in range(DC):
                    mm = pe.matmul(ps_h[:, g % 2, kc * D:(kc + 1) * D], a32[:, g % 2, 0, hc * D + kc * P:hc * D + (kc + 1) * P],
                                   a32[:, g % 2, 1, hc * D:(hc + 1) * D], start=(hc == 0), stop=(hc == DC - 1))
            mm.then_inc(mix_done, 1)

        def passes(out, lhs, rhs, start, stop):
            pe.matmul(out, lhs[0], rhs[0], start=start, stop=False)
            pe.matmul(out, lhs[0], rhs[1], start=False, stop=False)
            return pe.matmul(out, lhs[1], rhs[0], start=False, stop=stop)

        def mixing(k):
            pe.wait_ge(x_split, k + 1)
            if isinstance(k, int) and k < 3:
                if k >= 1:
                    pe.wait_ge(xn_ready[0], k)
            else:
                pe.wait_ge(xn_ready[1], k - 2)
            for t in range(GT):
                for kc in range(DC):
                    tok = slice(t * P, (t + 1) * P)
                    mm = passes(ps_tok[:, t, :], (x_hi[:, kc, tok], x_lo[:, kc, tok]),
                                (mix_hi[:, kc, :], mix_lo[:, kc, :]), kc == 0, kc == DC - 1)
            mm.then_inc(z_done, 1)

        def forward(n, k):
            pe.wait_ge(xn_ready[n], k + 1)
            for c in range(DC):
                for t in range(GT):
                    tr = pe.transpose(ps_feat[:, c, t * P:(t + 1) * P], xn[n][:, t, c * P:(c + 1) * P], ident_ap)
            tr.then_inc(fwd_done[n], 1)

        def back(k):
            pe.wait_ge(u2_ready, k + 1)
            pe.wait_ge(xn_ready[0], k + 3)
            for t in range(GT):
                for c in range(DC):
                    tr = pe.transpose(ps_tok[:, t, c * P:(c + 1) * P], u2[:, c, t * P:(t + 1) * P], ident_ap)
            tr.then_inc(back_done, 1)

        def up(s, b, par, m):
            if m == 0:
                pe.wait_ge(a_split, s + 1)
            if not (isinstance(s, int) and s == 0 and m < 2):
                pe.wait_ge(h_hi_ready, s * FC + (m - 1))
            for kc in range(DC):
                mm = passes(ps_h[:, m % 2, :], (w1(w_hi, par, kc, m), w1(w_lo, par, kc, m)),
                            (a_hi[:, b, kc, :], a_lo[:, b, kc, :]), kc == 0, kc == DC - 1)
            mm.then_inc(ff1_done, 1)

        def down(s, par, k):
            if k == 0 and not (isinstance(s, int) and s == 0):
                pe.wait_ge(u2_ready, s)
            pe.wait_ge(h_hi_ready, s * FC + (k + 1))
            pe.wait_ge(h_lo_ready, s * FC + (k + 1))
            for oc in range(DC):
                mm = passes(ps_y[:, oc, :], (w2(w_hi, par, k, oc), w2(w_lo, par, k, oc)),
                            (h_hi[:, k, :], h_lo[:, k, :]), k == 0, k == FC - 1)
            if k == FC - 1:
                mm.then_inc(ff2_done, 1)

        pe.wait_ge(mix_ready, LAYERS)
        mixing(0)
        pe.wait_ge(x_ready, NG)
        forward(0, 0)

        def body(s, l, b, par):
            two = not (isinstance(s, int) and s == 0)
            mixing(s + 1)
            pe.wait_ge(w_split, l * NG + NG)
            up(s, b, par, 0)
            up(s, b, par, 1)
            for m in range(2, FC):
                up(s, b, par, m)
                down(s, par, m - 2)
                if m == 3:
                    if isinstance(s, int) and s < 2:
                        pe.wait_ge(a32_ready, s + 1)
                    else:
                        pe.wait_ge(x_ready, s + (NG - 1))
                    forward(0, s + 1)
                if m == 5 and two:
                    back(s - 1)
            down(s, par, FC - 2)
            if two:
                pe.wait_ge(a32_ready, s + 2)
                forward(1, s - 1)
            down(s, par, FC - 1)
        slots(pe, body)
        pe.wait_ge(u2_ready, SLOTS)
        pe.wait_ge(xn_ready[0], SLOTS + 1)
        back_last = SLOTS - 1
        for t in range(GT):
            for c in range(DC):
                tr = pe.transpose(ps_tok[:, t, c * P:(c + 1) * P], u2[:, c, t * P:(t + 1) * P], ident_ap)
        tr.then_inc(back_done, 1)
        pe.wait_ge(x_ready, NG + SLOTS - 1)
        forward(1, back_last)

    @block.vector
    def _(dve):
        dve.wait_ge(ids_loaded, 16)
        dve.tensor_copy(idf[:, 0, :], ids[:]).then_inc(ids_steps, 1)
        dve.wait_ge(ids_steps, 1)
        dve.tensor_scalar(idf[:, 1, :], idf[:, 0, :], 0.0, float(VOCAB), ALU.is_lt, ALU.mult).then_inc(ids_steps, 1)
        dve.wait_ge(ids_steps, 2)
        dve.tensor_tensor(idf[:, 2, :], idf[:, 0, :], idf[:, 1, :], ALU.add).then_inc(ids_steps, 1)
        dve.wait_ge(ids_steps, 3)
        dve.tensor_scalar(idf[:, 0, :], idf[:, 2, :], 0.0, float(VOCAB - 1), ALU.max, ALU.min).then_inc(ids_steps, 1)
        dve.wait_ge(ids_steps, 4)
        dve.tensor_copy(idu[:], idf[:, 0, :]).then_inc(ids_ready, 1)

        def split_weights(n, par, b, g):
            dve.wait_ge(stage_loaded[b], (n // 2) * 16 + 16)
            dve.tensor_copy(w_hi[par][:, g, :], w_stage[:, b, :]).then_inc(hi_written, 1)
            return w_hi[par][:, g, :], w_lo[par][:, g, :], w_stage[:, b, :]

        dve.wait_ge(eye_ready, 2)
        for g in range(NG):
            hi, lo, raw = split_weights(g, 0, g % 2, g)
            dve.wait_ge(hi_written, g + 1)
            dve.tensor_tensor(lo, raw, hi.bitcast(F32), ALU.subtract).then_inc(w_split, 1)
            if g < LAYERS:
                dve.wait_ge(mix_done, g + 1)
                dve.tensor_tensor(mix[:, g, :], ps_h[:, g % 2, :], eye[:].rearrange("p a b -> p (a b)"), ALU.add).then_inc(mix_ready, 1)

        def split_x(k):
            dve.wait_ge(x_ready, k + 1)
            g, l = k % NG, (k // NG) % LAYERS
            for c in range(DC):
                dve.tensor_copy(x_hi[:, c, :], x32[:, c, bass.ds(g * G, G)])
            dve.tensor_copy(mix_hi[:].rearrange("p a b -> p (a b)"), mix[:, l, :]).then_inc(x_hi_done, 1)
            dve.wait_ge(x_hi_done, k + 1)
            for c in range(DC):
                dve.tensor_tensor(x_lo[:, c, :], x32[:, c, bass.ds(g * G, G)], x_hi[:, c, :].bitcast(F32), ALU.subtract)
            dve.tensor_tensor(mix_lo[:].rearrange("p a b -> p (a b)"), mix[:, l, :],
                              mix_hi[:].rearrange("p a b -> p (a b)").bitcast(F32), ALU.subtract).then_inc(x_split, 1)

        def statistics(n, k):
            if n == 0:
                dve.wait_ge(z_done, k + 1)
            else:
                dve.wait_ge(back_done, k + 1)
            for t in range(GT):
                ins = dve.bn_stats(stats[n][:, t, :], ps_tok[:, t, :])
            ins.then_inc(stats_done[n], 1)
            count = held(dve, k + 1)
            dve.wait_ge(eye_ready, 2)
            dve.wait_ge(stats_done[n], count)
            for t in range(GT):
                ins = dve.bn_aggr(mv[n][:, t, :], stats[n][:, t, :])
            ins.then_inc(mv_done[n], 1)
            dve.wait_ge(mv_done[n], k + 1)
            dve.tensor_scalar(var_eps[n][:], mv[n][:, :, 1], EPS, None, ALU.add).then_inc(ve_done[n], 1)

        def reciprocal(n, k):
            dve.wait_ge(std_done[n], k + 1)
            dve.reciprocal(rstd[n][:], std[n][:]).then_inc(rstd_done[n], 1)
            dve.wait_ge(rstd_done[n], k + 1)
            dve.scalar_tensor_tensor(out=nmr[n][:], in0=mv[n][:, :, 0], scalar=-1.0, in1=rstd[n][:],
                                     op0=ALU.mult, op1=ALU.mult).then_inc(nmr_done[n], 1)

        def split_a(k, b):
            dve.wait_ge(a32_ready, k + 1)
            dve.tensor_copy(a_hi[:, b], a32[:, b]).then_inc(a_hi_done, 1)
            dve.wait_ge(a_hi_done, k + 1)
            dve.tensor_tensor(a_lo[:, b], a32[:, b], a_hi[:, b].bitcast(F32), ALU.subtract).then_inc(a_split, 1)

        def residual(k, b, l):
            dve.wait_ge(ff2_done, k + 1)
            if not (isinstance(k, int) and k == 0):
                dve.wait_ge(back_done, k)
            for c in range(DC):
                ins = dve.scalar_tensor_tensor(out=u2[:, c, :], in0=ps_y[:, c, :], scalar=vec[:, l, FF_B2 + c:FF_B2 + c + 1],
                                               in1=a32[:, b, c, :], op0=ALU.add, op1=ALU.add)
            ins.then_inc(u2_ready, 1)

        def low_hidden(s, m):
            dve.wait_ge(h_hi_ready, s * FC + (m + 1))
            dve.tensor_tensor(h_lo[:, m, :], h32[:, m % 2, :], h_hi[:, m, :].bitcast(F32), ALU.subtract).then_inc(h_lo_ready, 1)

        split_x(0)
        statistics(0, 0)
        reciprocal(0, 0)
        split_x(1)
        split_a(0, 0)
        dve.wait_ge(vec_loaded, 32)

        def body(s, l, b, par):
            two = not (isinstance(s, int) and s == 0)
            if two:
                residual(s - 1, 1 - b, (s - 1) // NG)
            statistics(0, s + 1)
            low_hidden(s, 0)
            reciprocal(0, s + 1)
            low_hidden(s, 1)
            low_hidden(s, 2)
            split_x(s + 2)
            low_hidden(s, 3)
            split_a(s + 1, 1 - b)
            low_hidden(s, 4)
            low_hidden(s, 5)
            if two:
                statistics(1, s - 1)
            low_hidden(s, 6)
            if two:
                reciprocal(1, s - 1)
            piece(s, b, par)
            low_hidden(s, 7)

        def piece(s, b, par):
            g = s % NG
            n = s + NG
            dve.wait_ge(stage_loaded[b], (n // 2) * 16 + 16)
            dve.tensor_copy(w_hi[1 - par][:, g, :], w_stage[:, b, :]).then_inc(hi_written, 1)
            dve.wait_ge(hi_written, n + 1)
            dve.tensor_tensor(w_lo[1 - par][:, g, :], w_stage[:, b, :], w_hi[1 - par][:, g, :].bitcast(F32),
                              ALU.subtract).then_inc(w_split, 1)

        slots(dve, body)
        residual(SLOTS - 1, 1, LAYERS - 1)
        statistics(1, SLOTS - 1)
        reciprocal(1, SLOTS - 1)


HEADS = 16
DH = 64
PAIRS = HEADS // 2
LOCAL_PAIRS = 2
SORT_PAIRS = PAIRS - LOCAL_PAIRS
SEQ = 2048
BATCH = N_TOK // SEQ
BK = 32
NB = SEQ // BK
BT = P // BK
ST = SEQ // P
SG = SEQ // G
NEG = -3.4028234663852886e38


def attention(nc, ctx, io, x32):
    def sb(name, shape, dt=F32):
        return ctx.enter_context(nc.sbuf_tensor("a_" + name, shape, dt))

    def sem(name):
        return ctx.enter_context(nc.semaphore("a_" + name))

    y_hi = sb("y_hi", [P, DC, SEQ], F32R)
    y_lo = sb("y_lo", [P, DC, SEQ], F32R)
    w_stage = sb("w_stage", [P, 4, D])
    w_hi = sb("w_hi", [P, 3, DC, P], F32R)
    w_lo = sb("w_lo", [P, 3, DC, P], F32R)
    wo_hi = sb("wo_hi", [P, D], F32R)
    wo_lo = sb("wo_lo", [P, D], F32R)
    q_t = sb("q_t", [P, SEQ])
    keys = sb("keys", [P, 2, SEQ + 2])
    v_t = sb("v_t", [P, SEQ + 2 * BK])
    v_by_t = sb("v_by_t", [P, SEQ])
    k_bk = sb("k_bk", [P, BK // 2, P])
    v_bk = sb("v_bk", [P, BK // 2, P])
    v_tok = [sb(f"v_tok{i}", [P, ST, P]) for i in range(2)]
    scratch = sb("scratch", [P, 2, 1024])
    p_diag = sb("p_diag", [P, 2, 32, P])
    att_hi = sb("att_hi", [P, SEQ], F32R)
    att_lo = sb("att_lo", [P, SEQ], F32R)
    ident = sb("ident", [P, P])
    stats = [q_t[:, at:at + GT * 6].rearrange("p (t n) -> p t n", t=GT) for at in (0, 512)]
    mv = [q_t[:, at:at + GT * 2].rearrange("p (t n) -> p t n", t=GT) for at in (64, 576)]
    var_eps, std, rstd, nmr = ([q_t[:, at:at + GT] for at in (128 + 64 * n, 640 + 64 * n)] for n in range(4))
    b_out = sb("b_out", [P, DC])
    sort_w = sb("sort_w", [P, 2, NB])
    sums = sb("sums", [P, 2, NB])
    r_log = sb("r_log", [P, NB])
    r_two = sb("r_two", [P, 2, NB])
    r_diag = sb("r_diag", [P, 2, P])
    r_small = sb("r_small", [P, 4])
    s_small = sb("s_small", [P, 2, 16])
    mixed_t = scratch[:].rearrange("p a b -> p (a b)")
    x_static = scratch[:].rearrange("p a (c n) -> p a c n", c=DC)
    own_keys = keys[:, 0, 1:1 + SEQ]
    mixed_keys = keys[:, 1, 1:1 + SEQ]
    xn = [v_tok[i][:, 0:8, :].rearrange("p a b -> p (a b)").rearrange("p (t d) -> p t d", t=GT) for i in range(2)]
    values = {True: [v_tok[0], v_tok[1], k_bk], False: [v_tok[0], v_tok[1]]}

    ring = ctx.enter_context(nc.psum_tensor("a_ring", [P, 4, G], F32))
    quad = ctx.enter_context(nc.psum_tensor("a_quad", [P, 4, G], F32))

    ident_ready = sem("ident_ready")
    bias_loaded = sem("bias_loaded")
    pads_ready = sem("pads_ready")
    back_done = sem("back_done")
    norm_steps = sem("norm_steps")
    ve_done = sem("ve_done")
    std_done = sem("std_done")
    nmr_done = sem("nmr_done")
    xn_ready = sem("xn_ready")
    fwd_done = sem("fwd_done")
    y_hi_ready = sem("y_hi_ready")
    y_ready = sem("y_ready")
    bias_added = sem("bias_added")
    w_loaded = sem("w_loaded")
    w_hi_done = sem("w_hi_done")
    w_ready = sem("w_ready")
    wo_ready = sem("wo_ready")
    sort_loaded = sem("sort_loaded")
    proj_done = sem("proj_done")
    proj_read = sem("proj_read")
    sums_done = sem("sums_done")
    turned = {True: sem("turned_local"), False: sem("turned_sort")}
    turned_read = {True: sem("turned_read_local"), False: sem("turned_read_sort")}
    logits_done = sem("logits_done")
    logits_read = sem("logits_read")
    r_max_done = sem("r_max_done")
    r_neg_done = sem("r_neg_done")
    r_exp_done = sem("r_exp_done")
    r_inv_done = sem("r_inv_done")
    r_two_done = sem("r_two_done")
    r_turned = sem("r_turned")
    r_ready = sem("r_ready")
    mix_done = sem("mix_done")
    mix_read = [sem(f"mix_read{i}") for i in range(2)]
    kinds = {True: "local", False: "sort"}
    s_done = {k: sem("s_done_" + n) for k, n in kinds.items()}
    s_read = {k: sem("s_read_" + n) for k, n in kinds.items()}
    s_masked = sem("s_masked")
    s_max_done = {k: sem("s_max_done_" + n) for k, n in kinds.items()}
    s_sub_done = {k: sem("s_sub_done_" + n) for k, n in kinds.items()}
    s_exp_done = {k: sem("s_exp_done_" + n) for k, n in kinds.items()}
    s_sum_done = {k: sem("s_sum_done_" + n) for k, n in kinds.items()}
    s_inv_done = {k: sem("s_inv_done_" + n) for k, n in kinds.items()}
    s_norm_done = {k: sem("s_norm_done_" + n) for k, n in kinds.items()}
    p_ready = {k: sem("p_ready_" + n) for k, n in kinds.items()}
    v_by_t_ready = sem("v_by_t_ready")
    x_staged = sem("x_staged")
    pv_done = {k: sem("pv_done_" + n) for k, n in kinds.items()}
    att_hi_ready = sem("att_hi_ready")
    att_ready = sem("att_ready")
    out_done = sem("out_done")
    x_added = sem("x_added")

    UNITS = {True: 4, False: 2}
    TILES = {True: ST // 4, False: ST // 2}
    PER = {True: 12, False: 16}
    BLOCKS = {True: 3, False: 2}
    SCALE = {True: 1.0, False: DH ** -0.5}

    def pairs(eng, start, body):
        with eng.Fori(0, BATCH) as b:
            start(b)
            i, n, m = b * PAIRS, b * LOCAL_PAIRS, b * SORT_PAIRS
            body(i, n, True, (n + 1, True))
            body(i + 1, n + 1, True, (m, False))
            with eng.Fori(0, SORT_PAIRS - 1) as c:
                body(b * PAIRS + c + LOCAL_PAIRS, b * SORT_PAIRS + c, False, (b * SORT_PAIRS + c + 1, False))
            body(i + (PAIRS - 1), m + (SORT_PAIRS - 1), False, None)

    def mixed(unit, half):
        at = (unit % 2) * 16 + half * 8
        return (mixed_keys.rearrange("p (t u) -> p t u", u=NB), mixed_t.rearrange("p (u t) -> p t u", t=BK))[unit // 2][:, at:at + 8, :]

    def bank_of(c):
        return c % 4 if c < 4 else (c + 2) % 4

    block = ctx.enter_context(nc.Block())

    @block.sync
    def _(sp):
        sp.dma_start(b_out[:], io["b_out"]).then_inc(bias_loaded, 16)
        sp.dma_start(w_stage[:], io["wa"][0]).then_inc(w_loaded, 16)

        def start(b):
            pass

        def body(i, n, local, then):
            if not local:
                sp.wait_ge(r_max_done, n + 1)
                sp.dma_start(sort_w[:], io["sort_w"][n % SORT_PAIRS]).then_inc(sort_loaded, 16)
            sp.wait_ge(wo_ready, i + 1)
            sp.dma_start(w_stage[:], io["wa"][(i + 1) % PAIRS]).then_inc(w_loaded, 16)
        pairs(sp, start, body)
        sp.wait_ge(w_loaded, 16 * (BATCH * PAIRS + 1))

    @block.gpsimd
    def _(pool):
        pool.memset(ident[:], 0.0).then_inc(ident_ready, 1)
        pool.wait_ge(ident_ready, 1)
        pool.affine_select(out=ident[:], in_=ident[:], compare_op=ALU.not_equal, fill=1.0, base=0,
                           pattern=[[-1, P]], channel_multiplier=1).then_inc(ident_ready, 1)
        for i in range(2):
            pool.memset(p_diag[:, i], 0.0)
        pool.memset(r_diag[:], 0.0)
        pool.memset(keys[:, 0, 0:1], 0.0)
        pool.memset(keys[:, 0, SEQ + 1:], 0.0)
        pool.memset(v_t[:, 0:BK], 0.0)
        pool.memset(v_t[:, BK + SEQ:], 0.0).then_inc(pads_ready, 1)

        pool.wait_ge(bias_loaded, 16)

        def split_weights(i):
            count = held(pool, i * 16 + 16)
            pool.wait_ge(ident_ready, 2)
            pool.wait_ge(w_loaded, count)
            pool.tensor_copy(w_hi[:].rearrange("p a b c -> p (a b c)"), w_stage[:, 0:3, :].rearrange("p a b -> p (a b)")).then_inc(w_hi_done, 1)
            pool.wait_ge(w_hi_done, i * 2 + 1)
            pool.tensor_tensor(w_lo[:].rearrange("p a b c -> p (a b c)"), w_stage[:, 0:3, :].rearrange("p a b -> p (a b)"),
                               w_hi[:].rearrange("p a b c -> p (a b c)").bitcast(F32), ALU.subtract).then_inc(w_ready, 1)

        def split_out_weights(i):
            pool.tensor_copy(wo_hi[:], w_stage[:, 3, :]).then_inc(w_hi_done, 1)
            pool.wait_ge(w_hi_done, i * 2 + 2)
            pool.tensor_tensor(wo_lo[:], w_stage[:, 3, :], wo_hi[:].bitcast(F32), ALU.subtract).then_inc(wo_ready, 1)

        split_weights(0)
        split_out_weights(0)

        def start(b):
            pass

        def body(i, n, local, then):
            pool.wait_ge(proj_done, i * 12 + 12)
            split_weights(i + 1)
            if then and not then[1]:
                count = held(pool, i * 12 + 24)
                pool.wait_ge(ident_ready, 2)
                pool.wait_ge(proj_read, count)
                pool.tensor_copy(v_by_t[:].rearrange("p (t v) -> p v t", v=NB),
                                 v_t[:, BK:BK + SEQ].rearrange("p (v t) -> p v t", t=BK)).then_inc(v_by_t_ready, 1)
            count = held(pool, i * 8 + 8)
            pool.wait_ge(ident_ready, 2)
            pool.wait_ge(out_done, count)
            split_out_weights(i + 1)
        pairs(pool, start, body)

    @block.scalar
    def _(act):
        def start(b):
            def root(g):
                act.wait_ge(ve_done, b * SG + (g + 1))
                act.activation(std[g % 2], var_eps[g % 2], ACT.Sqrt).then_inc(std_done, 1)

            root(0)
            for g in range(SG):
                k = b * SG + g
                act.wait_ge(nmr_done, k + 1)
                if g >= 2:
                    act.wait_ge(fwd_done, k - 1)
                for t in range(GT):
                    ins = act.activation(xn[g % 2][:, t, :], ring[:, (g % 2) * 2 + t // 2, (t % 2) * D:(t % 2 + 1) * D], ACT.Identity,
                                         scale=rstd[g % 2][:, t:t + 1], bias=nmr[g % 2][:, t:t + 1])
                ins.then_inc(xn_ready, 1)
                if g + 1 < SG:
                    root(g + 1)
                act.wait_ge(fwd_done, k + 1)
                act.activation(y_hi[:, :, g * G:(g + 1) * G], quad[:, (g % 2) * 2:(g % 2) * 2 + 2, :], ACT.Copy).then_inc(y_hi_ready, 1)
            act.wait_ge(pads_ready, 1)
            read_projection(b * PAIRS)
            read_turned(b * LOCAL_PAIRS, True, 0, 4)

        def read_projection(i, parts=(0, 1, 2)):
            for j in [4 * part + g for part in parts for g in range(SG)]:
                kind, g = j // SG, j % SG
                act.wait_ge(proj_done, i * 12 + (j + 1))
                src = ring[:, j % 4, :]
                if kind == 0:
                    ins = act.activation(q_t[:, g * G:(g + 1) * G], src, ACT.Copy)
                elif kind == 1:
                    nb = G // BK
                    ins = act.activation(own_keys.rearrange("p (t v) -> p v t", v=NB)[:, g * nb:(g + 1) * nb, :],
                                         src.rearrange("p (v t) -> p v t", t=BK), ACT.Copy)
                else:
                    ins = act.activation(v_t[:, BK + g * G:BK + (g + 1) * G], src, ACT.Copy)
                ins.then_inc(proj_read, 1)

        def read_turned(n, local, first, last):
            dests = values[True] if local else [k_bk, v_tok[0], v_bk, v_tok[1]]
            for c in range(first, last):
                act.wait_ge(turned[local], n * PER[local] + (c + 1))
                act.activation(dests[c // 4][:, (c % 4) * 4:(c % 4) * 4 + 4, :].rearrange("p a b -> p (a b)"), ring[:, bank_of(c), :], ACT.Copy)\
                   .then_inc(turned_read[local], 1)

        def body(i, n, local, then):
            if not local:
                for r in range(2):
                    act.wait_ge(logits_done, n * 2 + (r + 1))
                    act.activation(r_log[r * DH:(r + 1) * DH, :], ring[r * DH:(r + 1) * DH, r, 0:NB], ACT.Relu).then_inc(logits_read, 1)
                read_turned(n, local, 4, 6)
                act.wait_ge(r_neg_done, n + 1)
                act.activation(r_log[:], r_log[:], ACT.Exp, bias=r_small[:, 1:2], accum_out=r_small[:, 2:3]).then_inc(r_exp_done, 1)
                read_turned(n, local, 6, 12)
                act.wait_ge(r_turned, n + 1)
                for half in range(2):
                    rows = slice(half * NB, (half + 1) * NB)
                    ins = act.activation(r_diag[rows, :, rows], ring[rows, 2, 0:P].rearrange("p (r u) -> p r u", r=2), ACT.Copy)
                ins.then_inc(r_ready, 1)
                for unit in range(4):
                    act.wait_ge(mix_done, n * 4 + (unit + 1))
                    act.activation(mixed(unit, 1), quad[:, (unit % 2) * 2 + 1, :].rearrange("p (t u) -> p t u", u=NB), ACT.Copy).then_inc(mix_read[1], 1)
                read_turned(n, local, 12, 16)
            U, T, W = UNITS[local], TILES[local], BLOCKS[local] * BK

            def read_scores(u):
                act.wait_ge(s_done[local], n * U + (u + 1))
                if u >= 2:
                    act.wait_ge(p_ready[local], n * U + (u - 1))
                act.activation(scratch[:, u % 2, 0:2 * T * W].rearrange("p (r n) -> p r n", r=2),
                               quad[:, (u % 2) * 2:(u % 2) * 2 + 2, 0:T * W], ACT.Copy, scale=SCALE[local]).then_inc(s_read[local], 1)

            def exponent(u):
                act.wait_ge(s_sub_done[local], n * U + (u + 1))
                sc = scratch[:, u % 2, 0:2 * T * W]
                act.activation(sc, sc, ACT.Exp).then_inc(s_exp_done[local], 1)

            read_scores(0)
            read_scores(1)
            if local:
                read_turned(n, local, 4, 8)
            exponent(0)
            exponent(1)
            if local:
                read_turned(n, local, 8, 12)
                read_scores(2)
                read_scores(3)
                exponent(2)
            if then:
                read_projection(i + 1, (0,))
            if local:
                exponent(3)
            if then:
                read_projection(i + 1, (1, 2))
            for g in range(SG):
                act.wait_ge(pv_done[local], n * U + (g * U // SG + 1))
                act.activation(att_hi[:, g * G:(g + 1) * G], quad[:, g, :], ACT.Copy).then_inc(att_hi_ready, 1)
            if then:
                read_turned(*then, 0, 4)
        pairs(act, start, body)

    @block.tensor
    def _(pe):
        pe.wait_ge(ident_ready, 2)

        def start(b):
            def back(g):
                pe.wait_ge(x_staged, b * SG + (g + 1))
                if g >= 2:
                    pe.wait_ge(xn_ready, b * SG + (g - 1))
                else:
                    pe.wait_ge(x_added, b * (PAIRS * 8) + 1)
                for t in range(GT):
                    for c in range(DC):
                        tr = pe.transpose(ring[:, (g % 2) * 2 + t // 2, (t % 2) * D + c * P:(t % 2) * D + (c + 1) * P],
                                          x_static[:, g % 2, c, t * P:(t + 1) * P], ident[:])
                tr.then_inc(back_done, 1)

            back(0)
            for g in range(SG):
                if g + 1 < SG:
                    back(g + 1)
                pe.wait_ge(xn_ready, b * SG + (g + 1))
                if g >= 2:
                    pe.wait_ge(y_ready, b * SG + (g - 1))
                else:
                    pe.wait_ge(att_ready, b * (PAIRS * 4) + 1)
                for c in range(DC):
                    for t in range(GT):
                        tr = pe.transpose(quad[:, (g % 2) * 2 + c, t * P:(t + 1) * P], xn[g % 2][:, t, c * P:(c + 1) * P], ident[:])
                tr.then_inc(fwd_done, 1)
            pe.wait_ge(pads_ready, 1)
            pe.wait_ge(y_ready, b * SG + SG)
            project(b * PAIRS)
            pe.wait_ge(proj_read, b * (PAIRS * 12) + 12)
            turn(b * LOCAL_PAIRS, True, 0, 4)

        def around(h, bk):
            first = keys[h, 0, bk:bk + 3]
            return bass.AP(tensor=first.tensor, offset=first.offset, ap=[first.ap[0], [1, 3], [NB, BK]])

        def passes(out, lhs, rhs, start, stop):
            pe.matmul(out, lhs[0], rhs[0], start=start, stop=False)
            pe.matmul(out, lhs[0], rhs[1], start=False, stop=False)
            return pe.matmul(out, lhs[1], rhs[0], start=False, stop=stop)

        def project(i, parts=(0, 1, 2)):
            if parts[0] == 0:
                pe.wait_ge(w_ready, i + 1)
            for j in [4 * part + g for part in parts for g in range(SG)]:
                kind, g = j // SG, j % SG
                if j >= 4:
                    pe.wait_ge(proj_read, i * 12 + (j - 3))
                for kc in range(DC):
                    mm = passes(ring[:, j % 4, :], (w_hi[:, kind, kc, :], w_lo[:, kind, kc, :]),
                                (y_hi[:, kc, g * G:(g + 1) * G], y_lo[:, kc, g * G:(g + 1) * G]), kc == 0, kc == DC - 1)
                mm.then_inc(proj_done, 1)

        def turn(n, local, first, last):
            for c in range(first, last):
                if c >= 4:
                    pe.wait_ge(turned_read[local], n * PER[local] + max(c - 3, 4))
                for k in range(4):
                    t = 4 * (c % 4) + k
                    if local:
                        src = v_t[:, (c // 4) * BK + t * P:(c // 4) * BK + (t + 1) * P]
                    else:
                        src = (own_keys, v_t[:, BK:BK + SEQ], v_by_t[:], mixed_t)[c // 4][:, t * P:(t + 1) * P]
                    tr = pe.transpose(ring[:, bank_of(c), k * P:(k + 1) * P], src, ident[:])
                tr.then_inc(turned[local], 1)

        def logits(i, n):
            pe.wait_ge(sums_done, n * 2 + 2)
            pe.wait_ge(sort_loaded, n * 16 + 16)
            for r in range(2):
                count = held(pe, i * 8 + (r + 6))
                pe.wait_ge(ident_ready, 2)
                pe.wait_ge(x_added, count)
                h = slice(r * DH, (r + 1) * DH)
                pe.matmul(ring[h, r, 0:NB], sums[h, 0, :], sort_w[h, 0, :], start=True, stop=False)
                pe.matmul(ring[h, r, 0:NB], sums[h, 1, :], sort_w[h, 1, :], start=False, stop=True).then_inc(logits_done, 1)

        def scores(i, n, local, u):
            U, T, W = UNITS[local], TILES[local], BLOCKS[local]
            if u >= 2 or local:
                count = held(pe, n * U + (u - 1) if u >= 2 else i * 4 + 1)
                pe.wait_ge(ident_ready, 2)
                pe.wait_ge(s_read[local] if u >= 2 else att_ready, count)
            for t in range(u * T, (u + 1) * T):
                for r in range(2):
                    h = slice(r * DH, (r + 1) * DH)
                    for j in range(BT):
                        bk = t * BT + j
                        if local:
                            rhs = around(h, bk)
                        else:
                            rhs = keys[h, :, 1 + bk:1 + bk + SEQ - NB + 1:NB]
                        out = quad[j * BK:(j + 1) * BK, (u % 2) * 2 + r, (t % T) * W * BK:(t % T + 1) * W * BK]
                        mm = pe.matmul(out.rearrange("p (a b) -> p a b", b=BK), q_t[h, bk * BK:(bk + 1) * BK], rhs, start=True, stop=True)
            mm.then_inc(s_done[local], 1)

        def body(i, n, local, then):
            U, T, W = UNITS[local], TILES[local], BLOCKS[local]
            if local:
                scores(i, n, local, 0)
                scores(i, n, local, 1)
            pe.wait_ge(x_added, i * 8 + 1)
            if local:
                turn(n, local, 4, 12)
                scores(i, n, local, 2)
                scores(i, n, local, 3)
            else:
                turn(n, local, 4, 6)
                pe.wait_ge(logits_read, n * 2 + 2)
                turn(n, local, 6, 8)
                pe.wait_ge(v_by_t_ready, n + 1)
                turn(n, local, 8, 12)
                pe.wait_ge(turned_read[False], n * PER[False] + 9)
                pe.wait_ge(r_two_done, n + 1)
                pe.transpose(ring[:, 2, 0:P], r_two[:].rearrange("p a b -> p (a b)"), ident[:]).then_inc(r_turned, 1)
                pe.wait_ge(r_ready, n + 1)
                for unit in range(4):
                    src = (k_bk, v_bk)[unit // 2]
                    count = held(pe, n * 4 + (unit - 1) if unit >= 2 else i * 4 + 1)
                    pe.wait_ge(ident_ready, 2)
                    if unit >= 2:
                        pe.wait_ge(mix_read[0], count)
                        pe.wait_ge(mix_read[1], count)
                    else:
                        pe.wait_ge(att_ready, count)
                    for m in range(8):
                        for r in range(2):
                            at = (m % 4) * P
                            mm = pe.matmul(quad[r * DH:(r + 1) * DH, (unit % 2) * 2 + m // 4, at:at + P],
                                           src[:, (unit % 2) * 8 + m, r * DH:(r + 1) * DH], r_diag[:, r, :], start=True, stop=True)
                    mm.then_inc(mix_done, 1)
                for read in mix_read:
                    pe.wait_ge(read, n * 4 + 4)
                turn(n, local, 12, 16)
                scores(i, n, local, 0)
                scores(i, n, local, 1)
            pe.wait_ge(turned_read[local], n * PER[local] + PER[local])
            if not local:
                pe.wait_ge(r_ready, n + 1)
            if then:
                project(i + 1, (0,) if local else (0, 1))
            for u in range(U):
                count = held(pe, n * U + (u + 1))
                if local:
                    pe.wait_ge(s_read[local], n * U + min(u + 3, U))
                else:
                    pe.wait_ge(s_read[local], n * U + (u + 1))
                pe.wait_ge(ident_ready, 2)
                pe.wait_ge(p_ready[local], count)
                for t in range(T):
                    tile = u * T + t
                    for r in range(2):
                        for w in range(W):
                            mm = pe.matmul(quad[r * DH:(r + 1) * DH, tile // GT, (tile % GT) * P:(tile % GT + 1) * P],
                                           values[local][w][:, tile, r * DH:(r + 1) * DH], p_diag[:, u % 2, (r * T + t) * W + w, :],
                                           start=(w == 0), stop=(w == W - 1))
                mm.then_inc(pv_done[local], 1)
                if then and u < U - 1 - local:
                    project(i + 1, (u + 1 if local else 2,))
            if then:
                pe.wait_ge(proj_read, i * 12 + 24)
                turn(*then, 0, 4)
            pe.wait_ge(wo_ready, i + 1)
            for j in range(8):
                g, oc = j // 2, j % 2
                if j < 4:
                    if then:
                        pe.wait_ge(turned_read[then[1]], then[0] * PER[then[1]] + (j + 1))
                else:
                    pe.wait_ge(x_added, i * 8 + (j - 2))
                pe.wait_ge(att_ready, i * 4 + (g + 2))
                cols = slice(g * G, (g + 1) * G)
                passes(ring[:, j % 4, :], (wo_hi[:, oc * P:(oc + 1) * P], wo_lo[:, oc * P:(oc + 1) * P]),
                       (att_hi[:, cols], att_lo[:, cols]), True, True).then_inc(out_done, 1)
            if then and not then[1]:
                logits(i, then[0])
        pairs(pe, start, body)

    @block.vector
    def _(dve):
        dve.memset(s_small[:, 0], 0.0).then_inc(r_max_done, 1)
        dve.memset(s_small[:, 1], 0.0).then_inc(x_added, 1)
        dve.memset(sums[:], 0.0).then_inc(att_ready, 1)

        def start(b):
            def stage(g):
                if g >= 2:
                    dve.wait_ge(back_done, b * SG + (g - 1))
                dve.tensor_copy(x_static[:, g % 2], x32[:, :, bass.ds(b * SEQ + g * G, G)]).then_inc(x_staged, 1)

            def low(g):
                dve.wait_ge(y_hi_ready, b * SG + (g + 1))
                ys = slice(g * G, (g + 1) * G)
                dve.tensor_tensor(y_lo[:, :, ys], quad[:, (g % 2) * 2:(g % 2) * 2 + 2, :], y_hi[:, :, ys].bitcast(F32), ALU.subtract).then_inc(y_ready, 1)

            def add_bias(g):
                dve.wait_ge(bias_loaded, 16)
                for c in range(DC):
                    xs = x32[:, c, bass.ds(b * SEQ + g * G, G)]
                    ins = dve.tensor_scalar(xs, xs, b_out[:, c:c + 1], None, ALU.add)
                ins.then_inc(bias_added, 1)

            stage(0)
            stage(1)
            for g in range(SG):
                k, h = b * SG + g, g % 2
                dve.wait_ge(back_done, k + 1)
                for t in range(GT):
                    ins = dve.bn_stats(stats[h][:, t, :], ring[:, h * 2 + t // 2, (t % 2) * D:(t % 2 + 1) * D])
                ins.then_inc(norm_steps, 1)
                count = held(dve, k * 3 + 1)
                dve.wait_ge(ident_ready, 2)
                dve.wait_ge(norm_steps, count)
                for t in range(GT):
                    ins = dve.bn_aggr(mv[h][:, t, :], stats[h][:, t, :])
                ins.then_inc(norm_steps, 1)
                dve.wait_ge(norm_steps, k * 3 + 2)
                dve.tensor_scalar(var_eps[h], mv[h][:, :, 1], EPS, None, ALU.add).then_inc(ve_done, 1)
                if g + 2 < SG:
                    stage(g + 2)
                dve.wait_ge(std_done, k + 1)
                if g >= 2:
                    dve.wait_ge(xn_ready, k - 1)
                dve.reciprocal(rstd[h], std[h]).then_inc(norm_steps, 1)
                dve.wait_ge(norm_steps, k * 3 + 3)
                dve.scalar_tensor_tensor(out=nmr[h], in0=mv[h][:, :, 0], scalar=-1.0, in1=rstd[h],
                                         op0=ALU.mult, op1=ALU.mult).then_inc(nmr_done, 1)
                if g >= 1:
                    low(g - 1)
                    add_bias(g - 1)
            low(SG - 1)
            dve.wait_ge(pads_ready, 1)
            add_bias(SG - 1)

        def body(i, n, local, then):
            if not local:
                dve.wait_ge(logits_read, n * 2 + 2)
                dve.tensor_reduce(r_small[:, 0:1], r_log[:], AX.X, ALU.max).then_inc(r_max_done, 1)
                dve.wait_ge(r_max_done, n + 2)
                dve.tensor_scalar(r_small[:, 1:2], r_small[:, 0:1], -1.0, None, ALU.mult).then_inc(r_neg_done, 1)
                dve.wait_ge(r_exp_done, n + 1)
                dve.reciprocal(r_small[:, 3:4], r_small[:, 2:3]).then_inc(r_inv_done, 1)
                dve.wait_ge(r_inv_done, n + 1)
                for c in range(2):
                    ins = dve.tensor_scalar(r_two[:, c, :], r_log[:], r_small[:, 3:4], None, ALU.mult)
                ins.then_inc(r_two_done, 1)
                for unit in range(4):
                    dve.wait_ge(mix_done, n * 4 + (unit + 1))
                    dve.tensor_copy(mixed(unit, 0), quad[:, (unit % 2) * 2, :].rearrange("p (t u) -> p t u", u=NB)).then_inc(mix_read[0], 1)
            U, T, W = UNITS[local], TILES[local], BLOCKS[local] * BK
            def small(u):
                return s_small[:, u % 2, 0:2 * T]

            def rows_of(u):
                return scratch[:, u % 2, 0:2 * T * W].rearrange("p (a w) -> p a w", w=W)

            def wide(u):
                return small(u).unsqueeze(2).to_broadcast([P, 2 * T, W])

            def less_maximum(u):
                k = n * U + u
                by_tile = scratch[:, u % 2, 0:2 * T * W].rearrange("p (r t w) -> p r t w", r=2, t=T)
                dve.wait_ge(s_read[local], k + 1)
                if local and u == 0:
                    dve.memset(by_tile[0:BK, :, 0, 0:BK], NEG).then_inc(s_masked, 1)
                    dve.wait_ge(s_masked, n * 2 + 1)
                if local and u == U - 1:
                    dve.memset(by_tile[P - BK:P, :, T - 1, 2 * BK:3 * BK], NEG).then_inc(s_masked, 1)
                    dve.wait_ge(s_masked, n * 2 + 2)
                dve.tensor_reduce(small(u), rows_of(u), AX.X, ALU.max).then_inc(s_max_done[local], 1)
                dve.wait_ge(s_max_done[local], k + 1)
                dve.tensor_tensor(rows_of(u), rows_of(u), wide(u), ALU.subtract).then_inc(s_sub_done[local], 1)

            def probabilities(u):
                k = n * U + u
                dve.wait_ge(s_exp_done[local], k + 1)
                dve.tensor_reduce(small(u), rows_of(u), AX.X, ALU.add).then_inc(s_sum_done[local], 1)
                dve.wait_ge(s_sum_done[local], k + 1)
                dve.reciprocal(small(u), small(u)).then_inc(s_inv_done[local], 1)
                dve.wait_ge(s_inv_done[local], k + 1)
                dve.tensor_tensor(rows_of(u), rows_of(u), wide(u), ALU.mult).then_inc(s_norm_done[local], 1)
                dve.wait_ge(s_norm_done[local], k + 1)
                if u >= 2:
                    dve.wait_ge(pv_done[local], n * U + (u - 1))
                for j in range(BT):
                    rows = slice(j * BK, (j + 1) * BK)
                    ins = dve.transpose(p_diag[rows, u % 2, 0:2 * T * BLOCKS[local], rows],
                                        scratch[rows, u % 2, 0:2 * T * W].rearrange("p (n k) -> p n k", k=BK))
                ins.then_inc(p_ready[local], 1)

            for u in range(0, U, 2):
                less_maximum(u)
                less_maximum(u + 1)
                probabilities(u)
                probabilities(u + 1)

            def bucket_sums(k):
                src = (q_t[:].rearrange("p (v t) -> p v t", t=BK), own_keys.rearrange("p (t v) -> p v t", v=NB))[k]
                dve.wait_ge(proj_read, i * 12 + (16 + 4 * k))
                dve.tensor_reduce(sums[:, k, :], src, AX.X, ALU.add).then_inc(sums_done, 1)

            for g in range(SG):
                if then and not then[1] and g % 2 == 0:
                    bucket_sums(g // 2)
                dve.wait_ge(att_hi_ready, i * 4 + (g + 1))
                cols = slice(g * G, (g + 1) * G)
                dve.tensor_tensor(att_lo[:, cols], quad[:, g, :], att_hi[:, cols].bitcast(F32), ALU.subtract).then_inc(att_ready, 1)
            at = (i // PAIRS) * SEQ
            dve.wait_ge(bias_added, (i // PAIRS) * SG + SG)
            for j in range(8):
                g, oc = j // 2, j % 2
                dve.wait_ge(out_done, i * 8 + (j + 1))
                xs = x32[:, oc, bass.ds(at + g * G, G)]
                dve.tensor_tensor(xs, ring[:, j % 4, :], xs, ALU.add).then_inc(x_added, 1)
        pairs(dve, start, body)


E = 7
CAP = 732
ET = -(-CAP // P)
LAST_ROWS = CAP - (ET - 1) * P
HALF = CAP // 2
REC = D + 4
NT = N_TOK // P
ES = 8
WC = 3 * D
SKIP = 1.0e6


def experts(nc, ctx, io, x32, rows_for, acc):
    def sb(name, shape, dt=F32):
        return ctx.enter_context(nc.sbuf_tensor("e_" + name, shape, dt))

    def sem(name):
        return ctx.enter_context(nc.semaphore("e_" + name))

    rec = sb("rec", [P, NT, REC])
    w_hi = sb("w_hi", [P, FC, WC], F32R)
    w_lo = sb("w_lo", [P, FC, WC], F32R)
    w_stage = sb("w_stage", [P, 2, WC])
    f_hi = sb("f_hi", [P, 2, DC, 768], F32R)
    f_lo = sb("f_lo", [P, 2, DC, 768], F32R)
    f32 = sb("f32", [P, DC, 768])
    xr = sb("xr", [P, ET, REC])
    s32 = sb("s32", [P, 2, G])
    g32 = sb("g32", [P, 768])
    g_hi = sb("g_hi", [P, 2, 768], F32R)
    g_lo = sb("g_lo", [P, 2, 768], F32R)
    yo = sb("yo", [P, ET, D])
    ht = sb("ht", [P, 2, GT, D])
    ident = sb("ident", [P, P])
    below = sb("below", [P, P])
    ones = sb("ones", [P, P])
    ln_g = sb("ln_g", [P, DC])
    ln_b = sb("ln_b", [P, DC])
    w_r = sb("w_r", [P, DC, E])
    stats = sb("stats", [P, 2, GT, 6])
    mv = sb("mv", [P, 2, GT, 2])
    var_eps = sb("ve", [P, 2, GT])
    std = sb("std", [P, 2, GT])
    rstd = sb("rstd", [P, 2, GT])
    nmr = sb("nmr", [P, 2, GT])
    iot = sb("iot", [P, 3, ES], I32)
    cst = sb("cst", [P, 3, ES])
    lg = sb("lg", [P, NT, ES])
    eq = sb("eq", [P, NT, ES])
    hot = sb("hot", [P, 2, NT, ES])
    top = sb("top", [P, 2, NT])
    which = sb("which", [P, 2, NT])
    small = sb("small", [P, 4, NT])
    tot = sb("tot", [P, ES])
    before = sb("before", [DH, 2 * NT, ES])
    at_pos = sb("at_pos", [P, 2 * NT, ES])
    place = sb("place", [P, 4, 2 * NT])
    place_u = sb("place_u", [P, 2 * NT], U32)
    gate = sb("gate", [P, ET])
    gate_next = sb("gate_next", [P, ET])
    tok_next = sb("tok_next", [P, ET], I32)
    gtmp = sb("gtmp", [P, 2, ET])
    tok = sb("tok", [P, ET], I32)

    ps = ctx.enter_context(nc.psum_tensor("e_ps", [P, 8, G], F32))

    consts_ready = sem("consts_ready")
    iota_done = sem("iota_done")
    cst_done = sem("cst_done")
    small_loaded = sem("small_loaded")
    back_done = sem("back_done")
    norm_steps = sem("norm_steps")
    ve_done = sem("ve_done")
    std_done = sem("std_done")
    nmr_done = sem("nmr_done")
    ht_ready = sem("ht_ready")
    ht_sent = [sem(f"ht_sent{i}") for i in range(2)]
    rec_ready = sem("rec_ready")
    fwd_done = sem("fwd_done")
    feat_ready = sem("feat_ready")
    logits_done = sem("logits_done")
    route = sem("route")
    gap_ready = sem("gap_ready")
    gate_exp_done = sem("gate_exp_done")
    hot_ready = sem("hot_ready")
    tot_done = sem("tot_done")
    before_ready = sem("before_ready")
    pos_done = sem("pos_done")
    place_ready = sem("place_ready")
    dispatched = sem("dispatched")
    w_loaded = [sem(f"w_loaded{i}") for i in range(2)]
    w_hi_done = sem("w_hi_done")
    w_ready = sem("w_ready")
    f_hi_done = sem("f_hi_done")
    f_ready = sem("f_ready")
    xr_loaded = sem("xr_loaded")
    xr_zeroed = sem("xr_zeroed")
    turned = sem("turned")
    f32_ready = sem("f32_ready")
    up_done = sem("up_done")
    silu_done = sem("silu_done")
    prod_done = sem("prod_done")
    g_hi_ready = sem("g_hi_ready")
    g_lo_ready = sem("g_lo_ready")
    down_done = sem("down_done")
    y_read = sem("y_read")
    y_sent = sem("y_sent")
    tok_done = sem("tok_done")
    gate_steps = sem("gate_steps")
    gate_ready = sem("gate_ready")

    JS = NG

    def jobs(eng, body):
        body(0, 0, None, None)
        body(1, 1, None, (0, 0, None))
        with eng.Fori(1, JS // 2 - 1) as i:
            for b in range(2):
                body(i * 2 + b, b, None, (i * 2 + (b - 1), 1 - b, None))
        for g in (JS - 2, JS - 1):
            body(g, g % 2, None, (g - 1, (g - 1) % 2, None))
        body(JS, None, 0, (JS - 1, (JS - 1) % 2, None))
        with eng.Fori(1, E - 1) as e:
            body(e + JS, None, e, (e + (JS - 1), None, e - 1))
        body(JS + E - 1, None, E - 1, (JS + E - 2, None, E - 2))

    def is_first(j):
        return isinstance(j, int) and j == 0

    def is_last_shared(j):
        return isinstance(j, int) and j == JS - 1

    def has_next(j, e):
        return is_last_shared(j) if e is None else not isinstance(e, int) or e < E - 1

    def part(j, e, m, h=0):
        return j * FC + m if e is None else e * (2 * FC) + (JS * FC + 2 * m + h)

    def y_bank(j, b, e):
        return 6 if e is None and b == 1 and not is_last_shared(j) else 4

    def w1(w, m, kc):
        return w[:, m, kc * P:(kc + 1) * P]

    def w3(w, m, kc):
        return w[:, m, D + kc * P:D + (kc + 1) * P]

    def w2(w, m):
        return w[:, m, 2 * D:3 * D]

    block = ctx.enter_context(nc.Block())

    @block.sync
    def _(sp):
        sp.dma_start(ln_g[:], io["ffn_g"]).then_inc(small_loaded, 16)
        sp.dma_start(ln_b[:], io["ffn_b"]).then_inc(small_loaded, 16)
        sp.dma_start(w_r[:], io["w_r"]).then_inc(small_loaded, 16)
        def send_rows(g):
            sp.wait_ge(ht_ready, g + 1)
            sp.dma_start(acc[g * G:(g + 1) * G, :].rearrange("(t p) d -> p t d", p=P), ht[:, g % 2, :, :]).then_inc(ht_sent[g % 2], 16)

        for q in range(FC):
            if q >= 2:
                sp.wait_ge(w_ready, q - 1)
            sp.dma_start(w_stage[:, q % 2, :], io["we"][q]).then_inc(w_loaded[q % 2], 16)
            send_rows(q)

        def load_weights(q0, first, last):
            for m in range(first, last):
                sp.wait_ge(w_ready, q0 + (m - 1))
                sp.dma_start(w_stage[:, m % 2, :], io["we"][q0 + m]).then_inc(w_loaded[m % 2], 16)

        def load_rows(e):
            full = (ET - 1) * P
            sp.dma_start(xr[:, 0:ET - 1, :], rows_for[bass.ds(e * CAP, full), :].rearrange("(t p) c -> p t c", p=P)).then_inc(xr_loaded, 16)
            sp.dma_start(xr[0:LAST_ROWS, ET - 1, :], rows_for[bass.ds(e * CAP + full, LAST_ROWS), :]).then_inc(xr_loaded, 16)

        sp.wait_ge(xr_zeroed, 1)
        load_weights(FC, 0, 2)
        sp.wait_ge(dispatched, 16 * 2 * NT)
        load_rows(0)
        load_weights(FC, 2, FC)
        with sp.Fori(0, E - 1) as e:
            sp.wait_ge(tok_done, e + 1)
            sp.wait_ge(gate_steps, e * 3 + 3)
            sp.wait_ge(turned, e * 3 + 3)
            load_rows(e + 1)
            load_weights(e * FC + 2 * FC, 0, FC)
        sp.wait_ge(y_sent, 16 * (JS + E * ET))

    @block.gpsimd
    def _(pool):
        pool.memset(ident[:], 0.0).then_inc(iota_done, 1)
        pool.memset(below[:], 1.0).then_inc(iota_done, 1)
        pool.memset(xr[:], 0.0).then_inc(xr_zeroed, 1)
        pool.memset(ones[:], 1.0)
        pool.wait_ge(iota_done, 2)
        pool.affine_select(out=ident[:], in_=ident[:], compare_op=ALU.not_equal, fill=1.0, base=0,
                           pattern=[[-1, P]], channel_multiplier=1)
        pool.affine_select(out=below[:], in_=below[:], compare_op=ALU.is_gt, fill=0.0, base=0,
                           pattern=[[1, P]], channel_multiplier=-1).then_inc(consts_ready, 1)
        pool.iota(iot[:, 0, :], pattern=[[-1, ES]], base=ES, channel_multiplier=0)
        pool.iota(iot[:, 1, :], pattern=[[CAP, ES]], base=0, channel_multiplier=0)
        pool.iota(iot[:, 2, :], pattern=[[1, ES]], base=0, channel_multiplier=0)
        pool.iota(rec[:].bitcast(I32)[:, :, D], pattern=[[P, NT]], base=0, channel_multiplier=1).then_inc(consts_ready, 1)

        for m in range(FC):
            pool.wait_ge(w_loaded[m % 2], (m // 2) * 16 + 16)
            pool.tensor_copy(w_hi[:, m, :], w_stage[:, m % 2, :]).then_inc(w_hi_done, 1)
            pool.wait_ge(w_hi_done, m + 1)
            pool.tensor_tensor(w_lo[:, m, :], w_stage[:, m % 2, :], w_hi[:, m, :].bitcast(F32), ALU.subtract).then_inc(w_ready, 1)

        def low_weights(q, m):
            pool.wait_ge(w_hi_done, q + 1)
            pool.tensor_tensor(w_lo[:, m, :], w_stage[:, m % 2, :], w_hi[:, m, :].bitcast(F32), ALU.subtract).then_inc(w_ready, 1)

        pool.wait_ge(place_ready, 1)
        for i in range(2):
            pool.wait_ge(ht_sent[i], 16 * NG // 2)
        sends = [(k, t) for k in range(2) for t in range(NT)]
        per = -(-len(sends) // (JS - 2))
        for j in range(JS):
            for k, t in sends[j * per:(j + 1) * per]:
                pool.indirect_dma_start(out=rows_for[:, :], in_=rec[:, t, :], in_offset=None,
                                        out_offset=bass.IndirectOffsetOnAxis(ap=place_u[:, k * NT + t:k * NT + t + 1], axis=0),
                                        bounds_check=E * CAP - 1, oob_is_err=False).then_inc(dispatched, 16)
            if j == JS - 1:
                for m in range(FC):
                    low_weights(FC + m, m)
            pool.wait_ge(y_read, j + 1)
            pool.dma_start(acc[j * G:(j + 1) * G, :].rearrange("(t p) d -> p t d", p=P), yo[:, 0:GT, :],
                           accum_op=ALU.add).then_inc(y_sent, 16)

        def send(e, t):
            if t == 0:
                pool.wait_ge(y_read, e + (JS + 1))
            count = held(pool, e * (16 * ET) + 16 * (JS + t))
            pool.wait_ge(iota_done, 2)
            pool.wait_ge(y_sent, count)
            n = P if t < ET - 1 else LAST_ROWS
            pool.indirect_dma_start(out=acc[:, :], in_=yo[0:n, t, :], in_offset=None,
                                    out_offset=bass.IndirectOffsetOnAxis(ap=tok[0:n, t:t + 1].bitcast(U32), axis=0),
                                    compute_op=ALU.add).then_inc(y_sent, 16)

        for m in range(FC):
            low_weights(2 * FC + m, m)
        with pool.Fori(0, E - 2) as e:
            send(e, 0)
            for m in range(FC):
                if m + 1 < ET:
                    send(e, m + 1)
                low_weights(e * FC + (3 * FC + m), m)
        for e in (E - 2, E - 1):
            for t in range(ET):
                send(e, t)

    @block.scalar
    def _(act):
        act.wait_ge(small_loaded, 48)

        def root(g):
            act.wait_ge(ve_done, g + 1)
            act.activation(std[:, g % 2], var_eps[:, g % 2], ACT.Sqrt).then_inc(std_done, 1)

        root(0)
        for g in range(NG):
            act.wait_ge(nmr_done, g + 1)
            for t in range(GT):
                ins = act.activation(rec[:, g * GT + t, 0:D], ps[:, (g % 2) * 2 + t // 2, (t % 2) * D:(t % 2 + 1) * D], ACT.Identity,
                                     scale=rstd[:, g % 2, t:t + 1], bias=nmr[:, g % 2, t:t + 1])
            ins.then_inc(rec_ready, 1)
            if g + 1 < NG:
                root(g + 1)
            act.wait_ge(fwd_done, g + 1)
            for c in range(DC):
                ins = act.activation(x32[:, c, g * G:(g + 1) * G], ps[:, 4 + c, :], ACT.Identity,
                                     scale=ln_g[:, c:c + 1], bias=ln_b[:, c:c + 1])
            ins.then_inc(feat_ready, 1)
        act.wait_ge(gap_ready, 1)
        act.activation(small[:, 1, :], small[:, 0, :], ACT.Exp).then_inc(gate_exp_done, 1)

        def read_turned(e, q):
            act.wait_ge(turned, e * 3 + (q + 1))
            n = 2 * P if q < 2 else CAP - 4 * P
            for c in range(DC):
                ins = act.activation(f32[:, c, q * 2 * P:q * 2 * P + n], ps[:, 7, c * 2 * P:c * 2 * P + n], ACT.Identity,
                                     scale=ln_g[:, c:c + 1], bias=ln_b[:, c:c + 1])
            ins.then_inc(f32_ready, 1)

        def high_weights(j, e, m):
            first = FC if e is None else e * FC + 2 * FC
            act.wait_ge(w_loaded[m % 2], (first + m) // 2 * 16 + 16)
            act.wait_ge(down_done, j * FC + (m + 1))
            act.activation(w_hi[:, m, :], w_stage[:, m % 2, :], ACT.Copy).then_inc(w_hi_done, 1)

        def result(j, b, e):
            act.wait_ge(down_done, j * FC + FC)
            if e is None:
                if not is_first(j):
                    act.wait_ge(y_sent, j * 16)
                bank = y_bank(j, b, e)
                act.activation(yo[:, 0:GT, :].rearrange("p t d -> p (t d)"), ps[:, bank:bank + 2, :].rearrange("p a b -> p (a b)"), ACT.Copy).then_inc(y_read, 1)
            else:
                act.wait_ge(gate_ready, e + 2)
                act.wait_ge(y_sent, 16 * JS + (16 * ET) * e)
                for t in range(ET):
                    n = P if t < ET - 1 else LAST_ROWS
                    ins = act.activation(yo[0:n, t, :], ps[0:n, 4 + t // 2, (t % 2) * D:(t % 2 + 1) * D], ACT.Copy, scale=gate[0:n, t:t + 1])
                ins.then_inc(y_read, 1)
            if has_next(j, e):
                high_weights(j, e, FC - 1)

        def body(j, b, e, last):
            for m in range(FC):
                k = j * FC + m
                if e is None:
                    act.wait_ge(up_done, part(j, e, m + 1))
                    if not (is_first(j) and m < 2):
                        act.wait_ge(prod_done, part(j, e, m - 1))
                    act.activation(s32[:, m % 2, :], ps[:, (m % 2) * 2, :], ACT.Silu).then_inc(silu_done, 1)
                else:
                    for h in range(2):
                        act.wait_ge(up_done, part(j, e, m, h + 1))
                        act.wait_ge(prod_done, part(j, e, m, h - 1))
                        act.activation(s32[:, h, 0:HALF], ps[:, 2 * h, 0:HALF], ACT.Silu).then_inc(silu_done, 1)
                act.wait_ge(prod_done, part(j, e, m + 1))
                if not (is_first(j) and m < 2):
                    act.wait_ge(down_done, k - 1)
                n = G if e is None else CAP
                act.activation(g_hi[:, m % 2, 0:n], g32[:, 0:n], ACT.Copy).then_inc(g_hi_ready, 1)
                if m == 0 and last:
                    result(*last)
                if has_next(j, e) and m >= 1:
                    high_weights(j, e, m - 1)
                if has_next(j, e) and 4 <= m < 7:
                    if m == 4 and e is not None:
                        act.wait_ge(f_ready, j + 1)
                    read_turned(0 if e is None else e + 1, m - 4)
        jobs(act, body)
        result(JS + E - 1, None, E - 1)

    @block.tensor
    def _(pe):
        pe.wait_ge(consts_ready, 1)

        def back(g):
            if g >= 2:
                pe.wait_ge(rec_ready, g - 1)
                pe.wait_ge(ht_ready, g - 1)
            for t in range(GT):
                for c in range(DC):
                    tr = pe.transpose(ps[:, (g % 2) * 2 + t // 2, (t % 2) * D + c * P:(t % 2) * D + (c + 1) * P],
                                      x32[:, c, g * G + t * P:g * G + (t + 1) * P], ident[:])
            tr.then_inc(back_done, 1)

        def logits(g):
            pe.wait_ge(feat_ready, g + 1)
            pe.wait_ge(small_loaded, 48)
            for t in range(GT):
                for c in range(DC):
                    at = (g * GT + t) * ES
                    mm = pe.matmul(ps[:, 6, at:at + E], x32[:, c, g * G + t * P:g * G + (t + 1) * P], w_r[:, c, :],
                                   start=(c == 0), stop=(c == DC - 1))
            mm.then_inc(logits_done, 1)

        back(0)
        for g in range(NG):
            if g + 1 < NG:
                back(g + 1)
            pe.wait_ge(rec_ready, g + 1)
            if g >= 1:
                pe.wait_ge(feat_ready, g)
            for c in range(DC):
                for t in range(GT):
                    tr = pe.transpose(ps[:, 4 + c, t * P:(t + 1) * P], rec[:, g * GT + t, c * P:(c + 1) * P], ident[:])
            tr.then_inc(fwd_done, 1)
            if g >= 1:
                logits(g - 1)
        logits(NG - 1)

        def passes(out, lhs, rhs, start, stop, check=False):
            pe.matmul(out, lhs[0], rhs[0], start=start, stop=False, skip_group_check=check)
            pe.matmul(out, lhs[0], rhs[1], start=False, stop=False, skip_group_check=check)
            return pe.matmul(out, lhs[1], rhs[0], start=False, stop=stop, skip_group_check=check)

        def up(j, b, e, m):
            if m == 0:
                pe.wait_ge(f_ready, j + 1)
            if e is None:
                if is_first(j):
                    pe.wait_ge(w_ready, m + 1)
                if not (is_first(j) and m < 2):
                    pe.wait_ge(prod_done, part(j, e, m - 1))
                elif m == 0:
                    pe.wait_ge(rec_ready, NG)
                    pe.wait_ge(ht_ready, NG)
                halves = [((m % 2) * 2, 0, G)]
            else:
                pe.wait_ge(w_ready, e * FC + (FC + m + 1))
                halves = [(2 * h, h * HALF, HALF) for h in range(2)]
            for h, (bank, at, n) in enumerate(halves):
                if e is not None:
                    pe.wait_ge(prod_done, part(j, e, m, h - 1))
                par = b if b is not None else e % 2
                for which_w, w in enumerate((w1, w3)):
                    for kc in range(DC):
                        rhs = [f[:, par, kc, at:at + n] for f in (f_hi, f_lo)]
                        mm = passes(ps[:, bank + which_w, 0:n], (w(w_hi, m, kc), w(w_lo, m, kc)), rhs, kc == 0, kc == DC - 1)
                mm.then_inc(up_done, 1)

        def down(j, b, e, m):
            k = j * FC + m
            pe.wait_ge(g_hi_ready, k + 1)
            pe.wait_ge(g_lo_ready, k + 1)
            if m == 0:
                if is_first(j):
                    pe.wait_ge(feat_ready, NG)
                elif e is None and isinstance(j, int) and j == 1:
                    pe.wait_ge(place_ready, 1)
                elif e is None and not is_last_shared(j):
                    pe.wait_ge(y_read, j - 1)
                else:
                    pe.wait_ge(y_read, j)
            for t in range(GT if e is None else ET):
                n = P if t < ET - 1 else LAST_ROWS
                g = [x[:, m % 2, t * P:t * P + n] for x in (g_hi, g_lo)]
                mm = passes(ps[0:n, y_bank(j, b, e) + t // 2, (t % 2) * D:(t % 2 + 1) * D], g, (w2(w_hi, m), w2(w_lo, m)),
                            m == 0 and t % 2 == 0, m == FC - 1, True)
            mm.then_inc(down_done, 1)

        def turn(e, q):
            if q == 0:
                pe.wait_ge(xr_loaded, e * 32 + 32)
                if isinstance(e, int) and e == 0:
                    pe.wait_ge(y_read, JS - 2)
                else:
                    pe.wait_ge(f32_ready, e * 3)
            else:
                pe.wait_ge(f32_ready, e * 3 + q)
            for c in range(DC):
                for t in (2 * q, 2 * q + 1):
                    n = P if t < ET - 1 else LAST_ROWS
                    tr = pe.transpose(ps[:, 7, c * 2 * P + (t % 2) * P:c * 2 * P + (t % 2) * P + n], xr[0:n, t, c * P:(c + 1) * P], ident[0:n, 0:n])
            tr.then_inc(turned, 1)

        def body(j, b, e, last):
            for m in range(FC):
                up(j, b, e, m)
                if m >= 1:
                    down(j, b, e, m - 1)
                elif last:
                    down(*last, FC - 1)
                if has_next(j, e) and 4 <= m < 7:
                    turn(0 if e is None else e + 1, m - 4)
            if is_first(j):
                pe.wait_ge(hot_ready, 1)
                for x in range(ES):
                    mm = pe.matmul(ps[0:2 * NT, 7, x:x + 1], hot[:].rearrange("p k t x -> p (k t) x")[:, :, x], ones[:, 0:1], start=True, stop=True)
                mm.then_inc(tot_done, 1)
                pe.wait_ge(before_ready, 1)
                pe.matmul(ps[:, 7, :], below[:], hot[:].rearrange("p k t x -> p (k t x)"), start=True, stop=False)
                pe.matmul(ps[:, 7, :], ones[0:2 * NT, :], before[:].rearrange("p k x -> p (k x)"), start=False, stop=True).then_inc(pos_done, 1)
        jobs(pe, body)
        down(JS + E - 1, None, E - 1, FC - 1)

    @block.vector
    def _(dve):
        dve.wait_ge(consts_ready, 2)
        dve.tensor_copy(cst[:], iot[:]).then_inc(cst_done, 1)
        for g in range(NG):
            b = g % 2
            dve.wait_ge(back_done, g + 1)
            for t in range(GT):
                ins = dve.bn_stats(stats[:, b, t, :], ps[:, b * 2 + t // 2, (t % 2) * D:(t % 2 + 1) * D])
            ins.then_inc(norm_steps, 1)
            dve.wait_ge(norm_steps, 3 * g + 1)
            for t in range(GT):
                ins = dve.bn_aggr(mv[:, b, t, :], stats[:, b, t, :])
            ins.then_inc(norm_steps, 1)
            dve.wait_ge(norm_steps, 3 * g + 2)
            dve.tensor_scalar(var_eps[:, b], mv[:, b, :, 1], 1.0 + EPS, EPS * EPS, ALU.mult, ALU.add).then_inc(ve_done, 1)
            if g >= 2:
                dve.wait_ge(ht_sent[b], 16 * (g // 2))
            dve.tensor_copy(ht[:, b], ps[:, b * 2:b * 2 + 2, :].rearrange("p a (t d) -> p (a t) d", d=D)).then_inc(ht_ready, 1)
            dve.wait_ge(std_done, g + 1)
            dve.reciprocal(rstd[:, b], std[:, b]).then_inc(norm_steps, 1)
            dve.wait_ge(norm_steps, 3 * g + 3)
            if g >= 2:
                dve.wait_ge(rec_ready, g - 1)
            dve.scalar_tensor_tensor(out=nmr[:, b], in0=mv[:, b, :, 0], scalar=-1.0, in1=rstd[:, b],
                                     op0=ALU.mult, op1=ALU.mult).then_inc(nmr_done, 1)

        def split_block(g, b):
            xs = x32[:, :, bass.ds(g * G, G)]
            if isinstance(g, int):
                dve.wait_ge(feat_ready, g + 1)
            dve.tensor_copy(f_hi[:, b, :, 0:G], xs).then_inc(f_hi_done, 1)
            dve.wait_ge(f_hi_done, g + 1)
            dve.tensor_tensor(f_lo[:, b, :, 0:G], xs, f_hi[:, b, :, 0:G].bitcast(F32), ALU.subtract).then_inc(f_ready, 1)

        def split_expert(e, q):
            dve.wait_ge(f32_ready, e * 3 + (q + 1))
            cols = slice(q * 2 * P, min((q + 1) * 2 * P, CAP))
            hi, lo = (f[:, bass.ds(e % 2, 1), :, cols].rearrange("p a c n -> p (a c) n") for f in (f_hi, f_lo))
            dve.tensor_copy(hi, f32[:, :, cols]).then_inc(f_hi_done, 1)
            dve.wait_ge(f_hi_done, e * 3 + (JS + q + 1))
            ins = dve.tensor_tensor(lo, f32[:, :, cols], hi.bitcast(F32), ALU.subtract)
            if q == 2:
                ins.then_inc(f_ready, 1)

        steps = [0]

        def step(ins):
            steps[0] += 1
            ins.then_inc(route, 1)
            dve.wait_ge(route, steps[0])

        def by_expert(x):
            return cst[:, x, :].unsqueeze(1).to_broadcast([P, NT, ES])

        def wide(x):
            return x.unsqueeze(2).to_broadcast([P, NT, ES])

        def choices():
            dve.memset(lg[:, :, E:ES], NEG)
            step(dve.tensor_copy(lg[:, :, 0:E], ps[:, 6, 0:NT * ES].rearrange("p (t x) -> p t x", x=ES)[:, :, 0:E]))
            for k in range(2):
                step(dve.tensor_reduce(top[:, k, :], lg[:], AX.X, ALU.max))
                step(dve.tensor_tensor(eq[:], lg[:], wide(top[:, k, :]), ALU.is_equal))
                step(dve.tensor_tensor(eq[:], eq[:], by_expert(0), ALU.mult))
                step(dve.tensor_reduce(which[:, k, :], eq[:], AX.X, ALU.max))
                step(dve.tensor_tensor(hot[:, k], by_expert(0), wide(which[:, k, :]), ALU.is_equal))
                if k == 0:
                    step(dve.scalar_tensor_tensor(out=lg[:], in0=hot[:, 0], scalar=NEG, in1=lg[:], op0=ALU.mult, op1=ALU.add))
            dve.tensor_tensor(small[:, 0, :], top[:, 1, :], top[:, 0, :], ALU.subtract).then_inc(gap_ready, 1)
            step(dve.tensor_scalar(rec[:, :, D + 2], which[:, 0, :], -1.0, float(ES), ALU.mult, ALU.add))
            dve.memset(tot[:], 0.0).then_inc(hot_ready, 1)
            dve.wait_ge(gate_exp_done, 1)
            step(dve.tensor_scalar(small[:, 2, :], small[:, 1, :], 1.0, None, ALU.add))
            step(dve.reciprocal(small[:, 3, :], small[:, 2, :]))
            dve.tensor_copy(rec[:, :, D + 1], small[:, 3, :])
            step(dve.tensor_tensor(rec[:, :, D + 3], small[:, 1, :], small[:, 3, :], ALU.mult))

        def places():
            dve.wait_ge(tot_done, 1)
            step(dve.tensor_copy(tot[0:2 * NT, :], ps[0:2 * NT, 7, 0:ES]))
            n = 2 * NT
            dve.tensor_tensor(before[:], tot[0:n, :].unsqueeze(1).to_broadcast([n, n, ES]),
                              below[0:n, 0:n].unsqueeze(2).to_broadcast([n, n, ES]), ALU.mult).then_inc(before_ready, 1)
            dve.wait_ge(pos_done, 1)
            hots = hot[:].rearrange("p k t x -> p (k t) x")
            caps = cst[:, 1, :].unsqueeze(1).to_broadcast([P, n, ES])
            step(dve.tensor_tensor(at_pos[:], ps[:, 7, :].rearrange("p (k x) -> p k x", x=ES), hots, ALU.mult))
            step(dve.tensor_reduce(place[:, 0, :], at_pos[:], AX.X, ALU.add))
            step(dve.tensor_tensor(at_pos[:], hots, caps, ALU.mult))
            dve.tensor_scalar(place[:, 2, :], place[:, 0, :], float(CAP), SKIP, ALU.is_ge, ALU.mult)
            step(dve.tensor_reduce(place[:, 1, :], at_pos[:], AX.X, ALU.add))
            step(dve.tensor_tensor(place[:, 3, :], place[:, 0, :], place[:, 1, :], ALU.add))
            step(dve.tensor_tensor(place[:, 3, :], place[:, 3, :], place[:, 2, :], ALU.add))
            dve.tensor_copy(place_u[:], place[:, 3, :]).then_inc(place_ready, 1)

        split_block(0, 0)
        dve.wait_ge(logits_done, NG)
        dve.wait_ge(cst_done, 1)
        choices()

        dve.memset(gate_next[:], 0.0).then_inc(gate_ready, 1)

        def gates(e):
            dve.wait_ge(xr_loaded, e * 32 + 32)
            dve.wait_ge(gate_ready, e + 1)
            dve.tensor_copy(tok_next[:], xr[:].bitcast(I32)[:, :, D]).then_inc(tok_done, 1)
            first, eid, second = (xr[:, :, D + 1 + n] for n in range(3))
            dve.tensor_scalar(gtmp[:, 0, :], eid, cst[:, 2, bass.ds(e, 1)], None, ALU.is_equal)
            dve.tensor_tensor(gtmp[:, 1, :], first, second, ALU.subtract).then_inc(gate_steps, 1)
            dve.wait_ge(gate_steps, e * 3 + 1)
            dve.tensor_tensor(gtmp[:, 0, :], gtmp[:, 0, :], gtmp[:, 1, :], ALU.mult).then_inc(gate_steps, 1)
            dve.wait_ge(gate_steps, e * 3 + 2)
            dve.tensor_tensor(gate_next[:], gtmp[:, 0, :], second, ALU.add).then_inc(gate_steps, 1)

        def pass_gates(e):
            dve.wait_ge(y_sent, 16 * JS + (16 * ET) * e)
            dve.wait_ge(tok_done, e + 1)
            dve.wait_ge(gate_steps, e * 3 + 3)
            dve.tensor_copy(tok[:], tok_next[:])
            dve.tensor_copy(gate[:], gate_next[:]).then_inc(gate_ready, 1)

        def body(j, b, e, last):
            for m in range(FC):
                k = j * FC + m
                if not (is_first(j) and m == 0):
                    dve.wait_ge(g_hi_ready, k)
                    dve.wait_ge(g_lo_ready, k)
                if e is None:
                    dve.wait_ge(silu_done, part(j, e, m + 1))
                    dve.tensor_tensor(g32[:, 0:G], s32[:, m % 2, :], ps[:, (m % 2) * 2 + 1, :], ALU.mult).then_inc(prod_done, 1)
                    n = G
                else:
                    for h in range(2):
                        dve.wait_ge(silu_done, part(j, e, m, h + 1))
                        dve.tensor_tensor(g32[:, h * HALF:(h + 1) * HALF], s32[:, h, 0:HALF], ps[:, 2 * h + 1, 0:HALF], ALU.mult).then_inc(prod_done, 1)
                    n = CAP
                dve.wait_ge(g_hi_ready, k + 1)
                dve.tensor_tensor(g_lo[:, m % 2, 0:n], g32[:, 0:n], g_hi[:, m % 2, 0:n].bitcast(F32), ALU.subtract).then_inc(g_lo_ready, 1)
                if m >= 5 and has_next(j, e):
                    split_expert(0 if e is None else e + 1, m - 5)
                if m == 7 and has_next(j, e):
                    gates(0 if e is None else e + 1)
                if m == 1 and e is None and not is_last_shared(j):
                    split_block(j + 1, 1 - b)
                if m == 6 and e is not None:
                    pass_gates(e)
            if is_first(j):
                places()
        jobs(dve, body)


def program(nc, io, acc):
    rows_for = nc.dram_tensor("rows_for", (E * CAP, REC), F32, kind="Internal").ap()
    with ExitStack() as ctx:
        x32 = ctx.enter_context(nc.sbuf_tensor("x32", [P, DC, N_TOK], F32))
        with ExitStack() as stage:
            tower(nc, stage, io, x32, rows_for, acc)
        with ExitStack() as stage:
            attention(nc, stage, io, x32)
        with ExitStack() as stage:
            experts(nc, stage, io, x32, rows_for, acc)


def expert_weights(a):
    import numpy as np

    def up(w):
        return w.reshape(DC, P, FC, P).transpose(2, 1, 0, 3).reshape(FC, P, D)

    parts = []
    for e in range(-1, E):
        w1, w3, w2 = (a("L0_ffn_" + n + "s") if e < 0 else a("L0_ffn_" + n)[e] for n in ("W1", "W3", "W2"))
        parts.append(np.concatenate([up(w1), up(w3), w2.reshape(FC, P, D)], 2))
    return np.concatenate(parts)


def attention_weights(a, rows):
    import numpy as np

    wq, wkv, wo = a("L0_attn_w_q"), a("L0_attn_w_kv"), a("L0_attn_w_out")
    h = HEADS * DH
    parts = []
    for p in range(PAIRS):
        at = p * P
        parts.append(np.stack([rows(wq[:, at:at + P], DC), rows(wkv[:, at:at + P], DC),
                               rows(wkv[:, h + at:h + at + P], DC), wo[at:at + P]], 1))
    return np.stack(parts)


def layout(i):
    import numpy as np

    def a(name):
        return np.asarray(i[name])

    def rows(w, chunks):
        return w.reshape(chunks, P, -1).transpose(1, 0, 2).reshape(P, -1)

    def cols(v):
        return np.moveaxis(v.reshape(v.shape[:-1] + (-1, P)), -1, 0)

    wqo, wf = [], []
    for l in range(LAYERS):
        wqo.append(np.stack([rows(a("L0_tok_Wq")[l].reshape(D, D), DC), rows(a("L0_tok_Wo")[l].T, DC)], 1))
        w1 = rows(a("L0_tok_ff_w1")[l].T, DC).reshape(P, NG, G // 2)
        w2 = rows(a("L0_tok_ff_w2")[l].T, FC).reshape(P, NG, G // 2)
        wf.append(np.concatenate([w1, w2], 2).transpose(1, 0, 2))
    return {
        "ids": np.ascontiguousarray(a("x").reshape(-1, P).T),
        "emb": a("L0_tok_emb_table"),
        "wqo": np.ascontiguousarray(np.stack(wqo)),
        "wf": np.ascontiguousarray(np.concatenate(wf)),
        "vec": np.ascontiguousarray(np.concatenate([cols(a("L0_tok_" + n)) for n in ("ln1_w", "ln1_b", "ln2_w", "ln2_b", "ff_b2")], 2)),
        "wa": np.ascontiguousarray(attention_weights(a, rows)),
        "b_out": np.ascontiguousarray(cols(a("L0_attn_b_out"))),
        "sort_w": np.ascontiguousarray(a("L0_attn_sort_w")[0].reshape(SORT_PAIRS, 2, 2, DH, NB)
                                       .transpose(0, 1, 3, 2, 4).reshape(SORT_PAIRS, P, 2, NB)),
        "ffn_g": np.ascontiguousarray(cols(a("L0_ffn_ln_g"))),
        "ffn_b": np.ascontiguousarray(cols(a("L0_ffn_ln_b"))),
        "w_r": np.ascontiguousarray(a("L0_ffn_Wr").reshape(DC, P, E).transpose(1, 0, 2)),
        "we": np.ascontiguousarray(expert_weights(a)),
        "b1": np.ascontiguousarray(cols(a("L0_tok_ff_b1"))),
    }


def kernel(**inputs):
    import numpy as np
    import concourse.bacc as bacc
    from concourse.bass_utils import run_bass_kernel_spmd

    arrays = {"in_" + name: v for name, v in layout(inputs).items()}
    nc = bacc.Bacc("TRN2", target_bir_lowering=False, num_devices=1)
    io = {name[3:]: nc.dram_tensor(name, v.shape, mybir.dt.from_np(v.dtype), kind="ExternalInput").ap()
          for name, v in arrays.items()}
    acc = nc.dram_tensor("out", (N_TOK + P, D), F32, kind="ExternalOutput").ap()
    program(nc, io, acc)
    got = run_bass_kernel_spmd(nc, [arrays], core_ids=[0]).results[0]["out"]
    return got[:N_TOK].reshape(2, N_TOK // 2, D)
```
